# Optimizing a Trainium2 kernel written in Bass

```python
import numpy as np
import jax
import jax.numpy as jnp

def _softmax(x, axis=-1):
    return jax.nn.softmax(x, axis=axis)

def _gelu(x):
    return jax.nn.gelu(x, approximate=True)

def _silu(x):
    return jax.nn.silu(x)

def _sigmoid(x):
    return jax.nn.sigmoid(x)

def _layernorm(x, axis=-1, eps=1e-05):
    m = jnp.mean(x, axis=axis, keepdims=True)
    v = jnp.var(x, axis=axis, keepdims=True)
    return (x - m) / jnp.sqrt(v + eps)

def _scatter_add(tgt, idx, src, axis=0):
    return tgt.at[idx].add(src)

def _segment_sum(src, seg, n):
    return jax.ops.segment_sum(src, seg, n)
kernel_name = 'mk_perceiver_d2_seqx_r8_b76988'

def setup_inputs(seed: int=0):
    np.random.seed(seed)
    _w = jnp.asarray

    def _rec_inputs():
        import jax
        import jax.numpy as jnp
        _rk = jax.random.key(seed)
        x = -0.000125 + 0.9999 * jax.random.normal(jax.random.fold_in(_rk, 1), (2, 32, 512), jnp.float32)
        _lenS = 32 - jax.random.randint(jax.random.fold_in(_rk, 7), (2,), 0, max(1, 32 // 4) + 1, jnp.int32)
        _lenS2 = 512 - jax.random.randint(jax.random.fold_in(_rk, 8), (2,), 0, max(1, 512 // 4) + 1, jnp.int32)
        _ctx_4096P = jax.random.normal(jax.random.fold_in(_rk, 11), (2, 16, 512), jnp.float32)
        _ctx_4096c = jax.random.dirichlet(jax.random.fold_in(_rk, 511), 0.3 * jnp.ones((16,), jnp.float32), (2, 512))
        _ctx_4096t = jnp.einsum('bsk,bkd->bsd', _ctx_4096c, _ctx_4096P)
        _ctx_4096t = _ctx_4096t * jax.lax.rsqrt(jnp.mean(jnp.square(_ctx_4096t)) + 1e-12) * 0.953939
        ctx_4096 = -5.72187e-05 + 0.999849 * (_ctx_4096t + 0.3 * jax.random.normal(jax.random.fold_in(_rk, 611), (2, 512, 512), jnp.float32))
        _validS = jnp.arange(32)[None, :] < _lenS[:, None]
        _validS2 = jnp.arange(512)[None, :] < _lenS2[:, None]
        _causal = jnp.tril(jnp.ones((32, 32), dtype=bool))
        mask_1x1xSxS2_ff0 = jnp.where(jnp.ones((1, 1, 32, 512), dtype=bool), 0.0, -1000000000.0).astype(jnp.float32)
        return (x, ctx_4096, mask_1x1xSxS2_ff0)
    x, ctx_4096, mask_1x1xSxS2_ff0 = _rec_inputs()

    def _L0_xattn_setup():
        import jax, jax.numpy as jnp
        import numpy as np
        QMIN = 0.0
        QMAX = 255.0

        def fake_quant(x, scale, zp):
            s = scale.reshape(())
            z = zp.reshape(())
            q = jnp.clip(jnp.round(x / s + z), QMIN, QMAX)
            return (q - z) * s
        key = jax.random.key(seed)
        k1, k2 = jax.random.split(key)
        B, M, K, N = (4, 256, 512, 512)
        x1 = jax.random.normal(k1, (B, M, K), dtype=jnp.float32)
        x2 = jax.random.normal(k2, (B, K, N), dtype=jnp.float32)
        x1_scale = jnp.full((1,), 8.0 / 255.0, dtype=jnp.float32)
        x1_zp = jnp.full((1,), 128.0, dtype=jnp.float32)
        x2_scale = jnp.full((1,), 8.0 / 255.0, dtype=jnp.float32)
        x2_zp = jnp.full((1,), 128.0, dtype=jnp.float32)
        return {'x1': x1, 'x2': x2, 'x1_scale': x1_scale, 'x1_zp': x1_zp, 'x2_scale': x2_scale, 'x2_zp': x2_zp}
    _L0_xattn_all = _L0_xattn_setup()
    _L0_xattn_in = {k: v for k, v in _L0_xattn_all.items() if k in ('x1_scale', 'x1_zp', 'x2_scale', 'x2_zp')}
    del _L0_xattn_all

    def _L0_attn_setup():
        import jax, jax.numpy as jnp
        import numpy as np
        HIDDEN = 512
        HEADS = 32
        D_K = HIDDEN // HEADS
        key = jax.random.key(seed)
        ks = jax.random.split(key, 5)
        scale = 1.0 / np.sqrt(HIDDEN)
        x = jax.random.normal(ks[0], (2, 256, HIDDEN), dtype=jnp.float32)
        w_q = jax.random.uniform(ks[1], (HIDDEN, HIDDEN), jnp.float32, -scale, scale)
        w_k = jax.random.uniform(ks[2], (HIDDEN, HIDDEN), jnp.float32, -scale, scale)
        w_v = jax.random.uniform(ks[3], (HIDDEN, HIDDEN), jnp.float32, -scale, scale)
        w_o = jax.random.uniform(ks[4], (HIDDEN, HIDDEN), jnp.float32, -scale, scale)
        return {'x': x, 'w_q': w_q, 'w_k': w_k, 'w_v': w_v, 'w_o': w_o}
    _L0_attn_all = _L0_attn_setup()
    _L0_attn_in = {k: v for k, v in _L0_attn_all.items() if k in ('w_q', 'w_k', 'w_v', 'w_o')}
    del _L0_attn_all

    def _L0_ffn_setup():
        import jax, jax.numpy as jnp
        import numpy as np
        DIM = 512
        INTER = 128
        E = 16
        GROUPS = 4
        LIM = 2
        K = 2
        SHARED_INTER = 2 * INTER
        SCALE = 1.0
        key = jax.random.key(seed)
        ks = jax.random.split(key, 16)

        def n(k, shape, s=0.02):
            return jax.random.normal(k, shape, jnp.float32) * s
        return {'x': jax.random.normal(ks[0], (1, 256, DIM), jnp.float32), 'router_w': n(ks[1], (DIM, E)), 'router_b': n(ks[2], (E,)), 'router_bias': n(ks[3], (E,), 1.0), 'ew1': n(ks[4], (E, DIM, INTER)), 'eb1': n(ks[5], (E, INTER)), 'ew2': n(ks[6], (E, DIM, INTER)), 'eb2': n(ks[7], (E, INTER)), 'ew3': n(ks[8], (E, INTER, DIM)), 'eb3': n(ks[9], (E, DIM)), 'sw1': n(ks[10], (DIM, SHARED_INTER)), 'sb1': n(ks[11], (SHARED_INTER,)), 'sw2': n(ks[12], (DIM, SHARED_INTER)), 'sb2': n(ks[13], (SHARED_INTER,)), 'sw3': n(ks[14], (SHARED_INTER, DIM)), 'sb3': n(ks[15], (DIM,))}
    _L0_ffn_all = _L0_ffn_setup()
    _L0_ffn_in = {k: v for k, v in _L0_ffn_all.items() if k in ('router_w', 'router_b', 'router_bias', 'ew1', 'eb1', 'ew2', 'eb2', 'ew3', 'eb3', 'sw1', 'sb1', 'sw2', 'sb2', 'sw3', 'sb3')}
    del _L0_ffn_all

    def _L1_xattn_setup():
        import jax, jax.numpy as jnp
        import numpy as np
        B, Q, K, D = (1, 128, 6404, 512)
        H, KVH, HD = (32, 8, 128)
        GROUPS = H // KVH
        EPS = 1e-05

        def _rmsnorm(x, w):
            xf = x.astype(jnp.float32)
            var = jnp.mean(xf * xf, axis=-1, keepdims=True)
            return (xf * jax.lax.rsqrt(var + EPS)).astype(x.dtype) * w
        key = jax.random.key(seed)
        ks = jax.random.split(key, 8)
        s = 0.02
        return {'hidden_states': jax.random.normal(ks[0], (B, Q, D), jnp.float32), 'cross_attention_states': jax.random.normal(ks[1], (B, K, D), jnp.float32), 'attention_mask': jnp.zeros((B, 1, Q, K), jnp.float32), 'Wq': jax.random.normal(ks[2], (H * HD, D), jnp.float32) * s, 'Wk': jax.random.normal(ks[3], (KVH * HD, D), jnp.float32) * s, 'Wv': jax.random.normal(ks[4], (KVH * HD, D), jnp.float32) * s, 'Wo': jax.random.normal(ks[5], (D, H * HD), jnp.float32) * s, 'q_norm_w': jnp.ones((HD,), jnp.float32), 'k_norm_w': jnp.ones((HD,), jnp.float32)}
    _L1_xattn_all = _L1_xattn_setup()
    _L1_xattn_in = {k: v for k, v in _L1_xattn_all.items() if k in ('Wq', 'Wk', 'Wv', 'Wo', 'q_norm_w', 'k_norm_w')}
    del _L1_xattn_all

    def _L1_attn_setup():
        import jax, jax.numpy as jnp
        import numpy as np
        HIDDEN = 512
        NUM_HEADS = 32
        HEAD_DIM = HIDDEN // NUM_HEADS
        THRESH = 0.001
        key = jax.random.key(seed)
        ks = jax.random.split(key, 9)
        w_std = 0.02
        x = jax.random.normal(ks[0], (4, 512, HIDDEN), dtype=jnp.float32)
        Wq = jax.random.normal(ks[1], (HIDDEN, HIDDEN), dtype=jnp.float32) * w_std
        bq = jax.random.normal(ks[2], (HIDDEN,), dtype=jnp.float32) * w_std
        Wk = jax.random.normal(ks[3], (HIDDEN, HIDDEN), dtype=jnp.float32) * w_std
        bk = jax.random.normal(ks[4], (HIDDEN,), dtype=jnp.float32) * w_std
        Wv = jax.random.normal(ks[5], (HIDDEN, HIDDEN), dtype=jnp.float32) * w_std
        bv = jax.random.normal(ks[6], (HIDDEN,), dtype=jnp.float32) * w_std
        Wo = jax.random.normal(ks[7], (HIDDEN, HIDDEN), dtype=jnp.float32) * w_std
        bo = jax.random.normal(ks[8], (HIDDEN,), dtype=jnp.float32) * w_std
        return {'x': x, 'Wq': Wq, 'bq': bq, 'Wk': Wk, 'bk': bk, 'Wv': Wv, 'bv': bv, 'Wo': Wo, 'bo': bo}
    _L1_attn_all = _L1_attn_setup()
    _L1_attn_in = {k: v for k, v in _L1_attn_all.items() if k in ('Wq', 'bq', 'Wk', 'bk', 'Wv', 'bv', 'Wo', 'bo')}
    del _L1_attn_all

    def _L1_ffn_setup():
        import jax, jax.numpy as jnp
        import numpy as np
        RANKS = (8, 16, 32, 64)
        TOPK = 1
        SCALING = 1.0 / 4
        key = jax.random.key(seed)
        ks = jax.random.split(key, 7)
        D_IN, D_OUT, MAX_R, N_RANKS = (512, 512, 64, len(RANKS))
        B_, S_ = (4, 256)
        return {'hidden_states': jax.random.normal(ks[0], (B_, S_, D_IN), jnp.float32), 'W': jax.random.normal(ks[1], (D_OUT, D_IN), jnp.float32) * 0.02, 'b': jax.random.normal(ks[2], (D_OUT,), jnp.float32) * 0.02, 'A': jax.random.normal(ks[3], (MAX_R, D_IN), jnp.float32) * 0.02, 'B': jnp.zeros((D_OUT, MAX_R), jnp.float32) + jax.random.normal(ks[4], (D_OUT, MAX_R), jnp.float32) * 0.02, 'gate_w': jax.random.normal(ks[5], (N_RANKS, D_IN), jnp.float32) * 0.02, 'gate_b': jax.random.normal(ks[6], (N_RANKS,), jnp.float32) * 0.02}
    _L1_ffn_all = _L1_ffn_setup()
    _L1_ffn_in = {k: v for k, v in _L1_ffn_all.items() if k in ('W', 'b', 'A', 'B', 'gate_w', 'gate_b')}
    del _L1_ffn_all
    return {'x': x, 'ctx_4096': ctx_4096, 'mask_1x1xSxS2_ff0': mask_1x1xSxS2_ff0, 'L0_xattn_x1_scale': _L0_xattn_in['x1_scale'], 'L0_xattn_x1_zp': _L0_xattn_in['x1_zp'], 'L0_xattn_x2_scale': _L0_xattn_in['x2_scale'], 'L0_xattn_x2_zp': _L0_xattn_in['x2_zp'], 'L0_attn_w_q': _L0_attn_in['w_q'], 'L0_attn_w_k': _L0_attn_in['w_k'], 'L0_attn_w_v': _L0_attn_in['w_v'], 'L0_attn_w_o': _L0_attn_in['w_o'], 'L0_ffn_router_w': _L0_ffn_in['router_w'], 'L0_ffn_router_b': _L0_ffn_in['router_b'], 'L0_ffn_router_bias': _L0_ffn_in['router_bias'], 'L0_ffn_ew1': _L0_ffn_in['ew1'], 'L0_ffn_eb1': _L0_ffn_in['eb1'], 'L0_ffn_ew2': _L0_ffn_in['ew2'], 'L0_ffn_eb2': _L0_ffn_in['eb2'], 'L0_ffn_ew3': _L0_ffn_in['ew3'], 'L0_ffn_eb3': _L0_ffn_in['eb3'], 'L0_ffn_sw1': _L0_ffn_in['sw1'], 'L0_ffn_sb1': _L0_ffn_in['sb1'], 'L0_ffn_sw2': _L0_ffn_in['sw2'], 'L0_ffn_sb2': _L0_ffn_in['sb2'], 'L0_ffn_sw3': _L0_ffn_in['sw3'], 'L0_ffn_sb3': _L0_ffn_in['sb3'], 'L1_xattn_Wq': _L1_xattn_in['Wq'], 'L1_xattn_Wk': _L1_xattn_in['Wk'], 'L1_xattn_Wv': _L1_xattn_in['Wv'], 'L1_xattn_Wo': _L1_xattn_in['Wo'], 'L1_xattn_q_norm_w': _L1_xattn_in['q_norm_w'], 'L1_xattn_k_norm_w': _L1_xattn_in['k_norm_w'], 'L1_attn_Wq': _L1_attn_in['Wq'], 'L1_attn_bq': _L1_attn_in['bq'], 'L1_attn_Wk': _L1_attn_in['Wk'], 'L1_attn_bk': _L1_attn_in['bk'], 'L1_attn_Wv': _L1_attn_in['Wv'], 'L1_attn_bv': _L1_attn_in['bv'], 'L1_attn_Wo': _L1_attn_in['Wo'], 'L1_attn_bo': _L1_attn_in['bo'], 'L1_ffn_W': _L1_ffn_in['W'], 'L1_ffn_b': _L1_ffn_in['b'], 'L1_ffn_A': _L1_ffn_in['A'], 'L1_ffn_B': _L1_ffn_in['B'], 'L1_ffn_gate_w': _L1_ffn_in['gate_w'], 'L1_ffn_gate_b': _L1_ffn_in['gate_b']}

def reference(x, ctx_4096, mask_1x1xSxS2_ff0, L0_xattn_x1_scale, L0_xattn_x1_zp, L0_xattn_x2_scale, L0_xattn_x2_zp, L0_attn_w_q, L0_attn_w_k, L0_attn_w_v, L0_attn_w_o, L0_ffn_router_w, L0_ffn_router_b, L0_ffn_router_bias, L0_ffn_ew1, L0_ffn_eb1, L0_ffn_ew2, L0_ffn_eb2, L0_ffn_ew3, L0_ffn_eb3, L0_ffn_sw1, L0_ffn_sb1, L0_ffn_sw2, L0_ffn_sb2, L0_ffn_sw3, L0_ffn_sb3, L1_xattn_Wq, L1_xattn_Wk, L1_xattn_Wv, L1_xattn_Wo, L1_xattn_q_norm_w, L1_xattn_k_norm_w, L1_attn_Wq, L1_attn_bq, L1_attn_Wk, L1_attn_bk, L1_attn_Wv, L1_attn_bv, L1_attn_Wo, L1_attn_bo, L1_ffn_W, L1_ffn_b, L1_ffn_A, L1_ffn_B, L1_ffn_gate_w, L1_ffn_gate_b):
    import jax
    import jax.numpy as jnp

    def _L0_xattn_ref(x1, x2, x1_scale, x1_zp, x2_scale, x2_zp):
        import jax, jax.numpy as jnp
        import numpy as np
        QMIN = 0.0
        QMAX = 255.0

        def fake_quant(x, scale, zp):
            s = scale.reshape(())
            z = zp.reshape(())
            q = jnp.clip(jnp.round(x / s + z), QMIN, QMAX)
            return (q - z) * s
        q1 = fake_quant(x1, x1_scale, x1_zp)
        q2 = fake_quant(x2, x2_scale, x2_zp)
        return jnp.matmul(q1, q2)

    def _L0_attn_ref(x, w_q, w_k, w_v, w_o):
        import jax, jax.numpy as jnp
        import numpy as np
        HIDDEN = 512
        HEADS = 32
        D_K = HIDDEN // HEADS
        B, S, _ = x.shape

        def proj(w):
            y = jnp.einsum('bsd,ed->bse', x, w)
            return y.reshape(B, S, HEADS, D_K).transpose(0, 2, 1, 3)
        q, k, v = (proj(w_q), proj(w_k), proj(w_v))
        scores = jnp.einsum('bhqd,bhkd->bhqk', q, k) / jnp.sqrt(jnp.float32(D_K))
        attn = jax.nn.softmax(scores, axis=-1)
        out = jnp.einsum('bhqk,bhkd->bhqd', attn, v)
        out = out.transpose(0, 2, 1, 3).reshape(B, S, HIDDEN)
        return jnp.einsum('bse,oe->bso', out, w_o)

    def _L0_ffn_ref(x, router_w, router_b, router_bias, ew1, eb1, ew2, eb2, ew3, eb3, sw1, sb1, sw2, sb2, sw3, sb3):
        import jax, jax.numpy as jnp
        import numpy as np
        DIM = 512
        INTER = 128
        E = 16
        GROUPS = 4
        LIM = 2
        K = 2
        SHARED_INTER = 2 * INTER
        SCALE = 1.0
        shape = x.shape
        xt = x.reshape(-1, DIM)
        T = xt.shape[0]
        logits = xt @ router_w + router_b
        scores = jax.nn.softmax(logits.astype(jnp.float32), axis=-1) + router_bias
        g = scores.reshape(T, GROUPS, E // GROUPS)
        _, gidx = jax.lax.top_k(g.max(axis=-1), LIM)
        keep = jnp.zeros((T, GROUPS), bool).at[jnp.arange(T)[:, None], gidx].set(True)
        masked = jnp.where(keep[:, :, None], g, -jnp.inf).reshape(T, E)
        _, idx = jax.lax.top_k(masked, K)
        vals = (jnp.take_along_axis(scores, idx, axis=1) * SCALE).astype(x.dtype)
        gate = jnp.zeros((T, E), x.dtype).at[jnp.arange(T)[:, None], idx].add(vals)

        def step(y, p):
            w1, b1, w2, b2, w3, b3, ge = p
            h = jax.nn.silu(xt @ w1 + b1) * (xt @ w2 + b2)
            return (y + ge[:, None] * (h @ w3 + b3), None)
        y, _ = jax.lax.scan(step, jnp.zeros_like(xt), (ew1, eb1, ew2, eb2, ew3, eb3, gate.T))
        z = jax.nn.silu(xt @ sw1 + sb1) * (xt @ sw2 + sb2) @ sw3 + sb3
        return (y + z).reshape(shape)

    def _L1_xattn_ref(hidden_states, cross_attention_states, attention_mask, Wq, Wk, Wv, Wo, q_norm_w, k_norm_w):
        import jax, jax.numpy as jnp
        import numpy as np
        B, Q, K, D = (1, 128, 6404, 512)
        H, KVH, HD = (32, 8, 128)
        GROUPS = H // KVH
        EPS = 1e-05

        def _rmsnorm(x, w):
            xf = x.astype(jnp.float32)
            var = jnp.mean(xf * xf, axis=-1, keepdims=True)
            return (xf * jax.lax.rsqrt(var + EPS)).astype(x.dtype) * w
        bsz, q_len, _ = hidden_states.shape
        kv_len = cross_attention_states.shape[1]
        q = (hidden_states @ Wq.T).reshape(bsz, q_len, H, HD).transpose(0, 2, 1, 3)
        k = (cross_attention_states @ Wk.T).reshape(bsz, kv_len, KVH, HD).transpose(0, 2, 1, 3)
        v = (cross_attention_states @ Wv.T).reshape(bsz, kv_len, KVH, HD).transpose(0, 2, 1, 3)
        q = _rmsnorm(q, q_norm_w)
        k = jnp.repeat(k, GROUPS, axis=1)
        v = jnp.repeat(v, GROUPS, axis=1)
        k = _rmsnorm(k, k_norm_w)
        scale = 1.0 / np.sqrt(HD)
        scores = jnp.einsum('bhqd,bhkd->bhqk', q, k) * scale
        scores = scores + attention_mask[:, :, :, :kv_len]
        probs = jax.nn.softmax(scores.astype(jnp.float32), axis=-1).astype(q.dtype)
        out = jnp.einsum('bhqk,bhkd->bhqd', probs, v)
        out = out.transpose(0, 2, 1, 3).reshape(bsz, q_len, H * HD)
        return out @ Wo.T

    def _L1_attn_ref(x, Wq, bq, Wk, bk, Wv, bv, Wo, bo):
        import jax, jax.numpy as jnp
        import numpy as np
        HIDDEN = 512
        NUM_HEADS = 32
        HEAD_DIM = HIDDEN // NUM_HEADS
        THRESH = 0.001
        B, S, Hd = x.shape
        H, D = (NUM_HEADS, HEAD_DIM)
        q = (x @ Wq.T + bq).reshape(B, S, H, D)
        k = (x @ Wk.T + bk).reshape(B, S, H, D)
        v = (x @ Wv.T + bv).reshape(B, S, H, D)
        inv_sqrt_d = np.float32(1.0 / np.sqrt(D))
        scores = jnp.einsum('bshd,bsgd->bshg', q, k) * inv_sqrt_d
        scores = jnp.where(scores > THRESH, scores, -jnp.inf)
        attn = jax.nn.softmax(scores, axis=-1)
        out = jnp.einsum('bshg,bsgd->bshd', attn, v).reshape(B, S, Hd)
        return out @ Wo.T + bo

    def _L1_ffn_ref(hidden_states, W, b, A, B, gate_w, gate_b):
        import jax, jax.numpy as jnp
        import numpy as np
        RANKS = (8, 16, 32, 64)
        TOPK = 1
        SCALING = 1.0 / 4
        bsz, seq, d_in = hidden_states.shape
        out = jnp.einsum('bsd,od->bso', hidden_states, W) + b
        x = hidden_states.reshape(-1, d_in)
        scores = x @ gate_w.T + gate_b
        probs = jax.nn.softmax(scores, axis=-1)
        routing_weights, selected = jax.lax.top_k(probs, TOPK)
        routing_weights = routing_weights / jnp.sum(routing_weights, axis=-1, keepdims=True)
        lora_outputs = jnp.stack([x @ A[:r, :].T @ B[:, :r].T for r in RANKS], axis=1)
        sel = jnp.take_along_axis(lora_outputs, selected[:, :, None], axis=1)
        final = jnp.sum(sel * routing_weights[:, :, None], axis=1)
        return out + final.reshape(bsz, seq, -1)
    x = x + _L0_xattn_ref(_layernorm(x, axis=-1), ctx_4096, L0_xattn_x1_scale, L0_xattn_x1_zp, L0_xattn_x2_scale, L0_xattn_x2_zp)
    x = x + _L0_attn_ref(_layernorm(x, axis=-1), L0_attn_w_q, L0_attn_w_k, L0_attn_w_v, L0_attn_w_o)
    x = x + _L0_ffn_ref(_layernorm(x, axis=-1), L0_ffn_router_w, L0_ffn_router_b, L0_ffn_router_bias, L0_ffn_ew1, L0_ffn_eb1, L0_ffn_ew2, L0_ffn_eb2, L0_ffn_ew3, L0_ffn_eb3, L0_ffn_sw1, L0_ffn_sb1, L0_ffn_sw2, L0_ffn_sb2, L0_ffn_sw3, L0_ffn_sb3)
    x = x + _L1_xattn_ref(_layernorm(x, axis=-1), ctx_4096, mask_1x1xSxS2_ff0, L1_xattn_Wq, L1_xattn_Wk, L1_xattn_Wv, L1_xattn_Wo, L1_xattn_q_norm_w, L1_xattn_k_norm_w)
    x = x + _L1_attn_ref(_layernorm(x, axis=-1), L1_attn_Wq, L1_attn_bq, L1_attn_Wk, L1_attn_bk, L1_attn_Wv, L1_attn_bv, L1_attn_Wo, L1_attn_bo)
    x = x + _L1_ffn_ref(_layernorm(x, axis=-1), L1_ffn_W, L1_ffn_b, L1_ffn_A, L1_ffn_B, L1_ffn_gate_w, L1_ffn_gate_b)
    return x

_drawn_inputs = setup_inputs


def setup_inputs(seed=0):
    import zlib

    import numpy as np

    out = dict(_drawn_inputs(seed))
    spreads = {'L1_xattn_q_norm_w': (1.0, 0.6), 'L1_xattn_k_norm_w': (1.0, 0.6)}
    factors = {'L0_attn_w_q': 8.0,
     'L0_attn_w_k': 8.0,
     'L0_attn_w_v': 8.0,
     'L0_attn_w_o': 8.0,
     'L0_ffn_router_w': 41.901,
     'L0_ffn_router_b': 200.0,
     'L0_ffn_router_bias': 8.0,
     'L0_ffn_ew1': 8.0,
     'L0_ffn_eb1': 8.0,
     'L0_ffn_ew2': 8.0,
     'L0_ffn_eb2': 8.0,
     'L0_ffn_ew3': 8.0,
     'L0_ffn_eb3': 47.444,
     'L0_ffn_sw1': 8.0,
     'L0_ffn_sb1': 64.0,
     'L0_ffn_sw2': 8.0,
     'L0_ffn_sb2': 64.0,
     'L0_ffn_sw3': 8.0,
     'L0_ffn_sb3': 200.0,
     'L1_xattn_Wq': 64.0,
     'L1_xattn_Wk': 64.0,
     'L1_xattn_Wv': 16.329,
     'L1_xattn_Wo': 17.162,
     'L1_attn_Wq': 8.0,
     'L1_attn_bq': 64.0,
     'L1_attn_Wk': 8.0,
     'L1_attn_bk': 64.0,
     'L1_attn_Wv': 8.0,
     'L1_attn_bv': 199.284,
     'L1_attn_Wo': 8.0,
     'L1_attn_bo': 200.0,
     'L1_ffn_b': 200.0,
     'L1_ffn_A': 51.962,
     'L1_ffn_B': 54.483,
     'L1_ffn_gate_w': 64.0,
     'L1_ffn_gate_b': 64.0,
     'L1_ffn_W': 50.533}
    for name, (base, spread) in spreads.items():
        noise = np.random.default_rng([zlib.crc32(name.encode()), seed]).standard_normal(out[name].shape)
        drawn = base * np.exp(spread * noise) if base else spread * noise
        out[name] = jnp.asarray(drawn.astype(out[name].dtype))
    for name, factor in factors.items():
        out[name] = (out[name] * factor).astype(out[name].dtype)
    return out
```

```python
from contextlib import ExitStack

import numpy as np

import concourse.bass as bass
from concourse import mybir

F32 = mybir.dt.float32
BF16 = mybir.dt.bfloat16
ALU = mybir.AluOpType
ACT = mybir.ActivationFunctionType
AX_X = mybir.AxisListType.X

P = 128
B, S, D = 2, 32, 512
T = B * S
CTX = 512
KC = D // P
NH, DK = 32, 16
HPC = P // DK
E, INTER, GROUPS = 16, 128, 4
H, KVH, HD = 32, 8, 128
GH = H // KVH
LN_EPS = 1e-5
BIG = 1e30
RANKS = (8, 16, 32, 64)
THRESH4 = 4 * float(np.float32(0.001))
MAGIC = 1.5 * 2.0 ** 23
QMID = 128.0

C_ID, C_HM, C_T16, C_T4 = 0, 128, 136, 392
C_QW, C_KW, C_RB, C_RBIAS, C_GB, C_Q = 408, 409, 410, 426, 442, 446
C_N = 450
FB_EB, FB_SB, FB_SB3, FB_N = 0, 2048, 2304, 2816
L_AG, L_BT, L_ROWS, L_QKB, L_N = 0, 272, 784, 2320, 2832

SLOT = 2048
SLOTS = 7
(I_WK, I_WQ, I_WV, I_WO, I_W1A, I_W2A, I_SH, I_W1B, I_W2B, I_W3, I_SW3, I_XQ, I_XO) = (
    0, 1, 2, 3, 4, 6, 8, 9, 11, 13, 17, 18, 26)
ITEMS = 34

FILL = [("start", 4), ("quant", 8), ("mix", 3), ("ln1", 5), ("heads", 2), ("soft1", 6), ("pv1", 2), ("ln2", 6),
        ("route", 0), ("ffn1", 4), ("ffn2", 4), ("ffn3", 3), ("ffn4", 2), ("ln3", 7), ("q0", 4), ("rest", 68)]
UNITS = 32
FILL_TO = {}
_n = 0
for _name, _k in FILL:
    FILL_TO[_name] = (_n, _n + _k)
    _n += _k
assert _n == 4 * UNITS

SEMS = """
x_in cst_in fb_in rw_in ctx_in0 ctx_in1 kv_in0 kv_in1 kv_in2 kv_in3 kv_in4 kv_in5 mask_in late_in l1w_in0 l1w_in1
l1w_in2 l1w_in3 l1w_in4 out_done
slot0 slot1 slot2 slot3 slot4 slot5 slot6 item_used
dve_step act_step pool_step const_ready scal_ready
var_ready rstd_ready xn_ready xnT_psum xT_ready
xq_ready xqT_psum xqT_ready ctx_aff q2_ready mix_done x_new
kbd_ready qT_sb vbd_zero vbd_ready s_done s_shift e_done pt_ready o_done ot_ready
router_done lg_ready re_done gate_ready gateT_psum gateT_ready
h1_done h2_done h1_free silu_in silu_done h_ready hT_psum hT_ready
qm_done qsq_done qms_ready rq_ready qn_ready qnT_psum qTx_ready
kv_unit_done ksq_done kms_ready rk_ready kn_ready kT_psum kT_ready v_ready
sx_done pmax_ready pexp_done pn_ready ptx_psum ptx_ready ox_done otx_ready
lq_done lk_done lv_done lqk_sb lv_sb vg_ready vg2_ready qd_psum kd_psum qd_ready kd_ready ls_done ls_shift le_done
at_ready lo_done of_ready ly_done
xa_done ge_in ge_done xm_ready xmT_psum xmT_ready f_done fin_ready
""".split()


def build(nc, x_d, cst_d, fb_d, rw_d, ctx_d, kv_d, items_d, mask_d, late_d, l1w_d, out_d):
    with ExitStack() as ctx:
        def sb(name, shape, dt=F32):
            return ctx.enter_context(nc.sbuf_tensor(name, shape, dt))

        s = {name: ctx.enter_context(nc.semaphore(name)) for name in SEMS}

        ring = sb("ring", [P, SLOTS, SLOT])
        kvw = sb("kvw", [P, 6, SLOT])
        kT = sb("kT", [P, KVH, B, CTX])
        V = sb("V", [P, 8, KVH * HD])
        r1 = sb("r1", [P, FB_N])
        r2 = sb("r2", [P, 3072])
        x = sb("x", [T, D])
        xn = sb("xn", [T, D])
        xT = sb("xT", [P, KC, T])
        cst = sb("cst", [P, C_N])
        nmask = sb("nmask", [P, CTX])
        ksq = sb("ksq", [P, 512])
        kn = sb("kn", [P, 2, 512])
        sc = sb("sc", [P, 260])
        ps = ctx.enter_context(nc.psum_tensor("ps", [P, 8, 512], F32))

        ctxn = V[:, 4:8, :].rearrange("p a (c n) -> p (a c) n", n=512)
        q2 = ring[:, 6, :].bitcast(BF16).rearrange("p (g n) -> p g n", n=512)
        ctxT = [kvw[:, b, :].rearrange("p (k n) -> p k n", k=KC) for b in range(B)]
        wkx = [kvw[:, 2 + i, :].rearrange("p (k n) -> p k n", k=KC) for i in range(2)]
        wvx = [kvw[:, 4 + i, :].rearrange("p (k n) -> p k n", k=KC) for i in range(2)]
        l1w = [kvw[:, i, :].rearrange("p (k n) -> p k n", k=KC) for i in range(5)]
        otx = kvw[:, 5, :].rearrange("p (h t) -> p h t", t=T)
        late = kT[:, 0:4, :, :].rearrange("p g b n -> p (g b n)")[:, 0:L_N]

        prob, probT = r1[:, 0:512], r1[:, 512:1024]
        qTs = r1[:, 1024:1280].rearrange("p (c t) -> p c t", c=KC)
        ots = r1[:, 1280:1536].rearrange("p (c t) -> p c t", c=KC)
        kbd = r2[:, 0:2048].rearrange("p (b c h k) -> p b c h k", b=B, c=KC, h=HPC)
        vbd = r2[:, 2048:3072].rearrange("p (g e) -> p g e", e=64)
        xq, xqT = r1[0:T, 0:256].bitcast(BF16), r1[:, 256:384].bitcast(BF16).rearrange("p (k t) -> p k t", k=KC)
        onesb = r1[:, 384:400].bitcast(BF16)
        mixt = r1[0:T, 512:1024]
        fb = r1
        fa, fs, fh = r2[:, 0:512], r2[:, 512:1024], r2[:, 1024:1536]
        fhT = [r2[:, 1536 + 512 * i:2048 + 512 * i].rearrange("p (j h t) -> p j h t", j=4, h=2) for i in range(2)]
        fhTs = r2[:, 2560:2688].rearrange("p (h t) -> p h t", h=2)
        fss = r2[:, 2688:2816]
        fhs = r2[:, 2816:2944]
        gateT = r2[0:E, 2944:3008]
        qTx = r1[:, 0:2048].rearrange("p (g b n) -> p g b n", b=B, n=P)
        qsq, qn = r2[:, 0:512], [r2[:, 512:1024], r2[:, 1024:1536]]
        pb = [r2[:, 512 * i:512 * i + 512] for i in range(3)]
        ptb = [r2[:, 1536 + 512 * i:2048 + 512 * i] for i in range(2)]
        qd = r1[0:DK, 0:2048].rearrange("p (n t) -> p n t", t=T)
        kd = r2[0:DK, 0:2048].rearrange("p (n t) -> p n t", t=T)
        lq, lk = r1[:, 2048:2304], r1[:, 2304:2560]
        lv, vg = kn[0:T, 0, :], kn[0:T, 1, :].rearrange("p (d t) -> p d t", t=32)
        vg2 = r1[:, 2560:2816].rearrange("p (d t) -> p d t", t=16)
        lpen, lp, at = ksq[:, :], r2[:, 2048:2560], r2[:, 2560:3072]
        of = kvw[:, 5, 0:256].rearrange("p (i t) -> p i t", i=4)
        xm, xmT = kvw[0:T, 5, 256:320], kvw[0:T, 5, 320:384]

        ident = cst[:, C_ID:C_ID + P]
        hmask = cst[:, C_HM:C_HM + HPC]
        st6, mv = sc[0:T, 0:6], sc[0:T, 6:8]
        ve, rstd = sc[0:T, 8:9], sc[0:T, 9:10]
        nhalf = sc[:, 10:14]
        r1s, r2s, off1, off2, sss, rsum, row = (sc[:, 14:15], sc[:, 15:16], sc[:, 16:17], sc[:, 17:18], sc[:, 18:19],
                                                sc[0:T, 19:20], sc[0:T, 20:21])
        qmid = sc[:, 21:22]
        nw = sc[:, 22:23]
        mx, sm, rc = sc[:, 24:40], sc[:, 40:56], sc[:, 56:72]
        kss = [sc[:, 72 + 4 * i:76 + 4 * i] for i in range(2)]
        kms = [sc[:, 80 + 4 * i:84 + 4 * i] for i in range(2)]
        rk = [sc[:, 88 + 4 * i:92 + 4 * i] for i in range(2)]
        lg, re, score, gate = sc[:, 96:112], sc[:, 112:128], sc[:, 128:144], sc[:, 144:160]
        gsel = sc[:, 160:168]
        gm, g4, pen4, rz = sc[:, 168:172], sc[:, 172:176], sc[:, 176:180], sc[:, 180:184]
        ms = sc[:, 184:200]
        pmx, psm, prc = sc[:, 200:216], sc[:, 216:232], sc[:, 232:248]
        ge, gsc = sc[0:T, 248:252], sc[0:T, 252:256]
        rw_t = sb("rw_t", [P, 64])
        pairs = r2[:, 0:256].rearrange("p (i j) -> p i j", j=16)
        pairs2 = r2[:, 256:512].rearrange("p (i j) -> p i j", j=16)

        def bank(n):
            return ps[:, n, :]

        def halves(n, lo=0, w=256):
            return [ps[T * h:T * h + T, n, lo:lo + w] for h in range(2)]

        def slot(i):
            return ring[:, i % SLOTS, :]

        def unit(u):
            tile, kind = u // 4, u % 4
            return tile, kind, tile // 4, tile % 4

        def k_of(u):
            return 2 * (u // 4) + u % 4

        def turned(n0, n1):
            return [u for u in range(UNITS) if u % 4 < 2 and n0 <= 4 * u + 6 < n1]

        def ended(n0, n1):
            return [u for u in range(UNITS) if n0 <= 4 * u + 3 < n1]

        def kms_q(m):
            return sc[:, 112 + 4 * m:116 + 4 * m]

        def kd_cols(j):
            return r2[0:DK, 512 * j:512 * j + 512]

        def of_part(j, c):
            return of[NH * j:NH * j + NH, :, :].rearrange("p i (c t) -> p i c t", c=4)[:, :, c:c + 2, :]

        def o_part(j, c):
            v = ps[0:NH, 4 + c:6 + c, 0:256].rearrange("p c (t i e) -> p e i c t", t=16, e=4)
            return v[:, j]

        block = ctx.enter_context(nc.Block())

        @block.sync
        def _(sp):
            def load_item(i):
                if i >= SLOTS:
                    sp.wait_ge(s["item_used"], i - SLOTS + 1)
                if i == 6:
                    sp.wait_ge(s["mix_done"], 1)
                sp.dma_start(slot(i), items_d[i]).then_inc(s[f"slot{i % SLOTS}"], 16)

            sp.dma_start(kvw[:, 0, :], kv_d[0]).then_inc(s["kv_in0"], 16)
            sp.dma_start(x[:, :], x_d).then_inc(s["x_in"], 16)
            sp.dma_start(ctxn[:, 0:4, :], ctx_d[:, 0:4, :]).then_inc(s["ctx_in0"], 16)
            sp.dma_start(kvw[:, 3, :], kv_d[3]).then_inc(s["kv_in3"], 16)
            for i in range(2):
                load_item(i)
            sp.dma_start(kvw[:, 5, :], kv_d[5]).then_inc(s["kv_in5"], 16)
            for i in range(2, 4):
                load_item(i)
            sp.dma_start(kvw[:, 1, :], kv_d[1]).then_inc(s["kv_in1"], 16)
            sp.dma_start(rw_t[:, :], rw_d).then_inc(s["rw_in"], 16)
            for i in range(4, 9):
                load_item(i)
                if i == 5:
                    for g in range(4):
                        sp.dma_start(nmask[32 * g:32 * g + 32, :], mask_d).then_inc(s["mask_in"], 16)
                if i == 7:
                    sp.wait_ge(s["item_used"], I_WO + 1)
                    sp.dma_start(fb[:, :], fb_d).then_inc(s["fb_in"], 16)
            for i in range(9, ITEMS - 4):
                load_item(i)
            sp.wait_ge(s["kv_unit_done"], UNITS)
            for i in range(5):
                sp.dma_start(kvw[:, i, :], l1w_d[i]).then_inc(s[f"l1w_in{i}"], 16)
                if i == 1:
                    sp.wait_ge(s["sx_done"], 8)
                    sp.dma_start(late, late_d).then_inc(s["late_in"], 16)
            for i in range(ITEMS - 4, ITEMS):
                load_item(i)
            for h in range(2):
                sp.wait_ge(s["fin_ready"], h + 1)
                sp.dma_start(out_d[:, 256 * h:256 * h + 256], x[:, 256 * h:256 * h + 256]).then_inc(s["out_done"], 16)
            sp.wait_ge(s["out_done"], 32)

        @block.tensor
        def _(pe):
            def fill(name):
                n0, n1 = FILL_TO[name]
                for n in range(n0, n1):
                    u, kc = n // 4, n % 4
                    tile, kind, b, c = unit(u)
                    if kc == 0:
                        if tile >= 1 and kind < 2:
                            pe.wait_ge(s["v_ready"], 2 * (tile - 1) + kind + 1)
                        if kind >= 2:
                            pe.wait_ge(s["kn_ready"], 2 * tile + kind - 1)
                        if tile == 0:
                            pe.wait_ge(s[f"kv_in{2 + kind}"], 16)
                        if kind == 0 and c == 0:
                            pe.wait_ge(s[f"kv_in{b}"], 16)
                    w = (wkx if kind < 2 else wvx)[kind % 2]
                    mm = pe.matmul(bank(u % 2), ctxT[b][:, kc, P * c:P * c + P], w[:, kc, :],
                                   start=(kc == 0), stop=(kc == KC - 1))
                    if kc == KC - 1:
                        mm.then_inc(s["kv_unit_done"], 1)
                    if kc == 2 and u >= 1 and (u - 1) % 4 < 2:
                        ki = k_of(u - 1)
                        pe.wait_ge(s["kn_ready"], ki + 1)
                        if ki >= 1:
                            pe.wait_ge(s["kT_ready"], ki)
                        for j in range(4):
                            mm = pe.transpose(ps[:, 2, P * j:P * j + P], kn[:, ki % 2, P * j:P * j + P], ident)
                        mm.then_inc(s["kT_psum"], 1)

            def item(i):
                pe.wait_ge(s[f"slot{i % SLOTS}"], 16 * (i // SLOTS + 1))

            def turn_xn(n):
                pe.wait_ge(s["xn_ready"], n)
                for kc in range(KC):
                    mm = pe.transpose(ps[:, 5, T * kc:T * kc + T], xn[:, P * kc:P * kc + P], ident[0:T, 0:T])
                mm.then_inc(s["xnT_psum"], 1)

            def project(n, lhs, w, start=True, stop=True):
                for kc in range(KC):
                    for h in range(2):
                        mm = pe.matmul(halves(n)[h], lhs[:, kc, :], w[:, kc, 256 * h:256 * h + 256],
                                       start=(start and kc == 0), stop=(stop and kc == KC - 1), skip_group_check=True)
                return mm

            pe.wait_ge(s["cst_in"], 16)
            fill("start")
            pe.wait_ge(s["xq_ready"], 1)
            pe.wait_ge(s["const_ready"], 3)
            identb = r1[0:T, 400:432].bitcast(BF16)
            xqTp = ps[:, 5, 0:128].bitcast(BF16).rearrange("p (k t) -> p k t", k=KC)
            for kc in range(KC):
                mm = pe.transpose(xqTp[:, kc, :], xq[:, P * kc:P * kc + P], identb)
            mm.then_inc(s["xqT_psum"], 1)
            fill("quant")
            pe.wait_ge(s["xqT_ready"], 1)
            for b in range(B):
                pe.wait_ge(s["q2_ready"], b + 1)
                for kc in range(KC):
                    for n, lhs in ((4, onesb), (3, xqT[:, kc, S * b:S * b + S])):
                        mm = pe.matmul(ps[S * b:S * b + S, n, :], lhs, q2[:, 4 * b + kc, :],
                                       start=(kc == 0), stop=(kc == KC - 1))
            mm.then_inc(s["mix_done"], 1)
            fill("mix")

            turn_xn(1)
            fill("ln1")
            pe.wait_ge(s["xT_ready"], 1)
            for i, n in ((I_WK, 3), (I_WQ, 4)):
                item(i)
                w = slot(i).rearrange("p (k n) -> p k n", k=KC)
                for c in range(KC):
                    for kc in range(KC):
                        mm = pe.matmul(ps[:, n, T * c:T * c + T], w[:, kc, P * c:P * c + P], xT[:, kc, :],
                                       start=(kc == 0), stop=(kc == KC - 1))
                mm.then_inc(s["item_used"], 1)
            item(I_WV)
            w = slot(I_WV).rearrange("p (k n) -> p k n", k=KC)
            for b in range(B):
                for kc in range(KC):
                    for c in range(KC):
                        mm = pe.matmul(ps[S * c:S * c + S, 6, P * b:P * b + P], xT[:, kc, S * b:S * b + S],
                                       w[:, kc, P * c:P * c + P], start=(kc == 0), stop=(kc == KC - 1),
                                       skip_group_check=True)
            mm.then_inc(s["item_used"], 1)
            fill("heads")
            pe.wait_ge(s["qT_sb"], 1)
            pe.wait_ge(s["kbd_ready"], 2)
            for b in range(B):
                for c in range(KC):
                    mm = pe.matmul(ps[S * c:S * c + S, 7, 256 * b:256 * b + 256], qTs[:, c, S * b:S * b + S],
                                   kbd[:, b, c, :, :], start=True, stop=True)
            mm.then_inc(s["s_done"], 1)
            fill("soft1")
            pe.wait_ge(s["pt_ready"], 1)
            pe.wait_ge(s["vbd_ready"], 4)
            for b in range(B):
                for j in range(HPC):
                    mm = pe.matmul(ps[T * (j // 4):T * (j // 4) + T, 4, T * (j % 4) + S * b:T * (j % 4) + S * b + S],
                                   vbd[:, HPC * b + j, :], probT[:, 256 * b + S * j:256 * b + S * j + S],
                                   start=True, stop=True)
            mm.then_inc(s["o_done"], 1)
            fill("pv1")
            item(I_WO)
            pe.wait_ge(s["ot_ready"], 1)
            project(6, ots, slot(I_WO).rearrange("p (k n) -> p k n", k=KC)).then_inc(s["item_used"], 1)

            fill("ln2")
            turn_xn(2)
            pe.wait_ge(s["xT_ready"], 2)
            pe.wait_ge(s["rw_in"], 16)
            for kc in range(KC):
                for h in range(2):
                    mm = pe.matmul(ps[T * h:T * h + T, 7, 0:E], xT[:, kc, :], rw_t[:, E * kc:E * kc + E],
                                   start=(kc == 0), stop=(kc == KC - 1))
            mm.then_inc(s["router_done"], 1)
            fill("route")

            def expert_in(i, n, done):
                for a in range(2):
                    item(i + a)
                    w = slot(i + a).rearrange("p (k h n) -> p k h n", k=2, h=2)
                    for k in range(2):
                        for h in range(2):
                            mm = pe.matmul(ps[T * h:T * h + T, n, :], xT[:, 2 * a + k, :], w[:, k, h, :],
                                           start=(a == 0 and k == 0), stop=(a == 1 and k == 1))
                    mm.then_inc(s["item_used"], 1)

            expert_in(I_W1A, 3, "h1_done")
            fill("ffn1")
            expert_in(I_W2A, 4, "h2_done")
            item(I_SH)
            pe.wait_ge(s["lg_ready"], 1)
            w = slot(I_SH).rearrange("p (k w h n) -> p k w h n", k=KC, w=2, h=2)
            for wn in range(2):
                for kc in range(KC):
                    for h in range(2):
                        mm = pe.matmul(ps[T * h:T * h + T, 7, P * wn:P * wn + P], xT[:, kc, :], w[:, kc, wn, h, :],
                                       start=(kc == 0), stop=(kc == KC - 1), skip_group_check=True)
            mm.then_inc(s["item_used"], 1)
            pe.wait_ge(s["silu_in"], 1)
            expert_in(I_W1B, 3, "h1_done")
            fill("ffn2")

            def turn_h(src, n, w):
                pe.wait_ge(s["h_ready"], n)
                if n == 1:
                    pe.wait_ge(s["xT_ready"], 2)
                else:
                    pe.wait_ge(s["hT_ready"], n - 1)
                for j in range(w):
                    mm = pe.transpose(ps[:, 5, P * j:P * j + P], src[:, P * j:P * j + P], ident)
                mm.then_inc(s["hT_psum"], 1)

            turn_h(fh, 1, 4)
            expert_in(I_W2B, 4, "h2_done")
            turn_h(fhs, 2, 1)
            fill("ffn3")
            for r in range(2):
                if r == 1:
                    turn_h(fh, 3, 4)
                    fill("ffn4")
                    pe.wait_ge(s["hT_ready"], 3)
                else:
                    pe.wait_ge(s["hT_ready"], 1)
                for a in range(2):
                    i = I_W3 + 2 * r + a
                    item(i)
                    w = slot(i).rearrange("p (j h n) -> p j h n", j=2, h=2)
                    for j in range(2):
                        for e in range(2):
                            for h in range(2):
                                mm = pe.matmul(halves(6)[h], fhT[r][:, 2 * a + j, e, :], w[:, j, e, 256 * h:256 * h + 256],
                                               start=(r + a + j + e == 0), stop=False, skip_group_check=True)
                    mm.then_inc(s["item_used"], 1)
            item(I_SW3)
            pe.wait_ge(s["gate_ready"], 1)
            pe.transpose(ps[0:E, 7, 256:256 + T], gate[0:T, :], ident[0:T, 0:T]).then_inc(s["gateT_psum"], 1)
            w3 = slot(I_SW3)
            for e in range(2):
                for h in range(2):
                    pe.matmul(halves(6)[h], fhTs[:, e, :], w3[:, 512 * e + 256 * h:512 * e + 256 * h + 256],
                              start=False, stop=False, skip_group_check=True)
            pe.wait_ge(s["gateT_ready"], 1)
            for h in range(2):
                mm = pe.matmul(halves(6)[h], gateT, w3[0:E, 1024 + 256 * h:1280 + 256 * h],
                               start=False, stop=True, skip_group_check=True)
            mm.then_inc(s["item_used"], 1)

            fill("ln3")
            turn_xn(3)
            pe.wait_ge(s["xT_ready"], 3)

            def turn_q(m):
                pe.wait_ge(s["qn_ready"], m + 1)
                if m >= 1:
                    pe.wait_ge(s["qTx_ready"], 2 * m)
                for j in range(4):
                    mm = pe.transpose(ps[:, 5, P * j:P * j + P], qn[m % 2][:, P * j:P * j + P], ident)
                mm.then_inc(s["qnT_psum"], 1)

            for m in range(4):
                for a in range(2):
                    i = I_XQ + 2 * m + a
                    item(i)
                    w = slot(i).rearrange("p (k h n) -> p k h n", k=2, h=2)
                    for k in range(2):
                        for h in range(2):
                            mm = pe.matmul(ps[T * h:T * h + T, (3, 4, 6, 7)[m], :], xT[:, 2 * a + k, :], w[:, k, h, :],
                                           start=(a == 0 and k == 0), stop=(a == 1 and k == 1))
                    mm.then_inc(s["item_used"], 1)
                if m >= 1:
                    turn_q(m - 1)
            fill("q0")
            turn_q(3)
            fill("rest")

            NU = KVH * B
            pe.wait_ge(s["kT_ready"], 16)
            pe.wait_ge(s["v_ready"], 16)
            pe.wait_ge(s["qTx_ready"], 8)

            def out_heads(g):
                i = I_XO + g
                item(i)
                pe.wait_ge(s["otx_ready"], 2 * g + 2)
                w = slot(i).rearrange("p (j n) -> p j n", j=GH)
                for j in range(GH):
                    for h in range(2):
                        mm = pe.matmul(halves(7)[h], otx[:, GH * g + j, :], w[:, j, 256 * h:256 * h + 256],
                                       start=(g == 0 and j == 0), stop=(g == KVH - 1 and j == GH - 1),
                                       skip_group_check=True)
                mm.then_inc(s["item_used"], 1)

            for k in range(NU + 3):
                if k < NU:
                    g, b = k // B, k % B
                    if k >= 2:
                        pe.wait_ge(s["pmax_ready"], k - 1)
                    pe.matmul(bank(k % 2), qTx[:, g, b, :], kT[:, g, b, :],
                              start=True, stop=True).then_inc(s["sx_done"], 1)
                u = k - 2
                if 0 <= u < NU:
                    pe.wait_ge(s["pn_ready"], u + 1)
                    if u >= 2:
                        pe.wait_ge(s["ptx_ready"], u - 1)
                    for j in range(4):
                        mm = pe.transpose(ps[:, (2, 5)[u % 2], P * j:P * j + P], pb[u % 3][:, P * j:P * j + P], ident)
                    mm.then_inc(s["ptx_psum"], 1)
                u = k - 3
                if 0 <= u < NU:
                    g, b = u // B, u % B
                    pe.wait_ge(s["ptx_ready"], u + 1)
                    if u >= 2:
                        pe.wait_ge(s["otx_ready"], u - 1)
                    for j in range(4):
                        mm = pe.matmul(ps[:, 3 + u % 2, 0:P], V[:, 4 * b + j, HD * g:HD * g + HD],
                                       ptb[u % 2][:, P * j:P * j + P], start=(j == 0), stop=(j == 3))
                    mm.then_inc(s["ox_done"], 1)
                if u >= 3 and u % 2 == 1:
                    out_heads(u // 2 - 1)
            out_heads(KVH - 1)

            turn_xn(4)
            pe.wait_ge(s["xT_ready"], 4)
            for i, n, done in ((0, 0, "lq_done"), (1, 1, "lk_done"), (2, 2, "lv_done")):
                pe.wait_ge(s[f"l1w_in{i}"], 16)
                project(n, xT, l1w[i]).then_inc(s[done], 1)
            for w, (src, banks, done) in enumerate(((lq, (3, 4, 5, 6), "qd_psum"), (lk, (7, 0, 1, 2), "kd_psum"))):
                pe.wait_ge(s["lqk_sb"], w + 1)
                for q in range(4):
                    if w == 1 and q == 3:
                        pe.wait_ge(s["lv_sb"], 1)
                    for j in range(4):
                        hh = 4 * q + j
                        mm = pe.transpose(ps[0:DK, banks[q], P * j:P * j + P], src[:, DK * hh:DK * hh + DK], ident)
                    mm.then_inc(s[done], 1)
            pe.wait_ge(s["qd_ready"], 4)
            pe.wait_ge(s["kd_ready"], 4)
            for tt in range(16):
                for c in range(4):
                    t = 16 * c + tt
                    mm = pe.matmul(ps[S * c:S * c + S, 3, NH * tt:NH * tt + NH], qd[:, :, t], kd[:, :, t],
                                   start=True, stop=True)
            mm.then_inc(s["ls_done"], 1)
            pe.wait_ge(s["at_ready"], 1)
            pe.wait_ge(s["vg2_ready"], 4)
            for tt in range(16):
                for c in range(4):
                    mm = pe.matmul(ps[0:NH, 4 + c, DK * tt:DK * tt + DK], at[NH * c:NH * c + NH, NH * tt:NH * tt + NH],
                                   vg2[NH * c:NH * c + NH, :, tt], start=True, stop=True)
            mm.then_inc(s["lo_done"], 1)
            pe.wait_ge(s["l1w_in3"], 16)
            pe.wait_ge(s["of_ready"], 8)
            project(0, of, l1w[3]).then_inc(s["ly_done"], 1)

            turn_xn(5)
            pe.wait_ge(s["xT_ready"], 5)
            for kc in range(KC):
                mm = pe.matmul(ps[0:T, 1, 0:68], xT[:, kc, :], late[:, L_AG + 68 * kc:L_AG + 68 * kc + 68],
                               start=(kc == 0), stop=(kc == KC - 1))
            mm.then_inc(s["xa_done"], 1)
            pe.wait_ge(s["l1w_in4"], 16)
            project(3, xT, l1w[4], stop=False)
            pe.wait_ge(s["xm_ready"], 1)
            pe.transpose(ps[0:T, 2, 0:T], xm, ident[0:T, 0:T]).then_inc(s["xmT_psum"], 1)
            pe.wait_ge(s["xmT_ready"], 1)
            for h in range(2):
                pe.matmul(halves(3)[h], xmT, late[0:T, L_BT + 256 * h:L_BT + 256 * h + 256],
                          start=False, stop=True, skip_group_check=True).then_inc(s["f_done"], 1)

        @block.vector
        def _(dve):
            steps = [0]

            def link(ins):
                steps[0] += 1
                ins.then_inc(s["dve_step"], 1)
                dve.wait_ge(s["dve_step"], steps[0])

            def evac(name):
                for u in ended(*FILL_TO[name]):
                    if u % 4 >= 2:
                        continue
                    ki = k_of(u)
                    dve.wait_ge(s["ksq_done"], ki + 1)
                    link(dve.tensor_reduce(kss[ki % 2], ksq[:, :].rearrange("p (g d) -> p g d", d=HD), AX_X, ALU.add))
                    dve.tensor_scalar(kms[ki % 2], kss[ki % 2], 1.0 / HD, LN_EPS, ALU.mult, ALU.add)\
                       .then_inc(s["kms_ready"], 1)
                    dve.wait_ge(s["rk_ready"], ki + 1)
                    if ki >= 2:
                        dve.wait_ge(s["kT_psum"], ki - 1)
                    dve.tensor_tensor(kn[:, ki % 2, :].rearrange("p (g d) -> p g d", d=HD),
                                      bank(u % 2).rearrange("p (g d) -> p g d", d=HD),
                                      rk[ki % 2].unsqueeze(2).to_broadcast([P, 4, HD]), ALU.mult)\
                       .then_inc(s["kn_ready"], 1)

            def normalise(n):
                link(dve.bn_stats(st6, x[:, :]))
                link(dve.bn_aggr(mv, st6))
                dve.tensor_scalar(ve, mv[:, 1:2], LN_EPS, None, ALU.add).then_inc(s["var_ready"], 1)
                dve.wait_ge(s["rstd_ready"], n + 1)
                ins = dve.tensor_scalar(xn[:, :], x[:, :], mv[:, 0:1], rstd, ALU.subtract, ALU.mult)
                if n:
                    ins.then_inc(s["xn_ready"], 1)
                else:
                    link(ins)

            def add_halves(n):
                a = dve.tensor_tensor(x[:, 0:256], halves(n)[0], x[:, 0:256], ALU.add)
                link(a)
                link(dve.tensor_tensor(x[:, 256:512], halves(n)[1], x[:, 256:512], ALU.add))

            dve.memset(nhalf, -0.5).then_inc(s["const_ready"], 1)
            dve.memset(onesb, 1.0).then_inc(s["const_ready"], 1)
            dve.wait_ge(s["cst_in"], 16)
            q = cst[:, C_Q:C_Q + 4]
            dve.tensor_copy(r1[0:T, 400:432].bitcast(BF16), ident[0:T, 0:T]).then_inc(s["const_ready"], 1)
            dve.reciprocal(r1s, q[:, 0:1])
            dve.reciprocal(r2s, q[:, 2:3]).then_inc(s["scal_ready"], 1)
            dve.tensor_scalar(off1, q[:, 1:2], -1.0, QMID, ALU.mult, ALU.add)
            dve.tensor_scalar(off2, q[:, 3:4], -1.0, QMID, ALU.mult, ALU.add)
            dve.tensor_tensor(sss, q[:, 0:1], q[:, 2:3], ALU.mult)
            link(dve.tensor_tensor(nw, cst[:, C_QW:C_QW + 1], cst[:, C_KW:C_KW + 1], ALU.mult))
            link(dve.tensor_scalar(nw, nw, -1.0 / float(np.sqrt(HD)), None, ALU.mult))
            dve.wait_ge(s["x_in"], 16)
            normalise(0)
            link(dve.tensor_scalar(xn[:, :], xn[:, :], r1s[0:T, :], q[0:T, 1:2], ALU.mult, ALU.add))
            link(dve.tensor_scalar(xn[:, :], xn[:, :], 0.0, 255.0, ALU.max, ALU.min))
            dve.tensor_scalar(xq, xn[:, :], MAGIC, MAGIC + QMID, ALU.add, ALU.subtract).then_inc(s["xq_ready"], 1)
            dve.wait_ge(s["xq_ready"], 1)
            link(dve.tensor_reduce(rsum, xq, AX_X, ALU.add))
            link(dve.scalar_tensor_tensor(row, off1[0:T, :], float(CTX), rsum, ALU.mult, ALU.add))
            link(dve.tensor_scalar(row, row, off2[0:T, :], None, ALU.mult))
            evac("start")
            for b in range(B):
                dve.wait_ge(s["ctx_aff"], b + 1)
                link(dve.tensor_scalar(ctxn[:, 4 * b:4 * b + 4, :], ctxn[:, 4 * b:4 * b + 4, :], 0.0, 255.0,
                                       ALU.max, ALU.min))
                dve.tensor_scalar(q2[:, 4 * b:4 * b + 4, :], ctxn[:, 4 * b:4 * b + 4, :], MAGIC, MAGIC + QMID,
                                  ALU.add, ALU.subtract).then_inc(s["q2_ready"], 1)
            evac("quant")
            dve.wait_ge(s["mix_done"], 1)
            link(dve.tensor_scalar(mixt, ps[0:T, 4, :], off1[0:T, :], row, ALU.mult, ALU.add))
            link(dve.tensor_tensor(mixt, ps[0:T, 3, :], mixt, ALU.add))
            link(dve.scalar_tensor_tensor(x[:, :], mixt, sss[0:T, :], x[:, :], ALU.mult, ALU.add))

            normalise(1)
            evac("mix")
            evac("ln1")
            dve.wait_ge(s["item_used"], I_WK + 1)
            for b in range(B):
                kTp = ps[:, 3, 0:256].rearrange("p (c b k) -> p c b k", c=KC, b=B)[:, :, b, :]
                for c in range(KC):
                    ins = dve.tensor_tensor(kbd[:, b, c, :, :], kTp[:, c, :].unsqueeze(1).to_broadcast([P, HPC, S]),
                                            hmask.unsqueeze(2).to_broadcast([P, HPC, S]), ALU.mult)
                ins.then_inc(s["kbd_ready"], 1)
            evac("heads")
            s3 = bank(7).rearrange("p (g k) -> p g k", k=S)
            e3 = bank(3).rearrange("p (g k) -> p g k", k=S)
            wide = [P, 16, S]
            dve.wait_ge(s["s_done"], 1)
            link(dve.tensor_reduce(mx, s3, AX_X, ALU.max))
            dve.tensor_tensor(s3, s3, mx.unsqueeze(2).to_broadcast(wide), ALU.subtract).then_inc(s["s_shift"], 1)
            dve.wait_ge(s["e_done"], 1)
            link(dve.tensor_reduce(sm, e3, AX_X, ALU.add))
            link(dve.reciprocal(rc, sm))
            link(dve.tensor_tensor(prob.rearrange("p (g k) -> p g k", k=S), e3, rc.unsqueeze(2).to_broadcast(wide),
                                   ALU.mult))
            dve.transpose(probT, prob).then_inc(s["pt_ready"], 1)
            evac("soft1")
            evac("pv1")
            dve.wait_ge(s["item_used"], I_WO + 1)
            add_halves(6)

            normalise(2)
            evac("ln2")
            dve.wait_ge(s["router_done"], 1)
            dve.tensor_tensor(lg, ps[:, 7, 0:E], cst[:, C_RB:C_RB + E], ALU.add).then_inc(s["lg_ready"], 1)
            dve.wait_ge(s["lg_ready"], 1)
            dve.tensor_reduce(rz[:, 0:1], lg, AX_X, ALU.max, negate=True).then_inc(s["lg_ready"], 1)
            dve.wait_ge(s["re_done"], 1)
            link(dve.reciprocal(rz[:, 2:3], rz[:, 1:2]))
            link(dve.scalar_tensor_tensor(score, re, rz[:, 2:3], cst[:, C_RBIAS:C_RBIAS + E], ALU.mult, ALU.add))
            link(dve.tensor_reduce(gm, score.rearrange("p (g e) -> p g e", g=GROUPS), AX_X, ALU.max))

            def top2(vals, n, tri, keep):
                a, b2 = pairs[:, 0:n, 0:n], pairs2[:, 0:n, 0:n]
                other, own = vals.unsqueeze(1).to_broadcast([P, n, n]), vals.unsqueeze(2).to_broadcast([P, n, n])
                dve.tensor_tensor(a, other, own, ALU.is_gt)
                link(dve.tensor_tensor(b2, other, own, ALU.is_equal))
                link(dve.tensor_tensor(b2, b2, tri, ALU.mult))
                link(dve.tensor_tensor(a, a, b2, ALU.add))
                link(dve.tensor_reduce(keep, a, AX_X, ALU.add))
                link(dve.tensor_scalar(keep, keep, 1.5, None, ALU.is_lt))

            top2(gm, GROUPS, cst[:, C_T4:C_T4 + 16].rearrange("p (i j) -> p i j", j=4), g4)
            link(dve.tensor_scalar(pen4, g4, 1.0, BIG, ALU.subtract, ALU.mult))
            m4, s4 = (t.rearrange("p (g e) -> p g e", g=GROUPS) for t in (ms, score))
            four = [P, GROUPS, E // GROUPS]
            link(dve.tensor_tensor(m4, s4, g4.unsqueeze(2).to_broadcast(four), ALU.mult))
            link(dve.tensor_tensor(m4, m4, pen4.unsqueeze(2).to_broadcast(four), ALU.add))
            top2(ms, E, cst[:, C_T16:C_T16 + 256].rearrange("p (i j) -> p i j", j=16), gate)
            dve.tensor_tensor(gate, gate, score, ALU.mult).then_inc(s["gate_ready"], 1)
            dve.wait_ge(s["gate_ready"], 1)
            g3 = gate.rearrange("p (r h j) -> p r h j", r=2, h=2)
            gs3 = gsel.rearrange("p (r j) -> p r j", r=2)
            dve.tensor_copy(gs3[0:T], g3[0:T, :, 0, :])
            link(dve.tensor_copy(gs3[T:P], g3[T:P, :, 1, :]))

            def inner(r):
                eb = fb[:, 1024 * r:1024 * r + 1024]
                dve.wait_ge(s["item_used"], (I_W1A, I_W1B)[r] + 2)
                dve.tensor_tensor(fa, bank(3), eb[:, 0:512], ALU.add).then_inc(s["silu_in"], 1)

            def gated(r):
                eb = fb[:, 1024 * r:1024 * r + 1024]
                dve.wait_ge(s["item_used"], (I_W2A, I_W2B)[r] + 2)
                link(dve.tensor_tensor(bank(4), bank(4), eb[:, 512:1024], ALU.add))
                dve.wait_ge(s["silu_done"], (1, 3)[r])
                if r == 1:
                    dve.wait_ge(s["hT_psum"], 1)
                for j in range(4):
                    ins = dve.scalar_tensor_tensor(fh[:, P * j:P * j + P], fs[:, P * j:P * j + P],
                                                   gsel[:, 4 * r + j:4 * r + j + 1], bank(4)[:, P * j:P * j + P],
                                                   ALU.mult, ALU.mult)
                ins.then_inc(s["h_ready"], 1)

            dve.wait_ge(s["fb_in"], 16)
            evac("route")
            inner(0)
            evac("ffn1")
            gated(0)
            dve.wait_ge(s["item_used"], I_SH + 1)
            dve.tensor_tensor(fss, ps[:, 7, 0:P], fb[:, FB_SB:FB_SB + P], ALU.add).then_inc(s["silu_in"], 1)
            dve.tensor_tensor(fhs, ps[:, 7, P:2 * P], fb[:, FB_SB + P:FB_SB + 2 * P], ALU.add).then_inc(s["x_new"], 1)
            dve.wait_ge(s["silu_done"], 2)
            dve.wait_ge(s["x_new"], 1)
            dve.tensor_tensor(fhs, fhs, fss, ALU.mult).then_inc(s["h_ready"], 1)
            inner(1)
            evac("ffn2")
            gated(1)
            link(dve.tensor_tensor(x[:, :], x[:, :], fb[0:T, FB_SB3:FB_SB3 + 512], ALU.add))
            evac("ffn3")
            evac("ffn4")
            dve.wait_ge(s["item_used"], I_SW3 + 1)
            add_halves(6)

            normalise(3)
            evac("ln3")
            for m in range(4):
                dve.wait_ge(s["qsq_done"], m + 1)
                link(dve.tensor_reduce(kms_q(m), qsq.rearrange("p (g d) -> p g d", d=HD), AX_X, ALU.add))
                dve.tensor_scalar(kms_q(m), kms_q(m), 1.0 / HD, LN_EPS, ALU.mult, ALU.add).then_inc(s["qms_ready"], 1)
                dve.wait_ge(s["rq_ready"], m + 1)
                if m >= 2:
                    dve.wait_ge(s["qnT_psum"], m - 1)
                dve.tensor_tensor(qn[m % 2].rearrange("p (g d) -> p g d", d=HD),
                                  bank((3, 4, 6, 7)[m]).rearrange("p (g d) -> p g d", d=HD),
                                  kms_q(m).unsqueeze(2).to_broadcast([P, 4, HD]), ALU.mult).then_inc(s["qn_ready"], 1)
            dve.wait_ge(s["mask_in"], 64)
            link(dve.tensor_scalar(nmask[:, :], nmask[:, :], -1.0, None, ALU.mult))
            evac("q0")
            evac("rest")

            dve.wait_ge(s["qnT_psum"], 4)
            NU = KVH * B

            def out_copy(u):
                g, b = u // B, u % B
                dve.wait_ge(s["ox_done"], u + 1)
                dve.tensor_copy(otx[:, GH * g:GH * g + GH, S * b:S * b + S],
                                ps[:, 3 + u % 2, 0:P].rearrange("p (h t) -> p h t", h=GH)).then_inc(s["otx_ready"], 1)

            for u in range(NU + 2):
                if u < NU:
                    dve.wait_ge(s["sx_done"], u + 1)
                    if u >= 3:
                        dve.wait_ge(s["ptx_psum"], u - 2)
                    dve.tensor_tensor_reduce(pb[u % 3], bank(u % 2), nmask[:, :], 1.0, 3.0e38, ALU.add, ALU.min,
                                             pmx[:, u:u + 1]).then_inc(s["pmax_ready"], 1)
                if u >= 1 and u <= NU:
                    v = u - 1
                    dve.wait_ge(s["pexp_done"], v + 1)
                    link(dve.reciprocal(prc[:, v:v + 1], psm[:, v:v + 1]))
                    dve.tensor_scalar(pb[v % 3], pb[v % 3], prc[:, v:v + 1], None, ALU.mult).then_inc(s["pn_ready"], 1)
                if u >= 4:
                    out_copy(u - 4)
            for u in range(NU - 2, NU):
                out_copy(u)
            dve.wait_ge(s["item_used"], ITEMS)
            add_halves(7)

            normalise(4)
            dve.wait_ge(s["late_in"], 16)
            qkb = late[:, L_QKB:L_QKB + 512]
            rows = late[0:T, L_ROWS:L_ROWS + 1536]
            dve.wait_ge(s["lq_done"], 1)
            dve.tensor_tensor(lq, ps[:, 0, 0:256], qkb[:, 0:256], ALU.add).then_inc(s["lqk_sb"], 1)
            dve.wait_ge(s["lk_done"], 1)
            dve.tensor_tensor(lk, ps[:, 1, 0:256], qkb[:, 256:512], ALU.add).then_inc(s["lqk_sb"], 1)
            dve.wait_ge(s["lv_done"], 1)
            dve.tensor_tensor(lv[:, 0:256], halves(2)[0], rows[:, 0:256], ALU.add)
            dve.tensor_tensor(lv[:, 256:512], halves(2)[1], rows[:, 256:512], ALU.add).then_inc(s["lv_sb"], 1)
            for j, n in enumerate((7, 0, 1, 2)):
                dve.wait_ge(s["kd_psum"], j + 1)
                dve.tensor_copy(kd_cols(j), ps[0:DK, n, :]).then_inc(s["kd_ready"], 1)
                if j == 0:
                    dve.wait_ge(s["lv_sb"], 1)
                    dve.transpose(kn[0:T, 1, :], lv).then_inc(s["vg_ready"], 1)
            link(dve.tensor_tensor(x[:, :], x[:, :], rows[:, 512:1024], ALU.add))
            dve.wait_ge(s["ls_done"], 1)
            link(dve.tensor_scalar(lpen, bank(3), THRESH4, -BIG, ALU.is_le, ALU.mult))
            link(dve.tensor_tensor(bank(3), bank(3), lpen, ALU.add))
            s3 = bank(3).rearrange("p (g k) -> p g k", k=S)
            e3 = bank(2).rearrange("p (g k) -> p g k", k=S)
            link(dve.tensor_reduce(mx, s3, AX_X, ALU.max))
            dve.tensor_tensor(s3, s3, mx.unsqueeze(2).to_broadcast(wide), ALU.subtract).then_inc(s["ls_shift"], 1)
            link(dve.tensor_scalar(ms, mx, -0.5 * BIG, None, ALU.is_gt))
            dve.wait_ge(s["le_done"], 1)
            link(dve.tensor_reduce(sm, e3, AX_X, ALU.add))
            link(dve.tensor_tensor(sm, sm, ms, ALU.mult))
            link(dve.reciprocal(rc, sm))
            link(dve.tensor_tensor(rc, rc, ms, ALU.mult))
            link(dve.tensor_tensor(lp.rearrange("p (g k) -> p g k", k=S), e3, rc.unsqueeze(2).to_broadcast(wide),
                                   ALU.mult))
            dve.transpose(at, lp).then_inc(s["at_ready"], 1)
            dve.wait_ge(s["lo_done"], 1)
            for j in range(4):
                dve.tensor_copy(of_part(j, 0), o_part(j, 0)).then_inc(s["of_ready"], 1)
            dve.wait_ge(s["ly_done"], 1)
            add_halves(0)

            normalise(5)
            link(dve.tensor_tensor(x[:, :], x[:, :], rows[:, 1024:1536], ALU.add))
            dve.wait_ge(s["xa_done"], 1)
            link(dve.tensor_tensor(gsc, ps[0:T, 1, 64:68], cst[0:T, C_GB:C_GB + 4], ALU.add))
            dve.tensor_reduce(rz[0:T, 0:1], gsc, AX_X, ALU.max, negate=True).then_inc(s["ge_in"], 1)
            dve.wait_ge(s["ge_done"], 1)
            top, inv, f = rz[0:T, 1:2], rz[0:T, 2:3], gm[0:T, :]
            link(dve.tensor_reduce(top, ge, AX_X, ALU.max))
            link(dve.reciprocal(inv, top))
            link(dve.tensor_tensor(f[:, 0:1], top, inv, ALU.mult))
            for i in range(1, 4):
                if i > 1:
                    link(dve.tensor_tensor(ge[:, i - 1:i], ge[:, i - 1:i], ge[:, i - 2:i - 1], ALU.max))
                link(dve.scalar_tensor_tensor(f[:, i:i + 1], ge[:, i - 1:i], top, f[:, 0:1], ALU.is_lt, ALU.mult))
            lo = 0
            for i, hi in enumerate(RANKS):
                ins = dve.tensor_scalar(xm[:, lo:hi], ps[0:T, 1, lo:hi], f[:, i:i + 1], None, ALU.mult)
                lo = hi
            ins.then_inc(s["xm_ready"], 1)
            dve.wait_ge(s["xmT_psum"], 1)
            dve.tensor_copy(xmT, ps[0:T, 2, 0:T]).then_inc(s["xmT_ready"], 1)
            for h in range(2):
                dve.wait_ge(s["f_done"], 2)
                dve.tensor_tensor(x[:, 256 * h:256 * h + 256], halves(3)[h], x[:, 256 * h:256 * h + 256], ALU.add)\
                   .then_inc(s["fin_ready"], 1)

        @block.scalar
        def _(act):
            def evac(name):
                n0, n1 = FILL_TO[name]
                for n in range(n0, n1):
                    u = n // 4
                    if n % 4 == 3:
                        tile, kind, b, c = unit(u)
                        act.wait_ge(s["kv_unit_done"], u + 1)
                        if kind < 2:
                            ki = k_of(u)
                            if ki >= 1:
                                act.wait_ge(s["kms_ready"], ki)
                            act.activation(ksq[:, :], bank(u % 2), ACT.Square).then_inc(s["ksq_done"], 1)
                        else:
                            if tile == 4 and kind == 2:
                                act.wait_ge(s["q2_ready"], 2)
                            act.activation(V[:, tile, 512 * (kind - 2):512 * (kind - 2) + 512], bank(u % 2), ACT.Copy)\
                               .then_inc(s["v_ready"], 1)
                    if n % 4 == 2 and u >= 1 and (u - 1) % 4 < 2:
                        ki = k_of(u - 1)
                        tile, kind, b, c = unit(u - 1)
                        act.wait_ge(s["kT_psum"], ki + 1)
                        act.activation(kT[:, 4 * kind:4 * kind + 4, b, P * c:P * c + P],
                                       bank(2).rearrange("p (g n) -> p g n", g=4), ACT.Copy).then_inc(s["kT_ready"], 1)

            def copy_xT(n):
                act.wait_ge(s["xnT_psum"], n)
                act.activation(xT[:, :, :], ps[:, 5, 0:256].rearrange("p (k t) -> p k t", k=KC), ACT.Copy)\
                   .then_inc(s["xT_ready"], 1)

            act.dma_start(kvw[:, 2, :], kv_d[2]).then_inc(s["kv_in2"], 16)
            act.dma_start(cst[:, :], cst_d).then_inc(s["cst_in"], 16)
            act.dma_start(ctxn[:, 4:8, :], ctx_d[:, 4:8, :]).then_inc(s["ctx_in1"], 16)
            act.dma_start(kvw[:, 4, :], kv_d[4]).then_inc(s["kv_in4"], 16)
            evac("start")
            act.wait_ge(s["scal_ready"], 1)
            act.wait_ge(s["xqT_psum"], 1)
            act.activation(xqT, ps[:, 5, 0:128].bitcast(BF16).rearrange("p (k t) -> p k t", k=KC), ACT.Copy)\
               .then_inc(s["xqT_ready"], 1)
            for b in range(B):
                act.wait_ge(s[f"ctx_in{b}"], 16)
                act.activation(ctxn[:, 4 * b:4 * b + 4, :], ctxn[:, 4 * b:4 * b + 4, :], ACT.Identity,
                               bias=cst[:, C_Q + 3:C_Q + 4], scale=r2s).then_inc(s["ctx_aff"], 1)
            evac("quant")
            evac("mix")
            copy_xT(1)
            evac("ln1")
            act.wait_ge(s["item_used"], I_WQ + 1)
            act.activation(qTs, ps[:, 4, 0:256].rearrange("p (c t) -> p c t", c=KC), ACT.Copy).then_inc(s["qT_sb"], 1)
            act.wait_ge(s["item_used"], I_WV + 1)
            act.wait_ge(s["vbd_zero"], 1)
            for c in range(KC):
                act.activation(vbd[S * c:S * c + S, :, DK * c:DK * c + DK],
                               ps[S * c:S * c + S, 6, 0:256].rearrange("p (g d) -> p g d", d=DK), ACT.Copy)\
                   .then_inc(s["vbd_ready"], 1)
            evac("heads")
            act.wait_ge(s["s_shift"], 1)
            act.activation(bank(3), bank(7), ACT.Exp, scale=0.25).then_inc(s["e_done"], 1)
            evac("soft1")
            act.wait_ge(s["o_done"], 1)
            act.activation(ots, ps[:, 4, 0:256].rearrange("p (c t) -> p c t", c=KC), ACT.Copy).then_inc(s["ot_ready"], 1)
            evac("pv1")

            evac("ln2")
            copy_xT(2)
            act.wait_ge(s["lg_ready"], 2)
            act.activation(re, lg, ACT.Exp, bias=rz[:, 0:1], accum_out=rz[:, 1:2]).then_inc(s["re_done"], 1)

            def copy_hT(n, dst, w):
                act.wait_ge(s["hT_psum"], n)
                act.activation(dst, ps[:, 5, 0:w], ACT.Copy).then_inc(s["hT_ready"], 1)

            evac("route")
            act.wait_ge(s["silu_in"], 1)
            act.activation(fs, fa, ACT.Silu).then_inc(s["silu_done"], 1)
            evac("ffn1")
            act.wait_ge(s["silu_in"], 2)
            act.activation(fss, fss, ACT.Silu).then_inc(s["silu_done"], 1)
            act.wait_ge(s["silu_in"], 3)
            act.wait_ge(s["h_ready"], 1)
            act.activation(fs, fa, ACT.Silu).then_inc(s["silu_done"], 1)
            evac("ffn2")
            copy_hT(1, r2[:, 1536:2048], 512)
            copy_hT(2, r2[:, 2560:2688], P)
            evac("ffn3")
            copy_hT(3, r2[:, 2048:2560], 512)
            evac("ffn4")
            act.wait_ge(s["gateT_psum"], 1)
            act.activation(gateT, ps[0:E, 7, 256:256 + T], ACT.Copy).then_inc(s["gateT_ready"], 1)

            evac("ln3")
            copy_xT(3)

            def copy_qT(m):
                act.wait_ge(s["qnT_psum"], m + 1)
                for a in range(2):
                    act.activation(qTx[:, 4 * a + m].rearrange("p b (j t) -> p b j t", j=GH),
                                   bank(5).rearrange("p (j a b t) -> p a b j t", j=GH, a=2, b=B)[:, a], ACT.Copy,
                                   scale=nw).then_inc(s["qTx_ready"], 1)

            for m in range(4):
                act.wait_ge(s["item_used"], I_XQ + 2 * m + 2)
                if m:
                    act.wait_ge(s["qms_ready"], m)
                act.activation(qsq, bank((3, 4, 6, 7)[m]), ACT.Square).then_inc(s["qsq_done"], 1)
                if m:
                    copy_qT(m - 1)
            evac("q0")
            copy_qT(3)
            evac("rest")

            NU = KVH * B
            for u in range(NU + 2):
                if u < NU:
                    act.wait_ge(s["pmax_ready"], u + 1)
                    act.activation(pb[u % 3], pb[u % 3], ACT.Exp, bias=pmx[:, u:u + 1], scale=-1.0,
                                   accum_out=psm[:, u:u + 1]).then_inc(s["pexp_done"], 1)
                if u >= 2:
                    v = u - 2
                    act.wait_ge(s["ptx_psum"], v + 1)
                    if v >= 2:
                        act.wait_ge(s["ox_done"], v - 1)
                    act.activation(ptb[v % 2], bank((2, 5)[v % 2]), ACT.Copy).then_inc(s["ptx_ready"], 1)

            copy_xT(4)
            for j, n in enumerate((3, 4, 5, 6)):
                act.wait_ge(s["qd_psum"], j + 1)
                act.activation(r1[0:DK, 512 * j:512 * j + 512], ps[0:DK, n, :], ACT.Copy).then_inc(s["qd_ready"], 1)
            act.wait_ge(s["vg_ready"], 1)
            for c in range(4):
                tb, th = c // 2, c % 2
                act.activation(vg2[S * c:S * c + S, :, :], vg[S * tb:S * tb + S, :, 16 * th:16 * th + 16], ACT.Copy)\
                   .then_inc(s["vg2_ready"], 1)
            act.wait_ge(s["ls_shift"], 1)
            act.activation(bank(2), bank(3), ACT.Exp, scale=0.25).then_inc(s["le_done"], 1)
            act.wait_ge(s["lo_done"], 1)
            for j in range(4):
                act.activation(of_part(j, 2), o_part(j, 2), ACT.Copy).then_inc(s["of_ready"], 1)
            copy_xT(5)
            act.wait_ge(s["ge_in"], 1)
            act.activation(ge, gsc, ACT.Exp, bias=rz[0:T, 0:1]).then_inc(s["ge_done"], 1)

        @block.gpsimd
        def _(pool):
            def evac(name):
                for u in ended(*FILL_TO[name]):
                    if u % 4 < 2:
                        ki = k_of(u)
                        pool.wait_ge(s["kms_ready"], ki + 1)
                        pool.tensor_tensor(rk[ki % 2], kms[ki % 2], nhalf, ALU.pow).then_inc(s["rk_ready"], 1)

            def rsqrt_var(n):
                pool.wait_ge(s["var_ready"], n + 1)
                pool.tensor_tensor(rstd, ve, nhalf[0:T, 0:1], ALU.pow).then_inc(s["rstd_ready"], 1)

            pool.memset(vbd, 0.0).then_inc(s["vbd_zero"], 1)
            pool.wait_ge(s["const_ready"], 1)
            rsqrt_var(0)
            evac("start")
            evac("quant")
            rsqrt_var(1)
            for name in ("mix", "ln1", "heads", "soft1", "pv1"):
                evac(name)
            rsqrt_var(2)
            for name in ("ln2", "route", "ffn1", "ffn2", "ffn3", "ffn4"):
                evac(name)
            rsqrt_var(3)
            evac("ln3")
            for m in range(4):
                pool.wait_ge(s["qms_ready"], m + 1)
                pool.tensor_tensor(kms_q(m), kms_q(m), nhalf, ALU.pow).then_inc(s["rq_ready"], 1)
            evac("q0")
            evac("rest")
            rsqrt_var(4)
            rsqrt_var(5)


def kernel(**inputs):
    import concourse.bacc as _bacc
    from concourse.bass_utils import run_bass_kernel_spmd as _run

    i = {k: np.asarray(v) for k, v in inputs.items()}
    f32 = np.float32

    def chunks(w, n=P):
        return w.reshape(-1, n, w.shape[1]).transpose(1, 0, 2)

    def rep(v, n=P):
        return np.broadcast_to(v.reshape(1, -1), (n, v.size))

    x_d = i["x"].reshape(T, D)
    ctx = i["ctx_4096"]
    ctx_d = ctx.reshape(B, KC, P, D).transpose(2, 0, 1, 3).reshape(P, B * KC, D)
    tri = lambda n: rep(np.tril(np.ones((n, n), f32), -1))
    cst_d = np.concatenate([
        np.eye(P, dtype=f32), np.kron(np.eye(HPC, dtype=f32), np.ones((DK, 1), f32)), tri(16), tri(4),
        i["L1_xattn_q_norm_w"].reshape(P, 1), i["L1_xattn_k_norm_w"].reshape(P, 1),
        rep(i["L0_ffn_router_b"]), rep(i["L0_ffn_router_bias"]), rep(i["L1_ffn_gate_b"]),
        rep(i["L0_xattn_x1_scale"]), rep(i["L0_xattn_x1_zp"]), rep(i["L0_xattn_x2_scale"]), rep(i["L0_xattn_x2_zp"]),
    ], axis=1)
    wkT, wvT = i["L1_xattn_Wk"].T, i["L1_xattn_Wv"].T
    kv_d = np.stack([chunks(w).reshape(P, SLOT) for w in (
        ctx[0].T, ctx[1].T, wkT[:, :512], wkT[:, 512:], wvT[:, :512], wvT[:, 512:])])

    items = [chunks(i[f"L0_attn_w_{n}"].T).reshape(P, SLOT) for n in "kqv"]
    wo = i["L0_attn_w_o"].T.reshape(KC, 2, 4, DK, D).transpose(1, 0, 3, 2, 4)
    items.append(wo.reshape(P, SLOT))
    ein = [i[f"L0_ffn_ew{n}"].reshape(2, 2, 4, 2, 2, P, INTER).transpose(0, 3, 5, 4, 1, 2, 6).reshape(2, 2, P, SLOT)
           for n in (1, 2)]
    shared = np.stack([i[f"L0_ffn_sw{n}"].reshape(KC, P, 2, INTER) for n in (1, 2)])
    items += [*ein[0][0], *ein[1][0], shared.transpose(2, 1, 0, 3, 4).reshape(P, SLOT), *ein[0][1], *ein[1][1]]
    e3 = i["L0_ffn_ew3"].reshape(2, 2, 2, 2, INTER, D)
    items += list(e3.transpose(0, 2, 4, 3, 1, 5).reshape(4, P, SLOT))
    sw3 = np.zeros((P, SLOT), f32)
    sw3[:, 0:1024] = chunks(i["L0_ffn_sw3"]).reshape(P, 1024)
    sw3[0:E, 1024:1536] = i["L0_ffn_eb3"]
    items.append(sw3)
    wq = i["L1_xattn_Wq"].T.reshape(2, 2, P, 2, 4, 512)
    items += list(wq.transpose(4, 0, 2, 1, 3, 5).reshape(8, P, SLOT))
    items += list(i["L1_xattn_Wo"].T.reshape(KVH, GH, HD, D).transpose(0, 2, 1, 3).reshape(KVH, P, SLOT))
    items_d = np.stack(items)

    eb = np.stack([i[f"L0_ffn_eb{n}"].reshape(2, 2, 512) for n in (1, 2)])
    sbs = np.stack([i[f"L0_ffn_sb{n}"].reshape(2, INTER) for n in (1, 2)])
    fb_d = np.concatenate([
        np.repeat(eb.transpose(2, 1, 0, 3).reshape(2, 2048), T, axis=0),
        np.repeat(sbs.transpose(1, 0, 2).reshape(2, 256), T, axis=0), rep(i["L0_ffn_sb3"])], axis=1)
    rw_d = chunks(i["L0_ffn_router_w"]).reshape(P, 64)
    mask_d = i["mask_1x1xSxS2_ff0"].reshape(S, CTX)

    by_d = lambda w: w.reshape(2, 16, DK, -1).transpose(2, 1, 0, 3).reshape(D, -1)
    lwo = i["L1_attn_Wo"].T.reshape(2, 16, 4, 4, D).transpose(3, 1, 0, 2, 4).reshape(P, SLOT)
    l1w_d = np.stack([chunks(i["L1_attn_Wq"].T).reshape(P, SLOT), chunks(i["L1_attn_Wk"].T).reshape(P, SLOT),
                      chunks(by_d(i["L1_attn_Wv"]).T).reshape(P, SLOT), lwo, chunks(i["L1_ffn_W"].T).reshape(P, SLOT)])
    ag = chunks(np.concatenate([i["L1_ffn_A"].T, i["L1_ffn_gate_w"].T], axis=1)).reshape(P, 272)
    bt = np.concatenate([i["L1_ffn_B"].T, np.zeros((P - 64, D), f32)])
    qkb = np.concatenate([np.repeat(i[f"L1_attn_b{n}"].reshape(2, 256), T, axis=0) for n in "qk"], axis=1)
    late_d = np.concatenate([ag, bt, rep(by_d(i["L1_attn_bv"])), rep(i["L1_attn_bo"]), rep(i["L1_ffn_b"]), qkb], axis=1)

    nc = _bacc.Bacc("TRN2", target_bir_lowering=False, num_devices=1)
    arrays, args = {}, []
    for name, a in (("x", x_d), ("cst", cst_d), ("fb", fb_d), ("rw", rw_d), ("ctx", ctx_d), ("kv", kv_d),
                    ("items", items_d), ("mask", mask_d), ("late", late_d), ("l1w", l1w_d)):
        a = np.ascontiguousarray(a)
        arrays[f"in_{name}"] = a
        args.append(nc.dram_tensor(f"in_{name}", a.shape, mybir.dt.from_np(a.dtype), kind="ExternalInput").ap())
    out = nc.dram_tensor("out_latents", (T, D), F32, kind="ExternalOutput").ap()
    build(nc, *args, out)
    r = _run(nc, [arrays], core_ids=[0])
    return r.results[0]["out_latents"].reshape(B, S, D)
```

```python
from contextlib import ExitStack

import numpy as np

import concourse.bass as bass
from concourse import mybir

F32 = mybir.dt.float32
F32R = mybir.dt.float32r
BF16 = mybir.dt.bfloat16
ALU = mybir.AluOpType
ACT = mybir.ActivationFunctionType
AX_X = mybir.AxisListType.X

P = 128
B, S, D = 2, 32, 512
T = B * S
CTX = 512
KC = D // P
NH, DK = 32, 16
HPC = P // DK
E, INTER, GROUPS = 16, 128, 4
H, KVH, HD = 32, 8, 128
GH = H // KVH
LN_EPS = 1e-5
BIG = 1e30
RANKS = (8, 16, 32, 64)
THRESH4 = 4 * float(np.float32(0.001))
MAGIC = 1.5 * 2.0 ** 23
QMID = 128.0

C_ID, C_HM, C_T16, C_T4 = 0, 128, 136, 392
C_QW, C_KW, C_RB, C_RBIAS, C_GB, C_Q = 408, 409, 410, 426, 442, 446
C_N = 450
FB_EB, FB_SB, FB_SB3, FB_N = 0, 2048, 2304, 2816
L_AG, L_BT, L_ROWS, L_QKB, L_N = 0, 272, 784, 2320, 2832

SLOT = 2048
SLOTS = 5
(I_WK, I_WQ, I_WV, I_WO, I_W1A, I_W2A, I_SH, I_W1B, I_W2B, I_W3, I_SW3, I_XQ, I_XO) = (
    0, 1, 2, 3, 4, 6, 8, 9, 11, 13, 17, 18, 26)
ITEMS = 34

FILL = [("start", 6), ("quant", 9), ("mix", 5), ("ln1", 6), ("heads", 1), ("soft1", 8), ("pv1", 2), ("ln2", 8),
        ("route", 0), ("ffn1", 4), ("ffn2", 4), ("ffn3", 4), ("ffn4", 3), ("ln3", 9), ("q0", 6), ("rest", 53)]
UNITS, TILES = 32, 8
KUNITS = 16
FILL_TO = {}
_n = 0
for _name, _k in FILL:
    FILL_TO[_name] = (_n, _n + _k)
    _n += _k
assert _n == 4 * UNITS

SEMS = """
x_in cst_in fb_in rw_in ctx_in0 ctx_in1 raw_in0 raw_in1 raw_in2 raw_in3 raw_in4 raw_in5 raw_in6 raw_in7 mask_in
late_in l1w_in0 l1w_in1 l1w_in2 l1w_in3 l1w_in4 out_done
slot0 slot1 slot2 slot3 slot4 item_used high_done low_done
dve_step act_step pool_step const_ready scal_ready
var_ready rstd_ready xn_ready xnT_psum xT_ready
xq_ready xqT_psum xqT_ready ctx_aff q2_ready mix_done x_new
kbd_ready qT_sb vbd_zero vbd_ready s_done s_shift e_done pt_ready o_done ot_ready
router_done lg_ready re_done gate_ready gateT_psum gateT_ready
silu_in silu_done h_ready hT_psum hT_ready
qsq_done qms_ready rq_ready qn_ready qnT_psum qTx_ready
kv_unit_done kraw_ready ksq_done kms_ready rk_ready kn_ready kT_psum kT_ready v_ready
sx_done pmax_ready pexp_done pn_ready ptx_psum ptx_ready ox_done otx_ready
lq_done lk_done lv_done lqk_sb lv_sb vg_ready vg2_ready qd_psum kd_psum qd_ready kd_ready ls_done ls_shift le_done
at_ready lo_done of_ready ly_done
xa_done ge_in ge_done xm_ready xmT_psum xmT_ready f_done fin_ready
""".split()


def build(nc, x_d, cst_d, fb_d, rw_d, ctx_d, kv_d, items_d, mask_d, late_d, l1w_d, out_d):
    with ExitStack() as ctx:
        def sb(name, shape, dt=F32):
            return ctx.enter_context(nc.sbuf_tensor(name, shape, dt))

        s = {name: ctx.enter_context(nc.semaphore(name)) for name in SEMS}

        ring = sb("ring", [P, SLOTS, SLOT])
        with nc.sbuf_tensor("cts", [P, 2, B, SLOT], F32R) as cts, nc.sbuf_tensor("wsp", [P, 2, 2, SLOT], F32R) as wsp:
            pass
        lastw = sb("lastw", [P, 8, SLOT])
        kT = sb("kT", [P, KVH, B, CTX])
        V = sb("V", [P, 2, TILES, 512])
        r1 = sb("r1", [P, FB_N])
        r2 = sb("r2", [P, 3072])
        x = sb("x", [T, D])
        xn = sb("xn", [T, D])
        xT = sb("xT", [P, KC, T])
        cst = sb("cst", [P, C_N])
        ksq = sb("ksq", [P, 512])
        kn = sb("kn", [P, 3, 512])
        nmask = kn[:, 2, :]
        sc = sb("sc", [P, 260])
        ps = ctx.enter_context(nc.psum_tensor("ps", [P, 8, 512], F32))

        ctxn = V[:, 0]
        q2 = ring[:, SLOTS - 1, :].bitcast(BF16).rearrange("p (g n) -> p g n", n=512)
        vraw = V[:, 1].rearrange("p t n -> p (t n)")
        kraw = kT[:, 4:8].rearrange("p g b n -> p (g b n)")
        hi_lo = {("c", b): (cts[:, 0, b, :], cts[:, 1, b, :]) for b in range(B)}
        hi_lo |= {("w", p): (wsp[:, p % 2, 0, :], wsp[:, p % 2, 1, :]) for p in range(4)}
        raw = {("c", b): vraw[:, SLOT * b:SLOT * b + SLOT] for b in range(B)}
        raw |= {("w", p): (kraw, vraw)[p // 2][:, SLOT * (p % 2):SLOT * (p % 2) + SLOT] for p in range(4)}
        PIECES = [(key, lo, n) for lo in (0, SLOT // 2) for key in (("c", 0), ("w", 0)) for n in (SLOT // 2,)]
        PIECES += [(key, 0, SLOT) for key in (("c", 1), ("w", 1), ("w", 2), ("w", 3))]
        SPLIT_AFTER = {0: (4,), 1: (5,), TILES: (6,), 2 * TILES: (7,)}
        l1w = [lastw[:, i, :].rearrange("p (k n) -> p k n", k=KC) for i in range(5)]
        otx = lastw[:, 5, :].rearrange("p (h t) -> p h t", t=T)
        late = lastw[:, 6:8, :].rearrange("p a n -> p (a n)")[:, 0:L_N]

        prob, probT = r1[:, 0:512], r1[:, 512:1024]
        qTs = r1[:, 1024:1280].rearrange("p (c t) -> p c t", c=KC)
        ots = r1[:, 1280:1536].rearrange("p (c t) -> p c t", c=KC)
        kbd = r2[:, 0:2048].rearrange("p (b c h k) -> p b c h k", b=B, c=KC, h=HPC)
        vbd = r2[:, 2048:3072].rearrange("p (g e) -> p g e", e=64)
        xq, xqT = r1[0:T, 0:256].bitcast(BF16), r1[:, 256:384].bitcast(BF16).rearrange("p (k t) -> p k t", k=KC)
        onesb = r1[:, 384:400].bitcast(BF16)
        mixt = r1[0:T, 512:1024]
        fb = r1
        fa, fs, fh = r2[:, 0:512], r2[:, 512:1024], r2[:, 1024:1536]
        fhT = [r2[:, 1536 + 512 * i:2048 + 512 * i].rearrange("p (j h t) -> p j h t", j=4, h=2) for i in range(2)]
        fhTs = r2[:, 2560:2688].rearrange("p (h t) -> p h t", h=2)
        fss = r2[:, 2688:2816]
        fhs = r2[:, 2816:2944]
        gateT = r2[0:E, 2944:3008]
        qTx = r1[:, 0:2048].rearrange("p (g b n) -> p g b n", b=B, n=P)
        qsq, qn = r2[:, 0:512], [r2[:, 512:1024], r2[:, 1024:1536]]
        pb = [r2[:, 512 * i:512 * i + 512] for i in range(3)]
        ptb = [r2[:, 1536 + 512 * i:2048 + 512 * i] for i in range(2)]
        qd = r1[0:DK, 0:2048].rearrange("p (n t) -> p n t", t=T)
        kd = r2[0:DK, 0:2048].rearrange("p (n t) -> p n t", t=T)
        lq, lk = r1[:, 2048:2304], r1[:, 2304:2560]
        lv, vg = kn[0:T, 0, :], kn[0:T, 1, :].rearrange("p (d t) -> p d t", t=32)
        vg2 = r1[:, 2560:2816].rearrange("p (d t) -> p d t", t=16)
        lp, at = r2[:, 2048:2560], r2[:, 2560:3072]
        of = lastw[:, 5, 0:256].rearrange("p (i t) -> p i t", i=4)
        xm, xmT = lastw[0:T, 5, 256:320], lastw[0:T, 5, 320:384]

        ident = cst[:, C_ID:C_ID + P]
        hmask = cst[:, C_HM:C_HM + HPC]
        st6, mv = sc[0:T, 0:6], sc[0:T, 6:8]
        ve, rstd = sc[0:T, 8:9], sc[0:T, 9:10]
        nhalf = sc[:, 10:14]
        r1s, r2s, off1, off2, sss, rsum, row = (sc[:, 14:15], sc[:, 15:16], sc[:, 16:17], sc[:, 17:18], sc[:, 18:19],
                                                sc[0:T, 19:20], sc[0:T, 20:21])
        qmid = sc[:, 21:22]
        nw = sc[:, 22:23]
        mx, sm, rc = sc[:, 24:40], sc[:, 40:56], sc[:, 56:72]
        kss = [sc[:, 72 + 4 * i:76 + 4 * i] for i in range(2)]
        kms = [sc[:, 80 + 4 * i:84 + 4 * i] for i in range(2)]
        rk = [sc[:, 88 + 4 * i:92 + 4 * i] for i in range(2)]
        lg, re, score, gate = sc[:, 96:112], sc[:, 112:128], sc[:, 128:144], sc[:, 144:160]
        gsel = sc[:, 160:168]
        gm, g4, pen4, rz = sc[:, 168:172], sc[:, 172:176], sc[:, 176:180], sc[:, 180:184]
        ms = sc[:, 184:200]
        pmx, psm, prc = sc[:, 200:216], sc[:, 216:232], sc[:, 232:248]
        ge, gsc = sc[0:T, 248:252], sc[0:T, 252:256]
        rw_t = sb("rw_t", [P, 64])
        pairs = r2[:, 0:256].rearrange("p (i j) -> p i j", j=16)
        pairs2 = r2[:, 256:512].rearrange("p (i j) -> p i j", j=16)

        def bank(n):
            return ps[:, n, :]

        def halves(n, lo=0, w=256):
            return [ps[T * h:T * h + T, n, lo:lo + w] for h in range(2)]

        def slot(i):
            return ring[:, i % SLOTS, :]

        def turned(n):
            return n // 4 - 3 if n % 4 == 1 and 0 <= n // 4 - 3 < KUNITS else None

        def ended(n0, n1):
            return [u for u in range(UNITS) if n0 <= 4 * u + 3 < n1]

        def kms_q(m):
            return sc[:, 112 + 4 * m:116 + 4 * m]

        def kd_cols(j):
            return r2[0:DK, 512 * j:512 * j + 512]

        def of_part(j, c):
            return of[NH * j:NH * j + NH, :, :].rearrange("p i (c t) -> p i c t", c=4)[:, :, c:c + 2, :]

        def o_part(j, c):
            v = ps[0:NH, 4 + c:6 + c, 0:256].rearrange("p c (t i e) -> p e i c t", t=16, e=4)
            return v[:, j]

        block = ctx.enter_context(nc.Block())

        @block.sync
        def _(sp):
            def load_item(i):
                if i >= SLOTS:
                    sp.wait_ge(s["item_used"], i - SLOTS + 1)
                if i == SLOTS - 1:
                    sp.wait_ge(s["mix_done"], 1)
                sp.dma_start(slot(i), items_d[i]).then_inc(s[f"slot{i % SLOTS}"], 16)

            def load_raw(i):
                key, lo, n = PIECES[i]
                if key == ("w", 2):
                    sp.wait_ge(s["low_done"], 5)
                sp.dma_start(raw[key][:, lo:lo + n], kv_d[key[1] + 2 * (key[0] == "w")][:, lo:lo + n])\
                  .then_inc(s[f"raw_in{i}"], 16)

            sp.dma_start(x[:, :], x_d).then_inc(s["x_in"], 16)
            load_raw(0)
            load_raw(2)
            sp.dma_start(ctxn[:, 0:4, :], ctx_d[:, 0:4, :]).then_inc(s["ctx_in0"], 16)
            load_raw(4)
            load_raw(5)
            load_item(0)
            for i in range(1, 4):
                load_item(i)
            sp.dma_start(rw_t[:, :], rw_d).then_inc(s["rw_in"], 16)
            for i in range(4, 9):
                load_item(i)
                if i == 6:
                    load_raw(6)
                if i == 7:
                    sp.wait_ge(s["item_used"], I_WO + 1)
                    sp.dma_start(fb[:, :], fb_d).then_inc(s["fb_in"], 16)
            load_raw(7)
            for i in range(9, ITEMS - 8 + SLOTS):
                load_item(i)
            sp.wait_ge(s["kT_psum"], KUNITS)
            for g in range(4):
                sp.dma_start(nmask[S * g:S * g + S, :], mask_d).then_inc(s["mask_in"], 16)
            sp.wait_ge(s["kv_unit_done"], UNITS)
            for i in range(5):
                sp.dma_start(lastw[:, i, :], l1w_d[i]).then_inc(s[f"l1w_in{i}"], 16)
            sp.dma_start(late, late_d).then_inc(s["late_in"], 16)
            for i in range(ITEMS - 8 + SLOTS, ITEMS):
                load_item(i)
            for h in range(2):
                sp.wait_ge(s["fin_ready"], h + 1)
                sp.dma_start(out_d[:, 256 * h:256 * h + 256], x[:, 256 * h:256 * h + 256]).then_inc(s["out_done"], 16)
            sp.wait_ge(s["out_done"], 32)

        @block.tensor
        def _(pe):
            def fill(name):
                n0, n1 = FILL_TO[name]
                for n in range(n0, n1):
                    u, kc = n // 4, n % 4
                    part, tile = u // TILES, u % TILES
                    b, c = tile // 4, tile % 4
                    if kc == 0:
                        if 2 <= u < KUNITS + 2:
                            pe.wait_ge(s["kraw_ready"], u - 1)
                        if u >= KUNITS + 2:
                            pe.wait_ge(s["v_ready"], u - KUNITS - 1)
                    if u == 0:
                        pe.wait_ge(s["low_done"], 2 + 2 * (kc // 2))
                    if kc == 0 and u == 4:
                        pe.wait_ge(s["low_done"], 5)
                    if kc == 0 and tile == 0 and part:
                        pe.wait_ge(s["low_done"], 5 + part)
                    hi, lo = (v[:, 512 * kc:512 * kc + 512] for v in hi_lo["w", part])
                    chi, clo = (v[:, 512 * kc + P * c:512 * kc + P * c + P] for v in hi_lo["c", b])
                    for q, (a, w) in enumerate(((chi, hi), (chi, lo), (clo, hi))):
                        mm = pe.matmul(bank(u % 2), a, w, start=(kc == 0 and q == 0), stop=(kc == KC - 1 and q == 2))
                    if kc == KC - 1:
                        mm.then_inc(s["kv_unit_done"], 1)
                    ki = turned(n)
                    if ki is not None:
                        pe.wait_ge(s["kn_ready"], ki + 1)
                        if ki >= 1:
                            pe.wait_ge(s["kT_ready"], ki)
                        for j in range(4):
                            mm = pe.transpose(ps[:, 2, P * j:P * j + P], kn[:, ki % 3, P * j:P * j + P], ident)
                        mm.then_inc(s["kT_psum"], 1)

            def item(i):
                pe.wait_ge(s[f"slot{i % SLOTS}"], 16 * (i // SLOTS + 1))

            def turn_xn(n):
                pe.wait_ge(s["xn_ready"], n)
                for kc in range(KC):
                    mm = pe.transpose(ps[:, 5, T * kc:T * kc + T], xn[:, P * kc:P * kc + P], ident[0:T, 0:T])
                mm.then_inc(s["xnT_psum"], 1)

            def project(n, lhs, w, start=True, stop=True):
                for kc in range(KC):
                    for h in range(2):
                        mm = pe.matmul(halves(n)[h], lhs[:, kc, :], w[:, kc, 256 * h:256 * h + 256],
                                       start=(start and kc == 0), stop=(stop and kc == KC - 1), skip_group_check=True)
                return mm

            fill("start")
            pe.wait_ge(s["xq_ready"], 1)
            pe.wait_ge(s["const_ready"], 3)
            identb = r1[0:T, 400:432].bitcast(BF16)
            xqTp = ps[:, 5, 0:128].bitcast(BF16).rearrange("p (k t) -> p k t", k=KC)
            for kc in range(KC):
                mm = pe.transpose(xqTp[:, kc, :], xq[:, P * kc:P * kc + P], identb)
            mm.then_inc(s["xqT_psum"], 1)
            fill("quant")
            pe.wait_ge(s["xqT_ready"], 1)
            for b in range(B):
                pe.wait_ge(s["q2_ready"], b + 1)
                for kc in range(KC):
                    for n, lhs in ((4, onesb), (3, xqT[:, kc, S * b:S * b + S])):
                        mm = pe.matmul(ps[S * b:S * b + S, n, :], lhs, q2[:, 4 * b + kc, :],
                                       start=(kc == 0), stop=(kc == KC - 1))
            mm.then_inc(s["mix_done"], 1)
            fill("mix")

            turn_xn(1)
            fill("ln1")
            pe.wait_ge(s["xT_ready"], 1)
            for i, n in ((I_WK, 3), (I_WQ, 4)):
                item(i)
                w = slot(i).rearrange("p (k n) -> p k n", k=KC)
                for c in range(KC):
                    for kc in range(KC):
                        mm = pe.matmul(ps[:, n, T * c:T * c + T], w[:, kc, P * c:P * c + P], xT[:, kc, :],
                                       start=(kc == 0), stop=(kc == KC - 1))
                mm.then_inc(s["item_used"], 1)
            item(I_WV)
            w = slot(I_WV).rearrange("p (k n) -> p k n", k=KC)
            for b in range(B):
                for kc in range(KC):
                    for c in range(KC):
                        mm = pe.matmul(ps[S * c:S * c + S, 6, P * b:P * b + P], xT[:, kc, S * b:S * b + S],
                                       w[:, kc, P * c:P * c + P], start=(kc == 0), stop=(kc == KC - 1),
                                       skip_group_check=True)
            mm.then_inc(s["item_used"], 1)
            fill("heads")
            pe.wait_ge(s["qT_sb"], 1)
            pe.wait_ge(s["kbd_ready"], 2)
            for b in range(B):
                for c in range(KC):
                    mm = pe.matmul(ps[S * c:S * c + S, 7, 256 * b:256 * b + 256], qTs[:, c, S * b:S * b + S],
                                   kbd[:, b, c, :, :], start=True, stop=True)
            mm.then_inc(s["s_done"], 1)
            fill("soft1")
            pe.wait_ge(s["pt_ready"], 1)
            pe.wait_ge(s["vbd_ready"], 4)
            for b in range(B):
                for j in range(HPC):
                    mm = pe.matmul(ps[T * (j // 4):T * (j // 4) + T, 4, T * (j % 4) + S * b:T * (j % 4) + S * b + S],
                                   vbd[:, HPC * b + j, :], probT[:, 256 * b + S * j:256 * b + S * j + S],
                                   start=True, stop=True)
            mm.then_inc(s["o_done"], 1)
            fill("pv1")
            item(I_WO)
            pe.wait_ge(s["ot_ready"], 1)
            project(6, ots, slot(I_WO).rearrange("p (k n) -> p k n", k=KC)).then_inc(s["item_used"], 1)

            fill("ln2")
            turn_xn(2)
            pe.wait_ge(s["xT_ready"], 2)
            pe.wait_ge(s["rw_in"], 16)
            for kc in range(KC):
                for h in range(2):
                    mm = pe.matmul(ps[T * h:T * h + T, 7, 0:E], xT[:, kc, :], rw_t[:, E * kc:E * kc + E],
                                   start=(kc == 0), stop=(kc == KC - 1))
            mm.then_inc(s["router_done"], 1)
            fill("route")

            def expert_in(i, n, done):
                for a in range(2):
                    item(i + a)
                    w = slot(i + a).rearrange("p (k h n) -> p k h n", k=2, h=2)
                    for k in range(2):
                        for h in range(2):
                            mm = pe.matmul(ps[T * h:T * h + T, n, :], xT[:, 2 * a + k, :], w[:, k, h, :],
                                           start=(a == 0 and k == 0), stop=(a == 1 and k == 1))
                    mm.then_inc(s["item_used"], 1)

            expert_in(I_W1A, 3, "h1_done")
            fill("ffn1")
            expert_in(I_W2A, 4, "h2_done")
            item(I_SH)
            pe.wait_ge(s["lg_ready"], 1)
            w = slot(I_SH).rearrange("p (k w h n) -> p k w h n", k=KC, w=2, h=2)
            for wn in range(2):
                for kc in range(KC):
                    for h in range(2):
                        mm = pe.matmul(ps[T * h:T * h + T, 7, P * wn:P * wn + P], xT[:, kc, :], w[:, kc, wn, h, :],
                                       start=(kc == 0), stop=(kc == KC - 1), skip_group_check=True)
            mm.then_inc(s["item_used"], 1)
            pe.wait_ge(s["silu_in"], 1)
            expert_in(I_W1B, 3, "h1_done")
            fill("ffn2")

            def turn_h(src, n, w):
                pe.wait_ge(s["h_ready"], n)
                if n == 1:
                    pe.wait_ge(s["xT_ready"], 2)
                else:
                    pe.wait_ge(s["hT_ready"], n - 1)
                for j in range(w):
                    mm = pe.transpose(ps[:, 5, P * j:P * j + P], src[:, P * j:P * j + P], ident)
                mm.then_inc(s["hT_psum"], 1)

            turn_h(fh, 1, 4)
            expert_in(I_W2B, 4, "h2_done")
            turn_h(fhs, 2, 1)
            fill("ffn3")
            for r in range(2):
                if r == 1:
                    turn_h(fh, 3, 4)
                    fill("ffn4")
                    pe.wait_ge(s["hT_ready"], 3)
                else:
                    pe.wait_ge(s["hT_ready"], 1)
                for a in range(2):
                    i = I_W3 + 2 * r + a
                    item(i)
                    w = slot(i).rearrange("p (j h n) -> p j h n", j=2, h=2)
                    for j in range(2):
                        for e in range(2):
                            for h in range(2):
                                mm = pe.matmul(halves(6)[h], fhT[r][:, 2 * a + j, e, :], w[:, j, e, 256 * h:256 * h + 256],
                                               start=(r + a + j + e == 0), stop=False, skip_group_check=True)
                    mm.then_inc(s["item_used"], 1)
            item(I_SW3)
            pe.wait_ge(s["gate_ready"], 1)
            pe.transpose(ps[0:E, 7, 256:256 + T], gate[0:T, :], ident[0:T, 0:T]).then_inc(s["gateT_psum"], 1)
            w3 = slot(I_SW3)
            for e in range(2):
                for h in range(2):
                    pe.matmul(halves(6)[h], fhTs[:, e, :], w3[:, 512 * e + 256 * h:512 * e + 256 * h + 256],
                              start=False, stop=False, skip_group_check=True)
            pe.wait_ge(s["gateT_ready"], 1)
            for h in range(2):
                mm = pe.matmul(halves(6)[h], gateT, w3[0:E, 1024 + 256 * h:1280 + 256 * h],
                               start=False, stop=True, skip_group_check=True)
            mm.then_inc(s["item_used"], 1)

            fill("ln3")
            turn_xn(3)
            pe.wait_ge(s["xT_ready"], 3)

            def turn_q(m):
                pe.wait_ge(s["qn_ready"], m + 1)
                if m >= 1:
                    pe.wait_ge(s["qTx_ready"], 2 * m)
                for j in range(4):
                    mm = pe.transpose(ps[:, 5, P * j:P * j + P], qn[m % 2][:, P * j:P * j + P], ident)
                mm.then_inc(s["qnT_psum"], 1)

            for m in range(4):
                for a in range(2):
                    i = I_XQ + 2 * m + a
                    item(i)
                    w = slot(i).rearrange("p (k h n) -> p k h n", k=2, h=2)
                    for k in range(2):
                        for h in range(2):
                            mm = pe.matmul(ps[T * h:T * h + T, (3, 4, 6, 7)[m], :], xT[:, 2 * a + k, :], w[:, k, h, :],
                                           start=(a == 0 and k == 0), stop=(a == 1 and k == 1))
                    mm.then_inc(s["item_used"], 1)
                if m >= 1:
                    turn_q(m - 1)
            fill("q0")
            turn_q(3)
            fill("rest")

            NU = KVH * B
            pe.wait_ge(s["kT_ready"], 16)
            pe.wait_ge(s["v_ready"], 16)
            pe.wait_ge(s["qTx_ready"], 8)

            def out_heads(g):
                i = I_XO + g
                item(i)
                pe.wait_ge(s["otx_ready"], 2 * g + 2)
                w = slot(i).rearrange("p (j n) -> p j n", j=GH)
                for j in range(GH):
                    for h in range(2):
                        mm = pe.matmul(halves(7)[h], otx[:, GH * g + j, :], w[:, j, 256 * h:256 * h + 256],
                                       start=(g == 0 and j == 0), stop=(g == KVH - 1 and j == GH - 1),
                                       skip_group_check=True)
                mm.then_inc(s["item_used"], 1)

            for k in range(NU + 3):
                if k < NU:
                    g, b = k // B, k % B
                    if k >= 2:
                        pe.wait_ge(s["pmax_ready"], k - 1)
                    pe.matmul(bank(k % 2), qTx[:, g, b, :], kT[:, g, b, :],
                              start=True, stop=True).then_inc(s["sx_done"], 1)
                u = k - 2
                if 0 <= u < NU:
                    pe.wait_ge(s["pn_ready"], u + 1)
                    if u >= 2:
                        pe.wait_ge(s["ptx_ready"], u - 1)
                    for j in range(4):
                        mm = pe.transpose(ps[:, (2, 5)[u % 2], P * j:P * j + P], pb[u % 3][:, P * j:P * j + P], ident)
                    mm.then_inc(s["ptx_psum"], 1)
                u = k - 3
                if 0 <= u < NU:
                    g, b = u // B, u % B
                    pe.wait_ge(s["ptx_ready"], u + 1)
                    if u >= 2:
                        pe.wait_ge(s["otx_ready"], u - 1)
                    for j in range(4):
                        mm = pe.matmul(ps[:, 3 + u % 2, 0:P], V[:, g // 4, 4 * b + j, HD * (g % 4):HD * (g % 4) + HD],
                                       ptb[u % 2][:, P * j:P * j + P], start=(j == 0), stop=(j == 3))
                    mm.then_inc(s["ox_done"], 1)
                if u >= 3 and u % 2 == 1:
                    out_heads(u // 2 - 1)
            out_heads(KVH - 1)

            turn_xn(4)
            pe.wait_ge(s["xT_ready"], 4)
            for i, n, done in ((0, 0, "lq_done"), (1, 1, "lk_done"), (2, 2, "lv_done")):
                pe.wait_ge(s[f"l1w_in{i}"], 16)
                project(n, xT, l1w[i]).then_inc(s[done], 1)
            for w, (src, banks, done) in enumerate(((lq, (3, 4, 5, 6), "qd_psum"), (lk, (7, 0, 1, 2), "kd_psum"))):
                pe.wait_ge(s["lqk_sb"], w + 1)
                for q in range(4):
                    if w == 1 and q == 3:
                        pe.wait_ge(s["lv_sb"], 1)
                    for j in range(4):
                        hh = 4 * q + j
                        mm = pe.transpose(ps[0:DK, banks[q], P * j:P * j + P], src[:, DK * hh:DK * hh + DK], ident)
                    mm.then_inc(s[done], 1)
            pe.wait_ge(s["qd_ready"], 4)
            pe.wait_ge(s["kd_ready"], 4)
            for tt in range(16):
                for c in range(4):
                    t = 16 * c + tt
                    mm = pe.matmul(ps[S * c:S * c + S, 3, NH * tt:NH * tt + NH], qd[:, :, t], kd[:, :, t],
                                   start=True, stop=True)
            mm.then_inc(s["ls_done"], 1)
            pe.wait_ge(s["at_ready"], 1)
            pe.wait_ge(s["vg2_ready"], 4)
            for tt in range(16):
                for c in range(4):
                    mm = pe.matmul(ps[0:NH, 4 + c, DK * tt:DK * tt + DK], at[NH * c:NH * c + NH, NH * tt:NH * tt + NH],
                                   vg2[NH * c:NH * c + NH, :, tt], start=True, stop=True)
            mm.then_inc(s["lo_done"], 1)
            pe.wait_ge(s["l1w_in3"], 16)
            pe.wait_ge(s["of_ready"], 8)
            project(0, of, l1w[3]).then_inc(s["ly_done"], 1)

            turn_xn(5)
            pe.wait_ge(s["xT_ready"], 5)
            for kc in range(KC):
                mm = pe.matmul(ps[0:T, 1, 0:68], xT[:, kc, :], late[:, L_AG + 68 * kc:L_AG + 68 * kc + 68],
                               start=(kc == 0), stop=(kc == KC - 1))
            mm.then_inc(s["xa_done"], 1)
            pe.wait_ge(s["l1w_in4"], 16)
            project(3, xT, l1w[4], stop=False)
            pe.wait_ge(s["xm_ready"], 1)
            pe.transpose(ps[0:T, 2, 0:T], xm, ident[0:T, 0:T]).then_inc(s["xmT_psum"], 1)
            pe.wait_ge(s["xmT_ready"], 1)
            for h in range(2):
                pe.matmul(halves(3)[h], xmT, late[0:T, L_BT + 256 * h:L_BT + 256 * h + 256],
                          start=False, stop=True, skip_group_check=True).then_inc(s["f_done"], 1)

        @block.vector
        def _(dve):
            steps = [0]

            def link(ins):
                steps[0] += 1
                ins.then_inc(s["dve_step"], 1)
                dve.wait_ge(s["dve_step"], steps[0])

            def evac(name):
                for u in ended(*FILL_TO[name]):
                    if 1 <= u <= KUNITS:
                        v = u - 1
                        dve.wait_ge(s["rk_ready"], v + 1)
                        for g in range(4):
                            cols = kn[:, v % 3, HD * g:HD * g + HD]
                            ins = dve.tensor_scalar(cols, cols, rk[v % 2][:, g:g + 1], None, ALU.mult)
                        ins.then_inc(s["kn_ready"], 1)
                    if u < KUNITS:
                        dve.wait_ge(s["ksq_done"], u + 1)
                        link(dve.tensor_reduce(kss[u % 2], ksq[:, :].rearrange("p (g d) -> p g d", d=HD), AX_X, ALU.add))
                        dve.tensor_scalar(kms[u % 2], kss[u % 2], 1.0 / HD, LN_EPS, ALU.mult, ALU.add)\
                           .then_inc(s["kms_ready"], 1)
                    for i in SPLIT_AFTER.get(u, ()):
                        split(i)

            def split(i):
                key, lo, n = PIECES[i]
                dve.wait_ge(s["high_done"], i + 1)
                hi, low = hi_lo[key]
                dve.tensor_tensor(low[:, lo:lo + n], raw[key][:, lo:lo + n], hi[:, lo:lo + n].bitcast(F32),
                                  ALU.subtract).then_inc(s["low_done"], 1)

            def normalise(n):
                link(dve.bn_stats(st6, x[:, :]))
                link(dve.bn_aggr(mv, st6))
                dve.tensor_scalar(ve, mv[:, 1:2], LN_EPS, None, ALU.add).then_inc(s["var_ready"], 1)
                dve.wait_ge(s["rstd_ready"], n + 1)
                ins = dve.tensor_scalar(xn[:, :], x[:, :], mv[:, 0:1], rstd, ALU.subtract, ALU.mult)
                if n:
                    ins.then_inc(s["xn_ready"], 1)
                else:
                    link(ins)

            def add_halves(n):
                a = dve.tensor_tensor(x[:, 0:256], halves(n)[0], x[:, 0:256], ALU.add)
                link(a)
                link(dve.tensor_tensor(x[:, 256:512], halves(n)[1], x[:, 256:512], ALU.add))

            dve.memset(nhalf, -0.5).then_inc(s["const_ready"], 1)
            dve.memset(onesb, 1.0).then_inc(s["const_ready"], 1)
            dve.wait_ge(s["cst_in"], 16)
            q = cst[:, C_Q:C_Q + 4]
            dve.tensor_copy(r1[0:T, 400:432].bitcast(BF16), ident[0:T, 0:T]).then_inc(s["const_ready"], 1)
            dve.reciprocal(r1s, q[:, 0:1])
            dve.reciprocal(r2s, q[:, 2:3]).then_inc(s["scal_ready"], 1)
            dve.tensor_scalar(off1, q[:, 1:2], -1.0, QMID, ALU.mult, ALU.add)
            dve.tensor_scalar(off2, q[:, 3:4], -1.0, QMID, ALU.mult, ALU.add)
            dve.tensor_tensor(sss, q[:, 0:1], q[:, 2:3], ALU.mult)
            link(dve.tensor_tensor(nw, cst[:, C_QW:C_QW + 1], cst[:, C_KW:C_KW + 1], ALU.mult))
            link(dve.tensor_scalar(nw, nw, -1.0 / float(np.sqrt(HD)), None, ALU.mult))
            dve.wait_ge(s["x_in"], 16)
            normalise(0)
            link(dve.tensor_scalar(xn[:, :], xn[:, :], r1s[0:T, :], q[0:T, 1:2], ALU.mult, ALU.add))
            link(dve.tensor_scalar(xn[:, :], xn[:, :], 0.0, 255.0, ALU.max, ALU.min))
            dve.tensor_scalar(xq, xn[:, :], MAGIC, MAGIC + QMID, ALU.add, ALU.subtract).then_inc(s["xq_ready"], 1)
            for i in range(4):
                split(i)
            dve.wait_ge(s["xq_ready"], 1)
            link(dve.tensor_reduce(rsum, xq, AX_X, ALU.add))
            link(dve.scalar_tensor_tensor(row, off1[0:T, :], float(CTX), rsum, ALU.mult, ALU.add))
            link(dve.tensor_scalar(row, row, off2[0:T, :], None, ALU.mult))
            for b in range(B):
                dve.wait_ge(s["ctx_aff"], b + 1)
                link(dve.tensor_scalar(ctxn[:, 4 * b:4 * b + 4, :], ctxn[:, 4 * b:4 * b + 4, :], 0.0, 255.0,
                                       ALU.max, ALU.min))
                dve.tensor_scalar(q2[:, 4 * b:4 * b + 4, :], ctxn[:, 4 * b:4 * b + 4, :], MAGIC, MAGIC + QMID,
                                  ALU.add, ALU.subtract).then_inc(s["q2_ready"], 1)
            evac("start")
            evac("quant")
            dve.wait_ge(s["mix_done"], 1)
            link(dve.tensor_scalar(mixt, ps[0:T, 4, :], off1[0:T, :], row, ALU.mult, ALU.add))
            link(dve.tensor_tensor(mixt, ps[0:T, 3, :], mixt, ALU.add))
            link(dve.scalar_tensor_tensor(x[:, :], mixt, sss[0:T, :], x[:, :], ALU.mult, ALU.add))

            normalise(1)
            evac("mix")
            evac("ln1")
            dve.wait_ge(s["item_used"], I_WK + 1)
            for b in range(B):
                kTp = ps[:, 3, 0:256].rearrange("p (c b k) -> p c b k", c=KC, b=B)[:, :, b, :]
                for c in range(KC):
                    ins = dve.tensor_tensor(kbd[:, b, c, :, :], kTp[:, c, :].unsqueeze(1).to_broadcast([P, HPC, S]),
                                            hmask.unsqueeze(2).to_broadcast([P, HPC, S]), ALU.mult)
                ins.then_inc(s["kbd_ready"], 1)
            evac("heads")
            s3 = bank(7).rearrange("p (g k) -> p g k", k=S)
            e3 = bank(3).rearrange("p (g k) -> p g k", k=S)
            wide = [P, 16, S]
            dve.wait_ge(s["s_done"], 1)
            link(dve.tensor_reduce(mx, s3, AX_X, ALU.max))
            dve.tensor_tensor(s3, s3, mx.unsqueeze(2).to_broadcast(wide), ALU.subtract).then_inc(s["s_shift"], 1)
            dve.wait_ge(s["e_done"], 1)
            link(dve.tensor_reduce(sm, e3, AX_X, ALU.add))
            link(dve.reciprocal(rc, sm))
            link(dve.tensor_tensor(prob.rearrange("p (g k) -> p g k", k=S), e3, rc.unsqueeze(2).to_broadcast(wide),
                                   ALU.mult))
            dve.transpose(probT, prob).then_inc(s["pt_ready"], 1)
            evac("soft1")
            evac("pv1")
            dve.wait_ge(s["item_used"], I_WO + 1)
            add_halves(6)

            normalise(2)
            evac("ln2")
            dve.wait_ge(s["router_done"], 1)
            dve.tensor_tensor(lg, ps[:, 7, 0:E], cst[:, C_RB:C_RB + E], ALU.add).then_inc(s["lg_ready"], 1)
            dve.wait_ge(s["lg_ready"], 1)
            dve.tensor_reduce(rz[:, 0:1], lg, AX_X, ALU.max, negate=True).then_inc(s["lg_ready"], 1)
            dve.wait_ge(s["re_done"], 1)
            link(dve.reciprocal(rz[:, 2:3], rz[:, 1:2]))
            link(dve.scalar_tensor_tensor(score, re, rz[:, 2:3], cst[:, C_RBIAS:C_RBIAS + E], ALU.mult, ALU.add))
            link(dve.tensor_reduce(gm, score.rearrange("p (g e) -> p g e", g=GROUPS), AX_X, ALU.max))

            def top2(vals, n, tri, keep):
                a, b2 = pairs[:, 0:n, 0:n], pairs2[:, 0:n, 0:n]
                other, own = vals.unsqueeze(1).to_broadcast([P, n, n]), vals.unsqueeze(2).to_broadcast([P, n, n])
                dve.tensor_tensor(a, other, own, ALU.is_gt)
                link(dve.tensor_tensor(b2, other, own, ALU.is_equal))
                link(dve.tensor_tensor(b2, b2, tri, ALU.mult))
                link(dve.tensor_tensor(a, a, b2, ALU.add))
                link(dve.tensor_reduce(keep, a, AX_X, ALU.add))
                link(dve.tensor_scalar(keep, keep, 1.5, None, ALU.is_lt))

            top2(gm, GROUPS, cst[:, C_T4:C_T4 + 16].rearrange("p (i j) -> p i j", j=4), g4)
            link(dve.tensor_scalar(pen4, g4, 1.0, BIG, ALU.subtract, ALU.mult))
            m4, s4 = (t.rearrange("p (g e) -> p g e", g=GROUPS) for t in (ms, score))
            four = [P, GROUPS, E // GROUPS]
            link(dve.tensor_tensor(m4, s4, g4.unsqueeze(2).to_broadcast(four), ALU.mult))
            link(dve.tensor_tensor(m4, m4, pen4.unsqueeze(2).to_broadcast(four), ALU.add))
            top2(ms, E, cst[:, C_T16:C_T16 + 256].rearrange("p (i j) -> p i j", j=16), gate)
            dve.tensor_tensor(gate, gate, score, ALU.mult).then_inc(s["gate_ready"], 1)
            dve.wait_ge(s["gate_ready"], 1)
            g3 = gate.rearrange("p (r h j) -> p r h j", r=2, h=2)
            gs3 = gsel.rearrange("p (r j) -> p r j", r=2)
            dve.tensor_copy(gs3[0:T], g3[0:T, :, 0, :])
            link(dve.tensor_copy(gs3[T:P], g3[T:P, :, 1, :]))

            def inner(r):
                eb = fb[:, 1024 * r:1024 * r + 1024]
                dve.wait_ge(s["item_used"], (I_W1A, I_W1B)[r] + 2)
                dve.tensor_tensor(fa, bank(3), eb[:, 0:512], ALU.add).then_inc(s["silu_in"], 1)

            def gated(r):
                eb = fb[:, 1024 * r:1024 * r + 1024]
                dve.wait_ge(s["item_used"], (I_W2A, I_W2B)[r] + 2)
                link(dve.tensor_tensor(bank(4), bank(4), eb[:, 512:1024], ALU.add))
                dve.wait_ge(s["silu_done"], (1, 3)[r])
                if r == 1:
                    dve.wait_ge(s["hT_psum"], 1)
                for j in range(4):
                    ins = dve.scalar_tensor_tensor(fh[:, P * j:P * j + P], fs[:, P * j:P * j + P],
                                                   gsel[:, 4 * r + j:4 * r + j + 1], bank(4)[:, P * j:P * j + P],
                                                   ALU.mult, ALU.mult)
                ins.then_inc(s["h_ready"], 1)

            dve.wait_ge(s["fb_in"], 16)
            evac("route")
            inner(0)
            evac("ffn1")
            gated(0)
            dve.wait_ge(s["item_used"], I_SH + 1)
            dve.tensor_tensor(fss, ps[:, 7, 0:P], fb[:, FB_SB:FB_SB + P], ALU.add).then_inc(s["silu_in"], 1)
            dve.tensor_tensor(fhs, ps[:, 7, P:2 * P], fb[:, FB_SB + P:FB_SB + 2 * P], ALU.add).then_inc(s["x_new"], 1)
            dve.wait_ge(s["silu_done"], 2)
            dve.wait_ge(s["x_new"], 1)
            dve.tensor_tensor(fhs, fhs, fss, ALU.mult).then_inc(s["h_ready"], 1)
            inner(1)
            evac("ffn2")
            gated(1)
            link(dve.tensor_tensor(x[:, :], x[:, :], fb[0:T, FB_SB3:FB_SB3 + 512], ALU.add))
            evac("ffn3")
            evac("ffn4")
            dve.wait_ge(s["item_used"], I_SW3 + 1)
            add_halves(6)

            normalise(3)
            evac("ln3")
            for m in range(4):
                dve.wait_ge(s["qsq_done"], m + 1)
                link(dve.tensor_reduce(kms_q(m), qsq.rearrange("p (g d) -> p g d", d=HD), AX_X, ALU.add))
                dve.tensor_scalar(kms_q(m), kms_q(m), 1.0 / HD, LN_EPS, ALU.mult, ALU.add).then_inc(s["qms_ready"], 1)
                dve.wait_ge(s["rq_ready"], m + 1)
                if m >= 2:
                    dve.wait_ge(s["qnT_psum"], m - 1)
                dve.tensor_tensor(qn[m % 2].rearrange("p (g d) -> p g d", d=HD),
                                  bank((3, 4, 6, 7)[m]).rearrange("p (g d) -> p g d", d=HD),
                                  kms_q(m).unsqueeze(2).to_broadcast([P, 4, HD]), ALU.mult).then_inc(s["qn_ready"], 1)
            evac("q0")
            evac("rest")
            dve.wait_ge(s["mask_in"], 64)
            link(dve.tensor_scalar(nmask, nmask, -1.0, None, ALU.mult))

            dve.wait_ge(s["qnT_psum"], 4)
            NU = KVH * B

            def out_copy(u):
                g, b = u // B, u % B
                dve.wait_ge(s["ox_done"], u + 1)
                dve.tensor_copy(otx[:, GH * g:GH * g + GH, S * b:S * b + S],
                                ps[:, 3 + u % 2, 0:P].rearrange("p (h t) -> p h t", h=GH)).then_inc(s["otx_ready"], 1)

            for u in range(NU + 2):
                if u < NU:
                    dve.wait_ge(s["sx_done"], u + 1)
                    if u >= 3:
                        dve.wait_ge(s["ptx_psum"], u - 2)
                    dve.tensor_tensor_reduce(pb[u % 3], bank(u % 2), nmask, 1.0, 3.0e38, ALU.add, ALU.min,
                                             pmx[:, u:u + 1]).then_inc(s["pmax_ready"], 1)
                if u >= 1 and u <= NU:
                    v = u - 1
                    dve.wait_ge(s["pexp_done"], v + 1)
                    link(dve.reciprocal(prc[:, v:v + 1], psm[:, v:v + 1]))
                    dve.tensor_scalar(pb[v % 3], pb[v % 3], prc[:, v:v + 1], None, ALU.mult).then_inc(s["pn_ready"], 1)
                if u >= 4:
                    out_copy(u - 4)
            for u in range(NU - 2, NU):
                out_copy(u)
            dve.wait_ge(s["item_used"], ITEMS)
            add_halves(7)

            normalise(4)
            dve.wait_ge(s["late_in"], 16)
            qkb = late[:, L_QKB:L_QKB + 512]
            rows = late[0:T, L_ROWS:L_ROWS + 1536]
            dve.wait_ge(s["lq_done"], 1)
            dve.tensor_tensor(lq, ps[:, 0, 0:256], qkb[:, 0:256], ALU.add).then_inc(s["lqk_sb"], 1)
            dve.wait_ge(s["lk_done"], 1)
            dve.tensor_tensor(lk, ps[:, 1, 0:256], qkb[:, 256:512], ALU.add).then_inc(s["lqk_sb"], 1)
            dve.wait_ge(s["lv_done"], 1)
            dve.tensor_tensor(lv[:, 0:256], halves(2)[0], rows[:, 0:256], ALU.add)
            dve.tensor_tensor(lv[:, 256:512], halves(2)[1], rows[:, 256:512], ALU.add).then_inc(s["lv_sb"], 1)
            for j, n in enumerate((7, 0, 1, 2)):
                dve.wait_ge(s["kd_psum"], j + 1)
                dve.tensor_copy(kd_cols(j), ps[0:DK, n, :]).then_inc(s["kd_ready"], 1)
                if j == 0:
                    dve.wait_ge(s["lv_sb"], 1)
                    dve.transpose(kn[0:T, 1, :], lv).then_inc(s["vg_ready"], 1)
            link(dve.tensor_tensor(x[:, :], x[:, :], rows[:, 512:1024], ALU.add))
            dve.wait_ge(s["ls_done"], 1)
            s3 = bank(3).rearrange("p (g k) -> p g k", k=S)
            l3 = lp.rearrange("p (g k) -> p g k", k=S)
            link(dve.tensor_reduce(mx, s3, AX_X, ALU.max))
            dve.tensor_tensor(l3, s3, mx.unsqueeze(2).to_broadcast(wide), ALU.subtract).then_inc(s["ls_shift"], 1)
            dve.wait_ge(s["le_done"], 1)
            link(dve.scalar_tensor_tensor(bank(3), bank(3), THRESH4, lp, ALU.is_gt, ALU.mult))
            link(dve.tensor_reduce(sm, s3, AX_X, ALU.add))
            link(dve.reciprocal(rc, sm))
            link(dve.tensor_tensor(l3, s3, rc.unsqueeze(2).to_broadcast(wide), ALU.mult))
            dve.transpose(at, lp).then_inc(s["at_ready"], 1)
            dve.wait_ge(s["lo_done"], 1)
            for j in range(4):
                dve.tensor_copy(of_part(j, 0), o_part(j, 0)).then_inc(s["of_ready"], 1)
            dve.wait_ge(s["ly_done"], 1)
            add_halves(0)

            normalise(5)
            link(dve.tensor_tensor(x[:, :], x[:, :], rows[:, 1024:1536], ALU.add))
            dve.wait_ge(s["xa_done"], 1)
            link(dve.tensor_tensor(gsc, ps[0:T, 1, 64:68], cst[0:T, C_GB:C_GB + 4], ALU.add))
            dve.tensor_reduce(rz[0:T, 0:1], gsc, AX_X, ALU.max, negate=True).then_inc(s["ge_in"], 1)
            dve.wait_ge(s["ge_done"], 1)
            top, inv, f = rz[0:T, 1:2], rz[0:T, 2:3], gm[0:T, :]
            link(dve.tensor_reduce(top, ge, AX_X, ALU.max))
            link(dve.reciprocal(inv, top))
            link(dve.tensor_tensor(f[:, 0:1], top, inv, ALU.mult))
            for i in range(1, 4):
                if i > 1:
                    link(dve.tensor_tensor(ge[:, i - 1:i], ge[:, i - 1:i], ge[:, i - 2:i - 1], ALU.max))
                link(dve.scalar_tensor_tensor(f[:, i:i + 1], ge[:, i - 1:i], top, f[:, 0:1], ALU.is_lt, ALU.mult))
            lo = 0
            for i, hi in enumerate(RANKS):
                ins = dve.tensor_scalar(xm[:, lo:hi], ps[0:T, 1, lo:hi], f[:, i:i + 1], None, ALU.mult)
                lo = hi
            ins.then_inc(s["xm_ready"], 1)
            dve.wait_ge(s["xmT_psum"], 1)
            dve.tensor_copy(xmT, ps[0:T, 2, 0:T]).then_inc(s["xmT_ready"], 1)
            for h in range(2):
                dve.wait_ge(s["f_done"], 2)
                dve.tensor_tensor(x[:, 256 * h:256 * h + 256], halves(3)[h], x[:, 256 * h:256 * h + 256], ALU.add)\
                   .then_inc(s["fin_ready"], 1)

        @block.scalar
        def _(act):
            def evac(name):
                n0, n1 = FILL_TO[name]
                for n in range(n0, n1):
                    u = n // 4
                    ki = turned(n)
                    if ki is not None:
                        act.wait_ge(s["kT_psum"], ki + 1)
                        g, b, c = 4 * (ki // TILES), ki % TILES // 4, ki % 4
                        act.activation(kT[:, g:g + 4, b, P * c:P * c + P],
                                       bank(2).rearrange("p (g n) -> p g n", g=4), ACT.Copy).then_inc(s["kT_ready"], 1)
                    if n % 4 != 3:
                        continue
                    if u < KUNITS:
                        act.wait_ge(s["kv_unit_done"], u + 1)
                        if u >= 3:
                            act.wait_ge(s["kT_psum"], u - 2)
                        act.activation(kn[:, u % 3, :], bank(u % 2), ACT.Copy).then_inc(s["kraw_ready"], 1)
                        act.wait_ge(s["kraw_ready"], u + 1)
                        if u:
                            act.wait_ge(s["kms_ready"], u)
                        act.activation(ksq[:, :], kn[:, u % 3, :], ACT.Square).then_inc(s["ksq_done"], 1)
                    else:
                        act.wait_ge(s["kv_unit_done"], u + 1)
                        if u == KUNITS:
                            act.wait_ge(s["q2_ready"], 2)
                        if u == KUNITS + TILES:
                            act.wait_ge(s["low_done"], 8)
                        act.activation(V[:, u // TILES - 2, u % TILES, :], bank(u % 2), ACT.Copy)\
                           .then_inc(s["v_ready"], 1)
                    for i in SPLIT_AFTER.get(u, ()):
                        split(i)

            def split(i):
                key, lo, n = PIECES[i]
                act.wait_ge(s[f"raw_in{i}"], 16)
                if key[0] == "w" and key[1] >= 2:
                    act.wait_ge(s["kv_unit_done"], TILES * (key[1] - 1))
                act.activation(hi_lo[key][0][:, lo:lo + n], raw[key][:, lo:lo + n], ACT.Copy)\
                   .then_inc(s["high_done"], 1)

            def copy_xT(n):
                act.wait_ge(s["xnT_psum"], n)
                act.activation(xT[:, :, :], ps[:, 5, 0:256].rearrange("p (k t) -> p k t", k=KC), ACT.Copy)\
                   .then_inc(s["xT_ready"], 1)

            act.dma_start(cst[:, :], cst_d).then_inc(s["cst_in"], 16)
            for i in (1, 3):
                key, lo, n = PIECES[i]
                act.dma_start(raw[key][:, lo:lo + n], kv_d[2][:, lo:lo + n]).then_inc(s[f"raw_in{i}"], 16)
            act.dma_start(ctxn[:, 4:8, :], ctx_d[:, 4:8, :]).then_inc(s["ctx_in1"], 16)
            act.wait_ge(s["const_ready"], 1)
            act.activation(sc[:, 256:257], nhalf[:, 0:1], ACT.Copy)
            for i in range(4):
                split(i)
            act.wait_ge(s["scal_ready"], 1)
            act.wait_ge(s["xqT_psum"], 1)
            act.activation(xqT, ps[:, 5, 0:128].bitcast(BF16).rearrange("p (k t) -> p k t", k=KC), ACT.Copy)\
               .then_inc(s["xqT_ready"], 1)
            for b in range(B):
                act.wait_ge(s[f"ctx_in{b}"], 16)
                act.activation(ctxn[:, 4 * b:4 * b + 4, :], ctxn[:, 4 * b:4 * b + 4, :], ACT.Identity,
                               bias=cst[:, C_Q + 3:C_Q + 4], scale=r2s).then_inc(s["ctx_aff"], 1)
            evac("start")
            evac("quant")
            evac("mix")
            copy_xT(1)
            evac("ln1")
            act.wait_ge(s["item_used"], I_WQ + 1)
            act.activation(qTs, ps[:, 4, 0:256].rearrange("p (c t) -> p c t", c=KC), ACT.Copy).then_inc(s["qT_sb"], 1)
            act.wait_ge(s["item_used"], I_WV + 1)
            act.wait_ge(s["vbd_zero"], 1)
            for c in range(KC):
                act.activation(vbd[S * c:S * c + S, :, DK * c:DK * c + DK],
                               ps[S * c:S * c + S, 6, 0:256].rearrange("p (g d) -> p g d", d=DK), ACT.Copy)\
                   .then_inc(s["vbd_ready"], 1)
            evac("heads")
            act.wait_ge(s["s_shift"], 1)
            act.activation(bank(3), bank(7), ACT.Exp, scale=0.25).then_inc(s["e_done"], 1)
            evac("soft1")
            act.wait_ge(s["o_done"], 1)
            act.activation(ots, ps[:, 4, 0:256].rearrange("p (c t) -> p c t", c=KC), ACT.Copy).then_inc(s["ot_ready"], 1)
            evac("pv1")

            evac("ln2")
            copy_xT(2)
            act.wait_ge(s["lg_ready"], 2)
            act.activation(re, lg, ACT.Exp, bias=rz[:, 0:1], accum_out=rz[:, 1:2]).then_inc(s["re_done"], 1)

            def copy_hT(n, dst, w):
                act.wait_ge(s["hT_psum"], n)
                act.activation(dst, ps[:, 5, 0:w], ACT.Copy).then_inc(s["hT_ready"], 1)

            evac("route")
            act.wait_ge(s["silu_in"], 1)
            act.activation(fs, fa, ACT.Silu).then_inc(s["silu_done"], 1)
            evac("ffn1")
            act.wait_ge(s["silu_in"], 2)
            act.activation(fss, fss, ACT.Silu).then_inc(s["silu_done"], 1)
            act.wait_ge(s["silu_in"], 3)
            act.wait_ge(s["h_ready"], 1)
            act.activation(fs, fa, ACT.Silu).then_inc(s["silu_done"], 1)
            evac("ffn2")
            copy_hT(1, r2[:, 1536:2048], 512)
            copy_hT(2, r2[:, 2560:2688], P)
            evac("ffn3")
            copy_hT(3, r2[:, 2048:2560], 512)
            evac("ffn4")
            act.wait_ge(s["gateT_psum"], 1)
            act.activation(gateT, ps[0:E, 7, 256:256 + T], ACT.Copy).then_inc(s["gateT_ready"], 1)

            evac("ln3")
            copy_xT(3)

            def copy_qT(m):
                act.wait_ge(s["qnT_psum"], m + 1)
                for a in range(2):
                    act.activation(qTx[:, 4 * a + m].rearrange("p b (j t) -> p b j t", j=GH),
                                   bank(5).rearrange("p (j a b t) -> p a b j t", j=GH, a=2, b=B)[:, a], ACT.Copy,
                                   scale=nw).then_inc(s["qTx_ready"], 1)

            for m in range(4):
                act.wait_ge(s["item_used"], I_XQ + 2 * m + 2)
                if m:
                    act.wait_ge(s["qms_ready"], m)
                act.activation(qsq, bank((3, 4, 6, 7)[m]), ACT.Square).then_inc(s["qsq_done"], 1)
                if m:
                    copy_qT(m - 1)
            evac("q0")
            copy_qT(3)
            evac("rest")

            NU = KVH * B
            for u in range(NU + 2):
                if u < NU:
                    act.wait_ge(s["pmax_ready"], u + 1)
                    act.activation(pb[u % 3], pb[u % 3], ACT.Exp, bias=pmx[:, u:u + 1], scale=-1.0,
                                   accum_out=psm[:, u:u + 1]).then_inc(s["pexp_done"], 1)
                if u >= 2:
                    v = u - 2
                    act.wait_ge(s["ptx_psum"], v + 1)
                    if v >= 2:
                        act.wait_ge(s["ox_done"], v - 1)
                    act.activation(ptb[v % 2], bank((2, 5)[v % 2]), ACT.Copy).then_inc(s["ptx_ready"], 1)

            copy_xT(4)
            for j, n in enumerate((3, 4, 5, 6)):
                act.wait_ge(s["qd_psum"], j + 1)
                act.activation(r1[0:DK, 512 * j:512 * j + 512], ps[0:DK, n, :], ACT.Copy).then_inc(s["qd_ready"], 1)
            act.wait_ge(s["vg_ready"], 1)
            for c in range(4):
                tb, th = c // 2, c % 2
                act.activation(vg2[S * c:S * c + S, :, :], vg[S * tb:S * tb + S, :, 16 * th:16 * th + 16], ACT.Copy)\
                   .then_inc(s["vg2_ready"], 1)
            act.wait_ge(s["ls_shift"], 1)
            act.activation(lp, lp, ACT.Exp, scale=0.25).then_inc(s["le_done"], 1)
            act.wait_ge(s["lo_done"], 1)
            for j in range(4):
                act.activation(of_part(j, 2), o_part(j, 2), ACT.Copy).then_inc(s["of_ready"], 1)
            copy_xT(5)
            act.wait_ge(s["ge_in"], 1)
            act.activation(ge, gsc, ACT.Exp, bias=rz[0:T, 0:1]).then_inc(s["ge_done"], 1)

        @block.gpsimd
        def _(pool):
            def evac(name):
                for u in ended(*FILL_TO[name]):
                    if u < KUNITS:
                        pool.wait_ge(s["kms_ready"], u + 1)
                        pool.tensor_tensor(rk[u % 2], kms[u % 2], nhalf, ALU.pow).then_inc(s["rk_ready"], 1)

            def rsqrt_var(n):
                pool.wait_ge(s["var_ready"], n + 1)
                pool.tensor_tensor(rstd, ve, nhalf[0:T, 0:1], ALU.pow).then_inc(s["rstd_ready"], 1)

            pool.memset(vbd, 0.0).then_inc(s["vbd_zero"], 1)
            pool.wait_ge(s["const_ready"], 1)
            rsqrt_var(0)
            evac("start")
            evac("quant")
            rsqrt_var(1)
            for name in ("mix", "ln1", "heads", "soft1", "pv1"):
                evac(name)
            rsqrt_var(2)
            for name in ("ln2", "route", "ffn1", "ffn2", "ffn3", "ffn4"):
                evac(name)
            rsqrt_var(3)
            evac("ln3")
            for m in range(4):
                pool.wait_ge(s["qms_ready"], m + 1)
                pool.tensor_tensor(kms_q(m), kms_q(m), nhalf, ALU.pow).then_inc(s["rq_ready"], 1)
            evac("q0")
            evac("rest")
            rsqrt_var(4)
            rsqrt_var(5)


def kernel(**inputs):
    import concourse.bacc as _bacc
    from concourse.bass_utils import run_bass_kernel_spmd as _run

    i = {k: np.asarray(v) for k, v in inputs.items()}
    f32 = np.float32

    def chunks(w, n=P):
        return w.reshape(-1, n, w.shape[1]).transpose(1, 0, 2)

    def rep(v, n=P):
        return np.broadcast_to(v.reshape(1, -1), (n, v.size))

    x_d = i["x"].reshape(T, D)
    ctx = i["ctx_4096"]
    ctx_d = ctx.reshape(B, KC, P, D).transpose(2, 0, 1, 3).reshape(P, B * KC, D)
    tri = lambda n: rep(np.tril(np.ones((n, n), f32), -1))
    cst_d = np.concatenate([
        np.eye(P, dtype=f32), np.kron(np.eye(HPC, dtype=f32), np.ones((DK, 1), f32)), tri(16), tri(4),
        i["L1_xattn_q_norm_w"].reshape(P, 1), i["L1_xattn_k_norm_w"].reshape(P, 1),
        rep(i["L0_ffn_router_b"]), rep(i["L0_ffn_router_bias"]), rep(i["L1_ffn_gate_b"]),
        rep(i["L0_xattn_x1_scale"]), rep(i["L0_xattn_x1_zp"]), rep(i["L0_xattn_x2_scale"]), rep(i["L0_xattn_x2_zp"]),
    ], axis=1)
    wkT, wvT = i["L1_xattn_Wk"].T, i["L1_xattn_Wv"].T
    kv_d = np.stack([chunks(w).reshape(P, SLOT) for w in (
        ctx[0].T, ctx[1].T, wkT[:, :512], wkT[:, 512:], wvT[:, :512], wvT[:, 512:])])

    items = [chunks(i[f"L0_attn_w_{n}"].T).reshape(P, SLOT) for n in "kqv"]
    wo = i["L0_attn_w_o"].T.reshape(KC, 2, 4, DK, D).transpose(1, 0, 3, 2, 4)
    items.append(wo.reshape(P, SLOT))
    ein = [i[f"L0_ffn_ew{n}"].reshape(2, 2, 4, 2, 2, P, INTER).transpose(0, 3, 5, 4, 1, 2, 6).reshape(2, 2, P, SLOT)
           for n in (1, 2)]
    shared = np.stack([i[f"L0_ffn_sw{n}"].reshape(KC, P, 2, INTER) for n in (1, 2)])
    items += [*ein[0][0], *ein[1][0], shared.transpose(2, 1, 0, 3, 4).reshape(P, SLOT), *ein[0][1], *ein[1][1]]
    e3 = i["L0_ffn_ew3"].reshape(2, 2, 2, 2, INTER, D)
    items += list(e3.transpose(0, 2, 4, 3, 1, 5).reshape(4, P, SLOT))
    sw3 = np.zeros((P, SLOT), f32)
    sw3[:, 0:1024] = chunks(i["L0_ffn_sw3"]).reshape(P, 1024)
    sw3[0:E, 1024:1536] = i["L0_ffn_eb3"]
    items.append(sw3)
    wq = i["L1_xattn_Wq"].T.reshape(2, 2, P, 2, 4, 512)
    items += list(wq.transpose(4, 0, 2, 1, 3, 5).reshape(8, P, SLOT))
    items += list(i["L1_xattn_Wo"].T.reshape(KVH, GH, HD, D).transpose(0, 2, 1, 3).reshape(KVH, P, SLOT))
    items_d = np.stack(items)

    eb = np.stack([i[f"L0_ffn_eb{n}"].reshape(2, 2, 512) for n in (1, 2)])
    sbs = np.stack([i[f"L0_ffn_sb{n}"].reshape(2, INTER) for n in (1, 2)])
    fb_d = np.concatenate([
        np.repeat(eb.transpose(2, 1, 0, 3).reshape(2, 2048), T, axis=0),
        np.repeat(sbs.transpose(1, 0, 2).reshape(2, 256), T, axis=0), rep(i["L0_ffn_sb3"])], axis=1)
    rw_d = chunks(i["L0_ffn_router_w"]).reshape(P, 64)
    mask_d = i["mask_1x1xSxS2_ff0"].reshape(S, CTX)

    by_d = lambda w: w.reshape(2, 16, DK, -1).transpose(2, 1, 0, 3).reshape(D, -1)
    lwo = i["L1_attn_Wo"].T.reshape(2, 16, 4, 4, D).transpose(3, 1, 0, 2, 4).reshape(P, SLOT)
    l1w_d = np.stack([chunks(i["L1_attn_Wq"].T).reshape(P, SLOT), chunks(i["L1_attn_Wk"].T).reshape(P, SLOT),
                      chunks(by_d(i["L1_attn_Wv"]).T).reshape(P, SLOT), lwo, chunks(i["L1_ffn_W"].T).reshape(P, SLOT)])
    ag = chunks(np.concatenate([i["L1_ffn_A"].T, i["L1_ffn_gate_w"].T], axis=1)).reshape(P, 272)
    bt = np.concatenate([i["L1_ffn_B"].T, np.zeros((P - 64, D), f32)])
    qkb = np.concatenate([np.repeat(i[f"L1_attn_b{n}"].reshape(2, 256), T, axis=0) for n in "qk"], axis=1)
    late_d = np.concatenate([ag, bt, rep(by_d(i["L1_attn_bv"])), rep(i["L1_attn_bo"]), rep(i["L1_ffn_b"]), qkb], axis=1)

    nc = _bacc.Bacc("TRN2", target_bir_lowering=False, num_devices=1)
    arrays, args = {}, []
    for name, a in (("x", x_d), ("cst", cst_d), ("fb", fb_d), ("rw", rw_d), ("ctx", ctx_d), ("kv", kv_d),
                    ("items", items_d), ("mask", mask_d), ("late", late_d), ("l1w", l1w_d)):
        a = np.ascontiguousarray(a)
        arrays[f"in_{name}"] = a
        args.append(nc.dram_tensor(f"in_{name}", a.shape, mybir.dt.from_np(a.dtype), kind="ExternalInput").ap())
    out = nc.dram_tensor("out_latents", (T, D), F32, kind="ExternalOutput").ap()
    build(nc, *args, out)
    r = _run(nc, [arrays], core_ids=[0])
    return r.results[0]["out_latents"].reshape(B, S, D)
```

```python
from contextlib import ExitStack

import numpy as np

import concourse.bass as bass
from concourse import mybir

F32 = mybir.dt.float32
F32R = mybir.dt.float32r
BF16 = mybir.dt.bfloat16
ALU = mybir.AluOpType
ACT = mybir.ActivationFunctionType
AX_X = mybir.AxisListType.X

P = 128
B, S, D = 2, 32, 512
T = B * S
CTX = 512
KC = D // P
NH, DK = 32, 16
HPC = P // DK
E, INTER, GROUPS = 16, 128, 4
H, KVH, HD = 32, 8, 128
GH = H // KVH
LN_EPS = 1e-5
BIG = 1e30
RANKS = (8, 16, 32, 64)
THRESH4 = 4 * float(np.float32(0.001))
MAGIC = 1.5 * 2.0 ** 23
QMID = 128.0

C_ID, C_HM, C_T16, C_T4 = 0, 128, 136, 392
C_QW, C_KW, C_RB, C_RBIAS, C_GB, C_Q = 408, 409, 410, 426, 442, 446
C_N = 450
FB_EB, FB_SB, FB_SB3, FB_N = 0, 2048, 2304, 2816
L_AG, L_BT, L_ROWS, L_QKB, L_N = 0, 272, 784, 2320, 2832

SLOT = 2048
SLOTS = 5
(I_WK, I_WQ, I_WV, I_WO, I_W1A, I_W2A, I_SH, I_W1B, I_W2B, I_W3, I_SW3, I_XQ, I_XO) = (
    0, 1, 2, 3, 4, 6, 8, 9, 11, 13, 17, 18, 26)
ITEMS = 34

FILL = [("start", 4), ("start2", 6), ("quant", 7), ("mix", 8), ("ln1", 4), ("heads", 0), ("soft1", 9), ("pv1", 3),
        ("ln2", 10), ("route", 0), ("ffn1", 2), ("ffn2", 0), ("ffn3", 3), ("ffn4", 2), ("ln3", 8),
        ("q0", 5), ("rest", 53), ("last", 4)]
WARM = [("first", 8), ("norm4", 11), ("turn4", 3), ("soft2", 6), ("move", 1), ("norm5", 11), ("turn5", 3), ("rank", 2)]
UNITS, TILES = 32, 8
KUNITS = 16
FILL_TO = {}
_n = 0
for _name, _k in FILL:
    FILL_TO[_name] = (_n, _n + _k)
    _n += _k
assert _n == 4 * UNITS

SEMS = """
x_in cst_in fb_in rw_in ctx_in0 ctx_in1 raw_in0 raw_in1 raw_in2 raw_in3 raw_in4 raw_in5 raw_in6 raw_in7
raw_in8 raw_in9 raw_in10 raw_in11 raw_in12 raw_in13 raw_in14 mask_in
late_in l1w_in0 l1w_in1 l1w_in2 l1w_in3 l1w_in4 out_done
slot0 slot1 slot2 slot3 slot4 item_used high_done low_done low_pool
warm_ready dve_step const_ready scal_ready
var_ready rstd_ready xn_ready xnT_psum xT_ready
xq_ready xqT_psum xqT_ready ctx_aff q2_ready mix_done x_new
kbd_ready qT_sb vbd_zero vbd_ready s_done s_shift e_done pt_ready o_done ot_ready
router_done lg_ready re_done gate_ready gateT_psum gateT_ready
silu_in silu_done h_ready hT_psum hT_ready
qsq_done qms_ready rq_ready qn_ready qnT_psum qTx_ready
kv_unit_done kraw_ready kms_ready kms_eps rk_ready kn_ready kT_psum kT_ready v_ready
sx_done pmax_ready pexp_done pn_ready ptx_psum ptx_ready ox_done otx_ready
lq_done lk_done lv_done lqk_sb vg_ready vg2_ready qd_psum kd_psum qd_ready kd_ready ls_done ls_shift le_done
at_ready lo_done lo_ready of_psum of_ready ly_done
xa_done ge_in ge_done xm_ready xmT_psum xmT_ready f_done fin_ready
""".split()


def build(nc, x_d, cst_d, fb_d, rw_d, ctx_d, kv_d, items_d, mask_d, late_d, l1w_d, out_d):
    with ExitStack() as ctx:
        def sb(name, shape, dt=F32):
            return ctx.enter_context(nc.sbuf_tensor(name, shape, dt))

        s = {name: ctx.enter_context(nc.semaphore(name)) for name in SEMS}

        ring = sb("ring", [P, SLOTS, SLOT])
        with nc.sbuf_tensor("cts", [P, 2, B, SLOT], F32R) as cts, nc.sbuf_tensor("wsp", [P, 2, 2, SLOT], F32R) as wsp:
            pass
        lastw = sb("lastw", [P, 8, SLOT])
        kT = sb("kT", [P, KVH, B, CTX])
        V = sb("V", [P, 2, TILES, 512])
        r1 = sb("r1", [P, FB_N])
        r2 = sb("r2", [P, 3072])
        x = sb("x", [T, D])
        xn = sb("xn", [T, D])
        xT = sb("xT", [P, KC, T])
        cst = sb("cst", [P, C_N])
        ksq = sb("ksq", [P, 512])
        kn = sb("kn", [P, 3, 512])
        nmask = kn[:, 2, :]
        sc = sb("sc", [P, 260])
        ps = ctx.enter_context(nc.psum_tensor("ps", [P, 8, 512], F32))

        ctxn = V[:, 0]
        q2 = ring[:, SLOTS - 1, :].bitcast(BF16).rearrange("p (g n) -> p g n", n=512)
        vraw = V[:, 1].rearrange("p t n -> p (t n)")
        kraw = kT[:, 4:8].rearrange("p g b n -> p (g b n)")
        hi_lo = {("c", b): (cts[:, 0, b, :], cts[:, 1, b, :]) for b in range(B)}
        hi_lo |= {("w", p): (wsp[:, p % 2, 0, :], wsp[:, p % 2, 1, :]) for p in range(4)}
        raw = {("c", b): vraw[:, SLOT * b:SLOT * b + SLOT] for b in range(B)}
        raw |= {("w", p): (kraw, vraw)[p // 2][:, SLOT * (p % 2):SLOT * (p % 2) + SLOT] for p in range(4)}
        PIECES = [(("c", 0), 0, 512)] + [(("w", 0), 512 * kc, 512) for kc in range(KC)]
        PIECES += [(("c", 0), 512 * c, 512) for c in range(1, 4)]
        PIECES += [(("c", 1), 512 * c, 512) for c in range(4)]
        PIECES += [(("w", p), 0, SLOT) for p in (1, 2, 3)]
        POOL_PIECES = (12,)
        SPLIT_AFTER = {0: (8, 9, 10, 11), 2: (12,), TILES: (13,), 2 * TILES: (14,)}
        l1w = [lastw[:, i, :].rearrange("p (k n) -> p k n", k=KC) for i in range(5)]
        otx = lastw[:, 5, :].rearrange("p (h t) -> p h t", t=T)
        late = lastw[:, 6:8, :].rearrange("p a n -> p (a n)")[:, 0:L_N]

        prob, probT = r1[:, 0:512], r1[:, 512:1024]
        qTs = r1[:, 1024:1280].rearrange("p (c t) -> p c t", c=KC)
        ots = r1[:, 1280:1536].rearrange("p (c t) -> p c t", c=KC)
        kbd = r2[:, 0:2048].rearrange("p (b c h k) -> p b c h k", b=B, c=KC, h=HPC)
        vbd = r2[:, 2048:3072].rearrange("p (g e) -> p g e", e=64)
        xq, xqT = r1[0:T, 0:256].bitcast(BF16), r1[:, 256:384].bitcast(BF16).rearrange("p (k t) -> p k t", k=KC)
        onesb = r1[:, 384:400].bitcast(BF16)
        mixt = r1[0:T, 512:1024]
        fb = r1
        fa, fs, fh = r2[:, 0:512], r2[:, 512:1024], r2[:, 1024:1536]
        fhT = [r2[:, 1536 + 512 * i:2048 + 512 * i].rearrange("p (j h t) -> p j h t", j=4, h=2) for i in range(2)]
        fhTs = r2[:, 2560:2688].rearrange("p (h t) -> p h t", h=2)
        fss = r2[:, 2688:2816]
        fhs = r2[:, 2816:2944]
        gateT = r2[0:E, 2944:3008]
        qTx = r1[:, 0:2048].rearrange("p (g b n) -> p g b n", b=B, n=P)
        qsq, qn = r2[:, 0:512], [r2[:, 512:1024], r2[:, 1024:1536]]
        pb = [r2[:, 512 * i:512 * i + 512] for i in range(3)]
        ptb = [r2[:, 1536 + 512 * i:2048 + 512 * i] for i in range(2)]
        qd = r1[0:DK, 0:2048].rearrange("p (n t) -> p n t", t=T)
        kd = r2[0:DK, 0:2048].rearrange("p (n t) -> p n t", t=T)
        lq, lk = r1[:, 2048:2304], r1[:, 2304:2560]
        heads_out = r1[:, 0:256]
        lv, vg = kn[0:T, 0, :], kn[0:T, 1, :].rearrange("p (d t) -> p d t", t=32)
        vg2 = r1[:, 2560:2816].rearrange("p (d t) -> p d t", t=16)
        lp, at = r2[:, 2048:2560], r2[:, 2560:3072]
        of = lastw[:, 5, 0:256].rearrange("p (i t) -> p i t", i=4)
        xm, xmT = lastw[0:T, 5, 256:320], lastw[0:T, 5, 320:384]

        SBANKS = (6, 0, 1)
        QBANKS, KBANKS = (3, 4, 5, 6), (7, 0, 1, 2)

        ident = cst[:, C_ID:C_ID + P]
        hmask = cst[:, C_HM:C_HM + HPC]
        st6, mv = sc[0:T, 0:6], sc[0:T, 6:8]
        ve, rstd = sc[0:T, 8:9], sc[0:T, 9:10]
        nhalf = sc[:, 10:14]
        r1s, r2s, off1, off2, sss, rsum, row = (sc[:, 14:15], sc[:, 15:16], sc[:, 16:17], sc[:, 17:18], sc[:, 18:19],
                                                sc[0:T, 19:20], sc[0:T, 20:21])
        rstd2 = sc[:, 9:10]
        nw = sc[:, 22:23]
        mx, sm, rc = sc[:, 24:40], sc[:, 40:56], sc[:, 56:72]
        kms = [sc[:, 80 + 4 * i:84 + 4 * i] for i in range(2)]
        rk = [sc[:, 88 + 4 * i:92 + 4 * i] for i in range(2)]
        lg, re, score, gate = sc[:, 96:112], sc[:, 112:128], sc[:, 128:144], sc[:, 144:160]
        gsel = sc[:, 160:168]
        gm, g4, pen4, rz = sc[:, 168:172], sc[:, 172:176], sc[:, 176:180], sc[:, 180:184]
        ms = sc[:, 184:200]
        pmx, psm, prc = sc[:, 200:216], sc[:, 216:232], sc[:, 232:248]
        ge, gsc = sc[0:T, 248:252], sc[0:T, 252:256]
        rw_t = sb("rw_t", [P, 64])
        pairs = r2[:, 0:256].rearrange("p (i j) -> p i j", j=16)
        pairs2 = r2[:, 256:512].rearrange("p (i j) -> p i j", j=16)

        def bank(n):
            return ps[:, n, :]

        def halves(n, lo=0, w=256):
            return [ps[T * h:T * h + T, n, lo:lo + w] for h in range(2)]

        def slot(i):
            return ring[:, i % SLOTS, :]

        def turned(n):
            return n // 4 - 3 if n % 4 == 1 and 0 <= n // 4 - 3 < KUNITS else None

        def ended(n0, n1):
            return [u for u in range(UNITS) if n0 <= 4 * u + 3 < n1]

        def kms_q(m):
            return sc[:, 112 + 4 * m:116 + 4 * m]

        def copy_qk(copy, eng, first):
            for dst, banks, psum, ready in ((qd, QBANKS, "qd_psum", "qd_ready"), (kd, KBANKS, "kd_psum", "kd_ready")):
                for j in range(first, 4, 2):
                    eng.wait_ge(s[psum], j + 1)
                    copy(dst[:, 8 * j:8 * j + 8, :], ps[0:DK, banks[j], :].rearrange("p (n t) -> p n t", t=T))\
                        .then_inc(s[ready], 1)

        def wait_low(eng, i):
            pool = i in POOL_PIECES
            eng.wait_ge(s["low_pool" if pool else "low_done"], sum((k in POOL_PIECES) == pool for k in range(i + 1)))

        def low_half(eng, i, done):
            key, lo, n = PIECES[i]
            eng.wait_ge(s["high_done"], i + 1)
            hi, low = hi_lo[key]
            eng.tensor_tensor(low[:, lo:lo + n], raw[key][:, lo:lo + n], hi[:, lo:lo + n].bitcast(F32),
                              ALU.subtract).then_inc(s[done], 1)

        block = ctx.enter_context(nc.Block())

        @block.sync
        def _(sp):
            def load_item(i):
                if i >= SLOTS:
                    sp.wait_ge(s["item_used"], i - SLOTS + 1)
                if i == SLOTS - 1:
                    sp.wait_ge(s["mix_done"], 1)
                sp.dma_start(slot(i), items_d[i]).then_inc(s[f"slot{i % SLOTS}"], 16)

            def load_raw(i):
                key, lo, n = PIECES[i]
                if key == ("w", 2):
                    wait_low(sp, 10)
                    wait_low(sp, 11)
                sp.dma_start(raw[key][:, lo:lo + n], kv_d[key[1] + 2 * (key[0] == "w")][:, lo:lo + n])\
                  .then_inc(s[f"raw_in{i}"], 16)

            for i in range(8):
                load_raw(i)
            sp.dma_start(x[:, :], x_d).then_inc(s["x_in"], 16)
            sp.dma_start(cst[:, :], cst_d).then_inc(s["cst_in"], 16)
            for b in range(B):
                sp.dma_start(ctxn[:, 4 * b:4 * b + 4, :], ctx_d[:, 4 * b:4 * b + 4, :]).then_inc(s[f"ctx_in{b}"], 16)
                if b == 0:
                    for i in range(8, 12):
                        load_raw(i)
            load_raw(12)
            load_item(0)
            for i in range(1, 4):
                load_item(i)
            sp.dma_start(rw_t[:, :], rw_d).then_inc(s["rw_in"], 16)
            for i in range(4, 9):
                load_item(i)
                if i == 6:
                    load_raw(13)
                if i == 7:
                    sp.wait_ge(s["item_used"], I_WO + 1)
                    sp.dma_start(fb[:, :], fb_d).then_inc(s["fb_in"], 16)
            load_raw(14)
            for i in range(9, ITEMS - 8 + SLOTS):
                load_item(i)
            sp.wait_ge(s["kT_psum"], KUNITS)
            for g in range(4):
                sp.dma_start(nmask[S * g:S * g + S, :], mask_d).then_inc(s["mask_in"], 16)
            sp.wait_ge(s["kv_unit_done"], UNITS)
            for i in range(5):
                sp.dma_start(lastw[:, i, :], l1w_d[i]).then_inc(s[f"l1w_in{i}"], 16)
            sp.dma_start(late, late_d).then_inc(s["late_in"], 16)
            for i in range(ITEMS - 8 + SLOTS, ITEMS):
                load_item(i)
            for h in range(2):
                sp.wait_ge(s["fin_ready"], h + 1)
                sp.dma_start(out_d[:, 256 * h:256 * h + 256], x[:, 256 * h:256 * h + 256]).then_inc(s["out_done"], 16)
            sp.wait_ge(s["out_done"], 32)

        @block.tensor
        def _(pe):
            def fill(name):
                n0, n1 = FILL_TO[name]
                for n in range(n0, n1):
                    u, kc = n // 4, n % 4
                    part, tile = u // TILES, u % TILES
                    b, c = tile // 4, tile % 4
                    if kc == 0:
                        if 2 <= u < KUNITS + 2:
                            pe.wait_ge(s["kraw_ready"], u - 1)
                        if u >= KUNITS + 2:
                            pe.wait_ge(s["v_ready"], u - KUNITS - 1)
                    if u == 0:
                        wait_low(pe, 1 + kc)
                    if part == 0 and kc == 0 and tile:
                        wait_low(pe, 4 + tile)
                    if kc == 0 and tile == 0 and part:
                        wait_low(pe, 11 + part)
                    hi, lo = (v[:, 512 * kc:512 * kc + 512] for v in hi_lo["w", part])
                    chi, clo = (v[:, 512 * c + P * kc:512 * c + P * kc + P] for v in hi_lo["c", b])
                    for q, (a, w) in enumerate(((chi, hi), (chi, lo), (clo, hi))):
                        mm = pe.matmul(bank(u % 2), a, w, start=(kc == 0 and q == 0), stop=(kc == KC - 1 and q == 2))
                    if kc == KC - 1:
                        mm.then_inc(s["kv_unit_done"], 1)
                    ki = turned(n)
                    if ki is not None:
                        pe.wait_ge(s["kn_ready"], ki + 1)
                        if ki >= 1:
                            pe.wait_ge(s["kT_ready"], ki)
                        for j in range(4):
                            mm = pe.transpose(ps[:, 2, P * j:P * j + P], kn[:, ki % 3, P * j:P * j + P], ident)
                        mm.then_inc(s["kT_psum"], 1)

            def warm(name, n, src=None):
                src = cst[:, 0:256].bitcast(BF16) if src is None else src
                for _ in range(dict(WARM)[name]):
                    pe.matmul(bank(n), src[:, 0:P], src, start=True, stop=True)

            def item(i):
                pe.wait_ge(s[f"slot{i % SLOTS}"], 16 * (i // SLOTS + 1))

            def turn_xn(n):
                pe.wait_ge(s["xn_ready"], n)
                for kc in range(KC):
                    mm = pe.transpose(ps[:, 5, T * kc:T * kc + T], xn[:, P * kc:P * kc + P], ident[0:T, 0:T])
                mm.then_inc(s["xnT_psum"], 1)

            def project(n, lhs, w, start=True, stop=True):
                for kc in range(KC):
                    for h in range(2):
                        mm = pe.matmul(halves(n)[h], lhs[:, kc, :], w[:, kc, 256 * h:256 * h + 256],
                                       start=(start and kc == 0), stop=(stop and kc == KC - 1), skip_group_check=True)
                return mm

            pe.wait_ge(s["warm_ready"], 1)
            warm("first", 7, kn[:, 0, 0:256].bitcast(BF16))
            fill("start")
            fill("start2")
            pe.wait_ge(s["xq_ready"], 1)
            pe.wait_ge(s["const_ready"], 3)
            identb = r1[0:T, 400:432].bitcast(BF16)
            xqTp = ps[:, 5, 0:128].bitcast(BF16).rearrange("p (k t) -> p k t", k=KC)
            for kc in range(KC):
                mm = pe.transpose(xqTp[:, kc, :], xq[:, P * kc:P * kc + P], identb)
            mm.then_inc(s["xqT_psum"], 1)
            fill("quant")
            pe.wait_ge(s["xqT_ready"], 1)
            pe.wait_ge(s["q2_ready"], B)
            for kc in range(KC):
                for b in range(B):
                    for n, row0, lhs in ((3, S * b, xqT[:, kc, S * b:S * b + S]), (4, T + S * b, onesb)):
                        mm = pe.matmul(ps[row0:row0 + S, n, :], lhs, q2[:, 4 * b + kc, :],
                                       start=(kc == 0), stop=(kc == KC - 1))
            mm.then_inc(s["mix_done"], 1)
            fill("mix")

            turn_xn(1)
            fill("ln1")
            pe.wait_ge(s["xT_ready"], 1)
            for i, n in ((I_WK, 3), (I_WQ, 4)):
                item(i)
                w = slot(i).rearrange("p (k n) -> p k n", k=KC)
                for c in range(KC):
                    for kc in range(KC):
                        mm = pe.matmul(ps[:, n, T * c:T * c + T], w[:, kc, P * c:P * c + P], xT[:, kc, :],
                                       start=(kc == 0), stop=(kc == KC - 1))
                mm.then_inc(s["item_used"], 1)
            item(I_WV)
            w = slot(I_WV).rearrange("p (k n) -> p k n", k=KC)
            for b in range(B):
                for kc in range(KC):
                    for c in range(KC):
                        mm = pe.matmul(ps[S * c:S * c + S, 6, P * b:P * b + P], xT[:, kc, S * b:S * b + S],
                                       w[:, kc, P * c:P * c + P], start=(kc == 0), stop=(kc == KC - 1),
                                       skip_group_check=True)
            mm.then_inc(s["item_used"], 1)
            fill("heads")
            pe.wait_ge(s["qT_sb"], 1)
            pe.wait_ge(s["kbd_ready"], 2)
            for b in range(B):
                for c in range(KC):
                    mm = pe.matmul(ps[S * c:S * c + S, 7, 256 * b:256 * b + 256], qTs[:, c, S * b:S * b + S],
                                   kbd[:, b, c, :, :], start=True, stop=True)
            mm.then_inc(s["s_done"], 1)
            fill("soft1")
            pe.wait_ge(s["pt_ready"], 1)
            pe.wait_ge(s["vbd_ready"], 4)
            for b in range(B):
                for j in range(HPC):
                    mm = pe.matmul(ps[T * (j // 4):T * (j // 4) + T, 4, T * (j % 4) + S * b:T * (j % 4) + S * b + S],
                                   vbd[:, HPC * b + j, :], probT[:, 256 * b + S * j:256 * b + S * j + S],
                                   start=True, stop=True)
            mm.then_inc(s["o_done"], 1)
            fill("pv1")
            item(I_WO)
            pe.wait_ge(s["ot_ready"], 1)
            project(6, ots, slot(I_WO).rearrange("p (k n) -> p k n", k=KC)).then_inc(s["item_used"], 1)

            fill("ln2")
            turn_xn(2)
            pe.wait_ge(s["xT_ready"], 2)
            pe.wait_ge(s["rw_in"], 16)
            for kc in range(KC):
                for h in range(2):
                    mm = pe.matmul(ps[T * h:T * h + T, 7, 0:E], xT[:, kc, :], rw_t[:, E * kc:E * kc + E],
                                   start=(kc == 0), stop=(kc == KC - 1))
            mm.then_inc(s["router_done"], 1)
            fill("route")

            def expert_in(i, n):
                for a in range(2):
                    item(i + a)
                    w = slot(i + a).rearrange("p (k h n) -> p k h n", k=2, h=2)
                    for k in range(2):
                        for h in range(2):
                            mm = pe.matmul(ps[T * h:T * h + T, n, :], xT[:, 2 * a + k, :], w[:, k, h, :],
                                           start=(a == 0 and k == 0), stop=(a == 1 and k == 1))
                    mm.then_inc(s["item_used"], 1)

            expert_in(I_W1A, 3)
            fill("ffn1")
            expert_in(I_W2A, 4)
            item(I_SH)
            pe.wait_ge(s["lg_ready"], 1)
            w = slot(I_SH).rearrange("p (k w h n) -> p k w h n", k=KC, w=2, h=2)
            for wn in range(2):
                for kc in range(KC):
                    for h in range(2):
                        mm = pe.matmul(ps[T * h:T * h + T, 7, P * wn:P * wn + P], xT[:, kc, :], w[:, kc, wn, h, :],
                                       start=(kc == 0), stop=(kc == KC - 1), skip_group_check=True)
            mm.then_inc(s["item_used"], 1)
            pe.wait_ge(s["silu_in"], 1)
            expert_in(I_W1B, 3)
            fill("ffn2")

            def turn_h(src, n, w):
                pe.wait_ge(s["h_ready"], n)
                if n == 1:
                    pe.wait_ge(s["xT_ready"], 2)
                else:
                    pe.wait_ge(s["hT_ready"], n - 1)
                for j in range(w):
                    mm = pe.transpose(ps[:, 5, P * j:P * j + P], src[:, P * j:P * j + P], ident)
                mm.then_inc(s["hT_psum"], 1)

            turn_h(fh, 1, 4)
            expert_in(I_W2B, 4)
            turn_h(fhs, 2, 1)
            fill("ffn3")
            for r in range(2):
                if r == 1:
                    turn_h(fh, 3, 4)
                    fill("ffn4")
                    pe.wait_ge(s["hT_ready"], 3)
                else:
                    pe.wait_ge(s["hT_ready"], 1)
                for a in range(2):
                    i = I_W3 + 2 * r + a
                    item(i)
                    w = slot(i).rearrange("p (j h n) -> p j h n", j=2, h=2)
                    for j in range(2):
                        for e in range(2):
                            for h in range(2):
                                mm = pe.matmul(halves(6)[h], fhT[r][:, 2 * a + j, e, :],
                                               w[:, j, e, 256 * h:256 * h + 256],
                                               start=(r + a + j + e == 0), stop=False, skip_group_check=True)
                    mm.then_inc(s["item_used"], 1)
            item(I_SW3)
            pe.wait_ge(s["gate_ready"], 1)
            pe.transpose(ps[0:E, 7, 256:256 + T], gate[0:T, :], ident[0:T, 0:T]).then_inc(s["gateT_psum"], 1)
            w3 = slot(I_SW3)
            for e in range(2):
                for h in range(2):
                    pe.matmul(halves(6)[h], fhTs[:, e, :], w3[:, 512 * e + 256 * h:512 * e + 256 * h + 256],
                              start=False, stop=False, skip_group_check=True)
            pe.wait_ge(s["gateT_ready"], 1)
            for h in range(2):
                mm = pe.matmul(halves(6)[h], gateT, w3[0:E, 1024 + 256 * h:1280 + 256 * h],
                               start=False, stop=True, skip_group_check=True)
            mm.then_inc(s["item_used"], 1)

            fill("ln3")
            turn_xn(3)
            pe.wait_ge(s["xT_ready"], 3)

            def turn_q(m):
                pe.wait_ge(s["qn_ready"], m + 1)
                if m >= 1:
                    pe.wait_ge(s["qTx_ready"], 2 * m)
                for j in range(4):
                    mm = pe.transpose(ps[:, 5, P * j:P * j + P], qn[m % 2][:, P * j:P * j + P], ident)
                mm.then_inc(s["qnT_psum"], 1)

            for m in range(4):
                for a in range(2):
                    i = I_XQ + 2 * m + a
                    item(i)
                    w = slot(i).rearrange("p (k h n) -> p k h n", k=2, h=2)
                    for k in range(2):
                        for h in range(2):
                            mm = pe.matmul(ps[T * h:T * h + T, (3, 4, 6, 7)[m], :], xT[:, 2 * a + k, :], w[:, k, h, :],
                                           start=(a == 0 and k == 0), stop=(a == 1 and k == 1))
                    mm.then_inc(s["item_used"], 1)
                if m >= 1:
                    turn_q(m - 1)
            fill("q0")
            turn_q(3)
            fill("rest")

            NU = KVH * B
            pe.wait_ge(s["kT_ready"], KUNITS)
            pe.wait_ge(s["qTx_ready"], 8)

            def out_heads(g):
                i = I_XO + g
                item(i)
                pe.wait_ge(s["otx_ready"], 2 * g + 2)
                w = slot(i).rearrange("p (j n) -> p j n", j=GH)
                for j in range(GH):
                    for h in range(2):
                        mm = pe.matmul(halves(7)[h], otx[:, GH * g + j, :], w[:, j, 256 * h:256 * h + 256],
                                       start=(g == 0 and j == 0), stop=(g == KVH - 1 and j == GH - 1),
                                       skip_group_check=True)
                mm.then_inc(s["item_used"], 1)

            for k in range(NU + 3):
                if k < NU:
                    g, b = k // B, k % B
                    if k >= 3:
                        pe.wait_ge(s["pmax_ready"], k - 2)
                    elif k:
                        pe.wait_ge(s["v_ready"], KUNITS - 2 + k)
                    pe.matmul(bank(SBANKS[k % 3]), qTx[:, g, b, :], kT[:, g, b, :],
                              start=True, stop=True).then_inc(s["sx_done"], 1)
                    if k == 0:
                        fill("last")
                u = k - 2
                if 0 <= u < NU:
                    pe.wait_ge(s["pn_ready"], u + 1)
                    if u >= 2:
                        pe.wait_ge(s["ptx_ready"], u - 1)
                    for j in range(4):
                        mm = pe.transpose(ps[:, (2, 5)[u % 2], P * j:P * j + P], pb[u % 3][:, P * j:P * j + P], ident)
                    mm.then_inc(s["ptx_psum"], 1)
                u = k - 3
                if 0 <= u < NU:
                    g, b = u // B, u % B
                    pe.wait_ge(s["ptx_ready"], u + 1)
                    if u >= 2:
                        pe.wait_ge(s["otx_ready"], u - 1)
                    for j in range(4):
                        mm = pe.matmul(ps[:, 3 + u % 2, 0:P], V[:, g // 4, 4 * b + j, HD * (g % 4):HD * (g % 4) + HD],
                                       ptb[u % 2][:, P * j:P * j + P], start=(j == 0), stop=(j == 3))
                    mm.then_inc(s["ox_done"], 1)
                if u >= 3 and u % 2 == 1:
                    out_heads(u // 2 - 1)
            out_heads(KVH - 1)

            warm("norm4", 6)
            turn_xn(4)
            warm("turn4", 6)
            pe.wait_ge(s["xT_ready"], 4)
            for i, done in ((0, "lq_done"), (1, "lk_done")):
                pe.wait_ge(s[f"l1w_in{i}"], 16)
                project(i, xT, l1w[i]).then_inc(s[done], 1)
            for w, (src, banks, done) in enumerate(((lq, QBANKS, "qd_psum"), (lk, KBANKS, "kd_psum"))):
                pe.wait_ge(s["lqk_sb"], w + 1)
                for q in range(4):
                    for j in range(4):
                        hh = 4 * q + j
                        mm = pe.transpose(ps[0:DK, banks[q], P * j:P * j + P], src[:, DK * hh:DK * hh + DK], ident)
                    mm.then_inc(s[done], 1)
            pe.wait_ge(s["l1w_in2"], 16)
            pe.wait_ge(s["qd_ready"], 4)
            project(3, xT, l1w[2]).then_inc(s["lv_done"], 1)
            pe.wait_ge(s["kd_ready"], 4)
            for f in range(2):
                for tt in range(8):
                    for c in range(4):
                        t = 16 * c + 8 * f + tt
                        mm = pe.matmul(ps[S * c:S * c + S, 4 + f, NH * tt:NH * tt + NH], qd[:, :, t], kd[:, :, t],
                                       start=True, stop=True)
                mm.then_inc(s["ls_done"], 1)
            warm("soft2", 2)
            pe.wait_ge(s["vg2_ready"], 4)
            for f in range(2):
                pe.wait_ge(s["at_ready"], f + 1)
                for tt in range(8):
                    for c in range(4):
                        t = 8 * f + tt
                        mm = pe.matmul(ps[S * c:S * c + S, 6 + f, DK * tt:DK * tt + DK],
                                       at[NH * c:NH * c + NH, NH * t:NH * t + NH], vg2[NH * c:NH * c + NH, :, t],
                                       start=True, stop=True)
                mm.then_inc(s["lo_done"], 1)
            for f in range(2):
                pe.wait_ge(s["lo_ready"], f + 1)
                for j in range(4):
                    for c in range(4):
                        src = heads_out[S * c:S * c + S, P * f:P * f + P]
                        src = src.rearrange("p (t i j) -> p j i t", i=4, j=4)[:, j]
                        dst = ps[S * j:S * j + S, c, 0:64].rearrange("p (i t) -> p i t", i=4)
                        mm = pe.matmul(dst[:, :, 8 * f:8 * f + 8], ident[S * c:S * c + S, S * c:S * c + S], src,
                                       start=True, stop=True)
            mm.then_inc(s["of_psum"], 1)
            pe.wait_ge(s["l1w_in3"], 16)
            warm("move", 5)
            pe.wait_ge(s["of_ready"], 1)
            project(4, of, l1w[3]).then_inc(s["ly_done"], 1)

            warm("norm5", 0)
            turn_xn(5)
            warm("turn5", 0)
            pe.wait_ge(s["xT_ready"], 5)
            for kc in range(KC):
                mm = pe.matmul(ps[0:T, 4, 0:68], xT[:, kc, :], late[:, L_AG + 68 * kc:L_AG + 68 * kc + 68],
                               start=(kc == 0), stop=(kc == KC - 1))
            mm.then_inc(s["xa_done"], 1)
            pe.wait_ge(s["l1w_in4"], 16)
            project(3, xT, l1w[4], stop=False)
            warm("rank", 0)
            pe.wait_ge(s["xm_ready"], 1)
            pe.transpose(ps[0:T, 2, 0:T], xm, ident[0:T, 0:T]).then_inc(s["xmT_psum"], 1)
            pe.wait_ge(s["xmT_ready"], 1)
            for h in range(2):
                pe.matmul(halves(3)[h], xmT, late[0:T, L_BT + 256 * h:L_BT + 256 * h + 256],
                          start=False, stop=True, skip_group_check=True).then_inc(s["f_done"], 1)

        @block.vector
        def _(dve):
            steps = [0]

            def link(ins):
                steps[0] += 1
                ins.then_inc(s["dve_step"], 1)
                dve.wait_ge(s["dve_step"], steps[0])

            def evac(name):
                for u in ended(*FILL_TO[name]):
                    if 1 <= u <= KUNITS:
                        v = u - 1
                        dve.wait_ge(s["rk_ready"], v + 1)
                        rows = kn[:, v % 3, :].rearrange("p (g d) -> p g d", d=HD)
                        dve.tensor_tensor(rows, rows, rk[v % 2].unsqueeze(2).to_broadcast([P, 4, HD]), ALU.mult)\
                           .then_inc(s["kn_ready"], 1)
                    for i in SPLIT_AFTER.get(u, ()):
                        split(i)

            def split(i):
                if i not in POOL_PIECES:
                    low_half(dve, i, "low_done")

            def normalise(n):
                link(dve.bn_stats(st6, x[:, :]))
                link(dve.bn_aggr(mv, st6))
                dve.tensor_scalar(ve, mv[:, 1:2], LN_EPS, None, ALU.add).then_inc(s["var_ready"], 1)
                dve.wait_ge(s["rstd_ready"], n + 1)
                ins = dve.tensor_scalar(xn[:, :], x[:, :], mv[:, 0:1], rstd, ALU.subtract, ALU.mult)
                if n:
                    ins.then_inc(s["xn_ready"], 1)
                else:
                    link(ins)

            def centre(n):
                link(dve.bn_stats(st6, x[:, :]))
                link(dve.bn_aggr(mv, st6))
                dve.tensor_scalar(ve, mv[:, 1:2], LN_EPS, None, ALU.add).then_inc(s["var_ready"], 1)
                dve.tensor_scalar(xn[:, :], x[:, :], mv[:, 0:1], None, ALU.subtract).then_inc(s["xn_ready"], 1)
                dve.wait_ge(s["rstd_ready"], n + 1)
                link(dve.tensor_copy(rstd2[T:P, :], rstd))

            def add_halves(n):
                a = dve.tensor_tensor(x[:, 0:256], halves(n)[0], x[:, 0:256], ALU.add)
                link(a)
                link(dve.tensor_tensor(x[:, 256:512], halves(n)[1], x[:, 256:512], ALU.add))

            dve.memset(kn[:, 0, 0:256], 1.0).then_inc(s["warm_ready"], 1)
            dve.memset(nhalf, -0.5).then_inc(s["const_ready"], 1)
            dve.memset(onesb, 1.0).then_inc(s["const_ready"], 1)
            for i in range(8):
                split(i)
            dve.wait_ge(s["cst_in"], 16)
            q = cst[:, C_Q:C_Q + 4]
            dve.tensor_copy(r1[0:T, 400:432].bitcast(BF16), ident[0:T, 0:T]).then_inc(s["const_ready"], 1)
            dve.reciprocal(r1s, q[:, 0:1])
            dve.reciprocal(r2s, q[:, 2:3]).then_inc(s["scal_ready"], 1)
            dve.tensor_scalar(off1, q[:, 1:2], -1.0, QMID, ALU.mult, ALU.add)
            dve.tensor_scalar(off2, q[:, 3:4], -1.0, QMID, ALU.mult, ALU.add)
            dve.tensor_tensor(sss, q[:, 0:1], q[:, 2:3], ALU.mult)
            link(dve.tensor_tensor(nw, cst[:, C_QW:C_QW + 1], cst[:, C_KW:C_KW + 1], ALU.mult))
            link(dve.tensor_scalar(nw, nw, -1.0 / float(np.sqrt(HD)), None, ALU.mult))
            dve.wait_ge(s["x_in"], 16)
            normalise(0)
            link(dve.tensor_scalar(xn[:, :], xn[:, :], r1s[0:T, :], q[0:T, 1:2], ALU.mult, ALU.add))
            link(dve.tensor_scalar(xn[:, :], xn[:, :], 0.0, 255.0, ALU.max, ALU.min))
            dve.tensor_scalar(xq, xn[:, :], MAGIC, MAGIC + QMID, ALU.add, ALU.subtract).then_inc(s["xq_ready"], 1)
            evac("start")
            dve.wait_ge(s["xq_ready"], 1)
            link(dve.tensor_reduce(rsum, xq, AX_X, ALU.add))
            link(dve.scalar_tensor_tensor(row, off1[0:T, :], float(CTX), rsum, ALU.mult, ALU.add))
            link(dve.tensor_scalar(row, row, off2[0:T, :], None, ALU.mult))
            for b in range(B):
                dve.wait_ge(s["ctx_aff"], b + 1)
                link(dve.tensor_scalar(ctxn[:, 4 * b:4 * b + 4, :], ctxn[:, 4 * b:4 * b + 4, :], 0.0, 255.0,
                                       ALU.max, ALU.min))
                dve.tensor_scalar(q2[:, 4 * b:4 * b + 4, :], ctxn[:, 4 * b:4 * b + 4, :], MAGIC, MAGIC + QMID,
                                  ALU.add, ALU.subtract).then_inc(s["q2_ready"], 1)
                if b == 0:
                    evac("start2")
            evac("quant")
            dve.wait_ge(s["mix_done"], 1)
            link(dve.tensor_scalar(mixt, ps[T:P, 4, :], off1[0:T, :], row, ALU.mult, ALU.add))
            link(dve.tensor_tensor(mixt, ps[0:T, 3, :], mixt, ALU.add))
            link(dve.scalar_tensor_tensor(x[:, :], mixt, sss[0:T, :], x[:, :], ALU.mult, ALU.add))

            normalise(1)
            evac("mix")
            evac("ln1")
            dve.wait_ge(s["item_used"], I_WK + 1)
            for b in range(B):
                kTp = ps[:, 3, 0:256].rearrange("p (c b k) -> p c b k", c=KC, b=B)[:, :, b, :]
                for c in range(KC):
                    ins = dve.tensor_tensor(kbd[:, b, c, :, :], kTp[:, c, :].unsqueeze(1).to_broadcast([P, HPC, S]),
                                            hmask.unsqueeze(2).to_broadcast([P, HPC, S]), ALU.mult)
                ins.then_inc(s["kbd_ready"], 1)
            evac("heads")
            s3 = bank(7).rearrange("p (g k) -> p g k", k=S)
            e3 = bank(3).rearrange("p (g k) -> p g k", k=S)
            wide = [P, 16, S]
            dve.wait_ge(s["s_done"], 1)
            link(dve.tensor_reduce(mx, s3, AX_X, ALU.max))
            dve.tensor_tensor(s3, s3, mx.unsqueeze(2).to_broadcast(wide), ALU.subtract).then_inc(s["s_shift"], 1)
            dve.wait_ge(s["e_done"], 1)
            link(dve.tensor_reduce(sm, e3, AX_X, ALU.add))
            link(dve.reciprocal(rc, sm))
            link(dve.tensor_tensor(prob.rearrange("p (g k) -> p g k", k=S), e3, rc.unsqueeze(2).to_broadcast(wide),
                                   ALU.mult))
            dve.transpose(probT, prob).then_inc(s["pt_ready"], 1)
            evac("soft1")
            evac("pv1")
            dve.wait_ge(s["item_used"], I_WO + 1)
            add_halves(6)

            normalise(2)
            evac("ln2")
            dve.wait_ge(s["router_done"], 1)
            dve.tensor_tensor(lg, ps[:, 7, 0:E], cst[:, C_RB:C_RB + E], ALU.add).then_inc(s["lg_ready"], 1)
            dve.wait_ge(s["lg_ready"], 1)
            dve.tensor_reduce(rz[:, 0:1], lg, AX_X, ALU.max, negate=True).then_inc(s["lg_ready"], 1)
            dve.wait_ge(s["re_done"], 1)
            link(dve.reciprocal(rz[:, 2:3], rz[:, 1:2]))
            link(dve.scalar_tensor_tensor(score, re, rz[:, 2:3], cst[:, C_RBIAS:C_RBIAS + E], ALU.mult, ALU.add))
            link(dve.tensor_reduce(gm, score.rearrange("p (g e) -> p g e", g=GROUPS), AX_X, ALU.max))

            def top2(vals, n, tri, keep):
                a, b2 = pairs[:, 0:n, 0:n], pairs2[:, 0:n, 0:n]
                other, own = vals.unsqueeze(1).to_broadcast([P, n, n]), vals.unsqueeze(2).to_broadcast([P, n, n])
                dve.tensor_tensor(a, other, own, ALU.is_gt)
                link(dve.tensor_tensor(b2, other, own, ALU.is_equal))
                link(dve.tensor_tensor(b2, b2, tri, ALU.mult))
                link(dve.tensor_tensor(a, a, b2, ALU.add))
                link(dve.tensor_reduce(keep, a, AX_X, ALU.add))
                link(dve.tensor_scalar(keep, keep, 1.5, None, ALU.is_lt))

            top2(gm, GROUPS, cst[:, C_T4:C_T4 + 16].rearrange("p (i j) -> p i j", j=4), g4)
            link(dve.tensor_scalar(pen4, g4, 1.0, BIG, ALU.subtract, ALU.mult))
            m4, s4 = (t.rearrange("p (g e) -> p g e", g=GROUPS) for t in (ms, score))
            four = [P, GROUPS, E // GROUPS]
            link(dve.tensor_tensor(m4, s4, g4.unsqueeze(2).to_broadcast(four), ALU.mult))
            link(dve.tensor_tensor(m4, m4, pen4.unsqueeze(2).to_broadcast(four), ALU.add))
            top2(ms, E, cst[:, C_T16:C_T16 + 256].rearrange("p (i j) -> p i j", j=16), gate)
            dve.tensor_tensor(gate, gate, score, ALU.mult).then_inc(s["gate_ready"], 1)
            dve.wait_ge(s["gate_ready"], 1)
            g3 = gate.rearrange("p (r h j) -> p r h j", r=2, h=2)
            gs3 = gsel.rearrange("p (r j) -> p r j", r=2)
            dve.tensor_copy(gs3[0:T], g3[0:T, :, 0, :])
            link(dve.tensor_copy(gs3[T:P], g3[T:P, :, 1, :]))

            def inner(r):
                eb = fb[:, 1024 * r:1024 * r + 1024]
                dve.wait_ge(s["item_used"], (I_W1A, I_W1B)[r] + 2)
                dve.tensor_tensor(fa, bank(3), eb[:, 0:512], ALU.add).then_inc(s["silu_in"], 1)

            def gated(r):
                eb = fb[:, 1024 * r:1024 * r + 1024]
                dve.wait_ge(s["item_used"], (I_W2A, I_W2B)[r] + 2)
                link(dve.tensor_tensor(bank(4), bank(4), eb[:, 512:1024], ALU.add))
                dve.wait_ge(s["silu_done"], (1, 3)[r])
                if r == 1:
                    dve.wait_ge(s["hT_psum"], 1)
                for j in range(4):
                    ins = dve.scalar_tensor_tensor(fh[:, P * j:P * j + P], fs[:, P * j:P * j + P],
                                                   gsel[:, 4 * r + j:4 * r + j + 1], bank(4)[:, P * j:P * j + P],
                                                   ALU.mult, ALU.mult)
                ins.then_inc(s["h_ready"], 1)

            dve.wait_ge(s["fb_in"], 16)
            evac("route")
            inner(0)
            evac("ffn1")
            gated(0)
            dve.wait_ge(s["item_used"], I_SH + 1)
            dve.tensor_tensor(fss, ps[:, 7, 0:P], fb[:, FB_SB:FB_SB + P], ALU.add).then_inc(s["silu_in"], 1)
            dve.tensor_tensor(fhs, ps[:, 7, P:2 * P], fb[:, FB_SB + P:FB_SB + 2 * P], ALU.add).then_inc(s["x_new"], 1)
            dve.wait_ge(s["silu_done"], 2)
            dve.wait_ge(s["x_new"], 1)
            dve.tensor_tensor(fhs, fhs, fss, ALU.mult).then_inc(s["h_ready"], 1)
            inner(1)
            evac("ffn2")
            gated(1)
            link(dve.tensor_tensor(x[:, :], x[:, :], fb[0:T, FB_SB3:FB_SB3 + 512], ALU.add))
            evac("ffn3")
            evac("ffn4")
            dve.wait_ge(s["item_used"], I_SW3 + 1)
            add_halves(6)

            normalise(3)
            evac("ln3")
            for m in range(4):
                dve.wait_ge(s["qsq_done"], m + 1)
                link(dve.tensor_reduce(kms_q(m), qsq.rearrange("p (g d) -> p g d", d=HD), AX_X, ALU.add))
                dve.tensor_scalar(kms_q(m), kms_q(m), 1.0 / HD, LN_EPS, ALU.mult, ALU.add).then_inc(s["qms_ready"], 1)
                dve.wait_ge(s["rq_ready"], m + 1)
                if m >= 2:
                    dve.wait_ge(s["qnT_psum"], m - 1)
                dve.tensor_tensor(qn[m % 2].rearrange("p (g d) -> p g d", d=HD),
                                  bank((3, 4, 6, 7)[m]).rearrange("p (g d) -> p g d", d=HD),
                                  kms_q(m).unsqueeze(2).to_broadcast([P, 4, HD]), ALU.mult).then_inc(s["qn_ready"], 1)
            evac("q0")
            evac("rest")
            dve.wait_ge(s["mask_in"], 64)
            link(dve.tensor_scalar(nmask, nmask, -1.0, None, ALU.mult))

            dve.wait_ge(s["qnT_psum"], 4)
            NU = KVH * B

            def out_copy(u):
                g, b = u // B, u % B
                dve.wait_ge(s["ox_done"], u + 1)
                dve.tensor_copy(otx[:, GH * g:GH * g + GH, S * b:S * b + S],
                                ps[:, 3 + u % 2, 0:P].rearrange("p (h t) -> p h t", h=GH)).then_inc(s["otx_ready"], 1)

            for u in range(NU + 2):
                if u < NU:
                    dve.wait_ge(s["sx_done"], u + 1)
                    if u >= 3:
                        dve.wait_ge(s["ptx_psum"], u - 2)
                    dve.tensor_tensor_reduce(pb[u % 3], bank(SBANKS[u % 3]), nmask, 1.0, 3.0e38, ALU.add, ALU.min,
                                             pmx[:, u:u + 1]).then_inc(s["pmax_ready"], 1)
                if u == 0:
                    evac("last")
                if u >= 1 and u <= NU:
                    v = u - 1
                    dve.wait_ge(s["pexp_done"], v + 1)
                    link(dve.reciprocal(prc[:, v:v + 1], psm[:, v:v + 1]))
                    dve.tensor_scalar(pb[v % 3], pb[v % 3], prc[:, v:v + 1], None, ALU.mult).then_inc(s["pn_ready"], 1)
                if u >= 4:
                    out_copy(u - 4)
            for u in range(NU - 2, NU):
                out_copy(u)
            dve.wait_ge(s["item_used"], ITEMS)
            add_halves(7)

            centre(4)
            dve.wait_ge(s["late_in"], 16)
            qkb = late[:, L_QKB:L_QKB + 512]
            rows = late[0:T, L_ROWS:L_ROWS + 1536]
            dve.wait_ge(s["lq_done"], 1)
            dve.scalar_tensor_tensor(lq, ps[:, 0, 0:256], rstd2, qkb[:, 0:256], ALU.mult, ALU.add)\
               .then_inc(s["lqk_sb"], 1)
            dve.wait_ge(s["lk_done"], 1)
            dve.scalar_tensor_tensor(lk, ps[:, 1, 0:256], rstd2, qkb[:, 256:512], ALU.mult, ALU.add)\
               .then_inc(s["lqk_sb"], 1)
            copy_qk(dve.tensor_copy, dve, 1)
            dve.wait_ge(s["lv_done"], 1)
            for h in range(2):
                ins = dve.scalar_tensor_tensor(lv[:, 256 * h:256 * h + 256], halves(3)[h], rstd2[T * h:T * h + T, :],
                                               rows[:, 256 * h:256 * h + 256], ALU.mult, ALU.add)
            steps[0] += 1
            ins.then_inc(s["dve_step"], 1)
            bias_step = steps[0]
            half = [P, 8, S]
            for f in range(2):
                cols = slice(256 * f, 256 * f + 256)
                lp3 = lp[:, cols].rearrange("p (g k) -> p g k", k=S)
                dve.wait_ge(s["ls_done"], f + 1)
                s3 = bank(4 + f)[:, 0:256].rearrange("p (g k) -> p g k", k=S)
                m = mx[:, 8 * f:8 * f + 8]
                link(dve.tensor_reduce(m, s3, AX_X, ALU.max))
                dve.tensor_tensor(lp3, s3, m.unsqueeze(2).to_broadcast(half), ALU.subtract).then_inc(s["ls_shift"], 1)
                if f == 0:
                    dve.wait_ge(s["dve_step"], bias_step)
                    dve.transpose(kn[0:T, 1, :], lv).then_inc(s["vg_ready"], 1)
                dve.wait_ge(s["le_done"], f + 1)
                link(dve.scalar_tensor_tensor(lp[:, cols], bank(4 + f)[:, 0:256], THRESH4, lp[:, cols],
                                              ALU.is_gt, ALU.mult))
                dve.transpose(at[:, cols], lp[:, cols]).then_inc(s["at_ready"], 1)
            link(dve.tensor_reduce(sm, lp.rearrange("p (g k) -> p g k", k=S), AX_X, ALU.add))
            link(dve.reciprocal(rc, sm))
            for f in range(2):
                dve.wait_ge(s["lo_done"], f + 1)
                dve.tensor_tensor(heads_out[:, P * f:P * f + P].rearrange("p (t d) -> p t d", d=DK),
                                  bank(6 + f)[:, 0:P].rearrange("p (t d) -> p t d", d=DK),
                                  rc[:, 8 * f:8 * f + 8].unsqueeze(2).to_broadcast([P, 8, DK]), ALU.mult)\
                   .then_inc(s["lo_ready"], 1)
            link(dve.tensor_tensor(x[:, :], x[:, :], rows[:, 512:1024], ALU.add))
            dve.wait_ge(s["ly_done"], 1)
            add_halves(4)

            centre(5)
            link(dve.tensor_tensor(x[:, :], x[:, :], rows[:, 1024:1536], ALU.add))
            dve.wait_ge(s["xa_done"], 1)
            link(dve.scalar_tensor_tensor(gsc, ps[0:T, 4, 64:68], rstd, cst[0:T, C_GB:C_GB + 4], ALU.mult, ALU.add))
            dve.tensor_reduce(rz[0:T, 0:1], gsc, AX_X, ALU.max, negate=True).then_inc(s["ge_in"], 1)
            dve.wait_ge(s["ge_done"], 1)
            top, inv, f = rz[0:T, 1:2], rz[0:T, 2:3], gm[0:T, :]
            before = sc[0:T, 72:75]
            dve.tensor_copy(before[:, 0:1], ge[:, 0:1])
            dve.tensor_tensor(before[:, 1:2], ge[:, 0:1], ge[:, 1:2], ALU.max)
            link(dve.tensor_reduce(top, ge, AX_X, ALU.max))
            dve.tensor_tensor(before[:, 2:3], before[:, 1:2], ge[:, 2:3], ALU.max)
            link(dve.reciprocal(inv, top))
            link(dve.tensor_tensor(f[:, 0:1], top, inv, ALU.mult))
            link(dve.scalar_tensor_tensor(f[:, 1:4], before, top, f[:, 0:1].to_broadcast([T, 3]), ALU.is_lt, ALU.mult))
            for i, (a, b) in enumerate(zip((0,) + RANKS, RANKS)):
                ins = dve.tensor_scalar(xm[:, a:b], ps[0:T, 4, a:b], f[:, i:i + 1], None, ALU.mult)
            ins.then_inc(s["xm_ready"], 1)
            dve.wait_ge(s["xmT_psum"], 1)
            dve.tensor_copy(xmT, ps[0:T, 2, 0:T]).then_inc(s["xmT_ready"], 1)
            for h in range(2):
                dve.wait_ge(s["f_done"], 2)
                cols = x[:, 256 * h:256 * h + 256]
                dve.scalar_tensor_tensor(cols, halves(3)[h], rstd2[T * h:T * h + T, :], cols, ALU.mult, ALU.add)\
                   .then_inc(s["fin_ready"], 1)

        @block.scalar
        def _(act):
            def evac(name):
                n0, n1 = FILL_TO[name]
                for n in range(n0, n1):
                    u = n // 4
                    ki = turned(n)
                    if ki is not None:
                        act.wait_ge(s["kT_psum"], ki + 1)
                        g, b, c = 4 * (ki // TILES), ki % TILES // 4, ki % 4
                        act.activation(kT[:, g:g + 4, b, P * c:P * c + P],
                                       bank(2).rearrange("p (g n) -> p g n", g=4), ACT.Copy).then_inc(s["kT_ready"], 1)
                    if n % 4 != 3:
                        continue
                    if u < KUNITS:
                        act.wait_ge(s["kv_unit_done"], u + 1)
                        if u >= 3:
                            act.wait_ge(s["kT_psum"], u - 2)
                        act.activation(kn[:, u % 3, :], bank(u % 2), ACT.Copy).then_inc(s["kraw_ready"], 1)
                        act.wait_ge(s["kraw_ready"], u + 1)
                        if u >= 2:
                            act.wait_ge(s["rk_ready"], u - 1)
                        if u:
                            act.wait_ge(s["kms_ready"], u)
                        for g in range(4):
                            head = slice(HD * g, HD * g + HD)
                            ins = act.activation(ksq[:, head], kn[:, u % 3, head], ACT.Square,
                                                 scale=float(HD ** -0.5), accum_out=kms[u % 2][:, g:g + 1])
                        ins.then_inc(s["kms_ready"], 1)
                    else:
                        act.wait_ge(s["kv_unit_done"], u + 1)
                        if u == KUNITS:
                            act.wait_ge(s["q2_ready"], 2)
                        if u == KUNITS + TILES:
                            wait_low(act, 14)
                        act.activation(V[:, u // TILES - 2, u % TILES, :], bank(u % 2), ACT.Copy)\
                           .then_inc(s["v_ready"], 1)
                    for i in SPLIT_AFTER.get(u, ()):
                        split(i)

            def split(i):
                key, lo, n = PIECES[i]
                act.wait_ge(s[f"raw_in{i}"], 16)
                if key[0] == "w" and key[1] >= 2:
                    act.wait_ge(s["kv_unit_done"], TILES * (key[1] - 1))
                act.activation(hi_lo[key][0][:, lo:lo + n], raw[key][:, lo:lo + n], ACT.Copy)\
                   .then_inc(s["high_done"], 1)

            def copy_xT(n):
                act.wait_ge(s["xnT_psum"], n)
                act.activation(xT[:, :, :], ps[:, 5, 0:256].rearrange("p (k t) -> p k t", k=KC), ACT.Copy)\
                   .then_inc(s["xT_ready"], 1)

            act.wait_ge(s["const_ready"], 1)
            act.activation(sc[:, 256:257], nhalf[:, 0:1], ACT.Copy)
            for i in range(8):
                split(i)
            evac("start")
            act.wait_ge(s["scal_ready"], 1)
            for b in range(B):
                act.wait_ge(s[f"ctx_in{b}"], 16)
                act.activation(ctxn[:, 4 * b:4 * b + 4, :], ctxn[:, 4 * b:4 * b + 4, :], ACT.Identity,
                               bias=cst[:, C_Q + 3:C_Q + 4], scale=r2s).then_inc(s["ctx_aff"], 1)
                if b == 0:
                    evac("start2")
            act.wait_ge(s["xqT_psum"], 1)
            act.activation(xqT, ps[:, 5, 0:128].bitcast(BF16).rearrange("p (k t) -> p k t", k=KC), ACT.Copy)\
               .then_inc(s["xqT_ready"], 1)
            evac("quant")
            evac("mix")
            copy_xT(1)
            evac("ln1")
            act.wait_ge(s["item_used"], I_WQ + 1)
            act.activation(qTs, ps[:, 4, 0:256].rearrange("p (c t) -> p c t", c=KC), ACT.Copy).then_inc(s["qT_sb"], 1)
            act.wait_ge(s["item_used"], I_WV + 1)
            act.wait_ge(s["vbd_zero"], 1)
            for c in range(KC):
                act.activation(vbd[S * c:S * c + S, :, DK * c:DK * c + DK],
                               ps[S * c:S * c + S, 6, 0:256].rearrange("p (g d) -> p g d", d=DK), ACT.Copy)\
                   .then_inc(s["vbd_ready"], 1)
            evac("heads")
            act.wait_ge(s["s_shift"], 1)
            act.activation(bank(3), bank(7), ACT.Exp, scale=0.25).then_inc(s["e_done"], 1)
            evac("soft1")
            act.wait_ge(s["o_done"], 1)
            act.activation(ots, ps[:, 4, 0:256].rearrange("p (c t) -> p c t", c=KC), ACT.Copy)\
               .then_inc(s["ot_ready"], 1)
            evac("pv1")

            evac("ln2")
            copy_xT(2)
            act.wait_ge(s["lg_ready"], 2)
            act.activation(re, lg, ACT.Exp, bias=rz[:, 0:1], accum_out=rz[:, 1:2]).then_inc(s["re_done"], 1)

            def copy_hT(n, dst, w):
                act.wait_ge(s["hT_psum"], n)
                act.activation(dst, ps[:, 5, 0:w], ACT.Copy).then_inc(s["hT_ready"], 1)

            evac("route")
            act.wait_ge(s["silu_in"], 1)
            act.activation(fs, fa, ACT.Silu).then_inc(s["silu_done"], 1)
            evac("ffn1")
            act.wait_ge(s["silu_in"], 2)
            act.activation(fss, fss, ACT.Silu).then_inc(s["silu_done"], 1)
            act.wait_ge(s["silu_in"], 3)
            act.wait_ge(s["h_ready"], 1)
            act.activation(fs, fa, ACT.Silu).then_inc(s["silu_done"], 1)
            evac("ffn2")
            copy_hT(1, r2[:, 1536:2048], 512)
            copy_hT(2, r2[:, 2560:2688], P)
            evac("ffn3")
            copy_hT(3, r2[:, 2048:2560], 512)
            evac("ffn4")
            act.wait_ge(s["gateT_psum"], 1)
            act.activation(gateT, ps[0:E, 7, 256:256 + T], ACT.Copy).then_inc(s["gateT_ready"], 1)

            evac("ln3")
            copy_xT(3)

            def copy_qT(m):
                act.wait_ge(s["qnT_psum"], m + 1)
                for a in range(2):
                    act.activation(qTx[:, 4 * a + m].rearrange("p b (j t) -> p b j t", j=GH),
                                   bank(5).rearrange("p (j a b t) -> p a b j t", j=GH, a=2, b=B)[:, a], ACT.Copy,
                                   scale=nw).then_inc(s["qTx_ready"], 1)

            for m in range(4):
                act.wait_ge(s["item_used"], I_XQ + 2 * m + 2)
                if m:
                    act.wait_ge(s["qms_ready"], m)
                act.activation(qsq, bank((3, 4, 6, 7)[m]), ACT.Square).then_inc(s["qsq_done"], 1)
                if m:
                    copy_qT(m - 1)
            evac("q0")
            copy_qT(3)
            act.activation(sc[:, 257:258], nhalf[:, 0:1], ACT.Exp)
            evac("rest")

            NU = KVH * B
            for u in range(NU + 2):
                if u < NU:
                    act.wait_ge(s["pmax_ready"], u + 1)
                    act.activation(pb[u % 3], pb[u % 3], ACT.Exp, bias=pmx[:, u:u + 1], scale=-1.0,
                                   accum_out=psm[:, u:u + 1]).then_inc(s["pexp_done"], 1)
                if u == 0:
                    evac("last")
                if u >= 2:
                    v = u - 2
                    act.wait_ge(s["ptx_psum"], v + 1)
                    if v >= 2:
                        act.wait_ge(s["ox_done"], v - 1)
                    act.activation(ptb[v % 2], bank((2, 5)[v % 2]), ACT.Copy).then_inc(s["ptx_ready"], 1)

            copy_xT(4)
            copy_qk(lambda out, src: act.activation(out, src, ACT.Copy), act, 0)
            for f in range(2):
                act.wait_ge(s["ls_shift"], f + 1)
                act.activation(lp[:, 256 * f:256 * f + 256], lp[:, 256 * f:256 * f + 256], ACT.Exp, scale=0.25)\
                   .then_inc(s["le_done"], 1)
                if f == 0:
                    act.wait_ge(s["vg_ready"], 1)
                    for c in range(4):
                        tb, th = c // 2, c % 2
                        act.activation(vg2[S * c:S * c + S, :, :], vg[S * tb:S * tb + S, :, 16 * th:16 * th + 16],
                                       ACT.Copy).then_inc(s["vg2_ready"], 1)
            act.wait_ge(s["of_psum"], 1)
            act.activation(of.rearrange("p i (c t) -> p i c t", c=4),
                           ps[:, 0:4, 0:64].rearrange("p c (i t) -> p i c t", i=4), ACT.Copy)\
               .then_inc(s["of_ready"], 1)
            copy_xT(5)
            act.wait_ge(s["ge_in"], 1)
            act.activation(ge, gsc, ACT.Exp, bias=rz[0:T, 0:1]).then_inc(s["ge_done"], 1)

        @block.gpsimd
        def _(pool):
            def evac(name):
                for u in ended(*FILL_TO[name]):
                    if u < KUNITS:
                        pool.wait_ge(s["kms_ready"], u + 1)
                        pool.tensor_scalar(kms[u % 2], kms[u % 2], LN_EPS, None, ALU.add).then_inc(s["kms_eps"], 1)
                        pool.wait_ge(s["kms_eps"], u + 1)
                        if u >= 2:
                            pool.wait_ge(s["kn_ready"], u - 1)
                        pool.tensor_tensor(rk[u % 2], kms[u % 2], nhalf, ALU.pow).then_inc(s["rk_ready"], 1)
                    for i in SPLIT_AFTER.get(u, ()):
                        if i in POOL_PIECES:
                            low_half(pool, i, "low_pool")

            def rsqrt_var(n):
                pool.wait_ge(s["var_ready"], n + 1)
                pool.tensor_tensor(rstd, ve, nhalf[0:T, 0:1], ALU.pow).then_inc(s["rstd_ready"], 1)

            pool.memset(vbd, 0.0).then_inc(s["vbd_zero"], 1)
            pool.wait_ge(s["const_ready"], 1)
            rsqrt_var(0)
            evac("start")
            evac("start2")
            evac("quant")
            rsqrt_var(1)
            for name in ("mix", "ln1", "heads", "soft1", "pv1"):
                evac(name)
            rsqrt_var(2)
            for name in ("ln2", "route", "ffn1", "ffn2", "ffn3", "ffn4"):
                evac(name)
            rsqrt_var(3)
            evac("ln3")
            for m in range(4):
                pool.wait_ge(s["qms_ready"], m + 1)
                pool.tensor_tensor(kms_q(m), kms_q(m), nhalf, ALU.pow).then_inc(s["rq_ready"], 1)
            evac("q0")
            evac("rest")
            evac("last")
            rsqrt_var(4)
            rsqrt_var(5)


def kernel(**inputs):
    import concourse.bacc as _bacc
    from concourse.bass_utils import run_bass_kernel_spmd as _run

    i = {k: np.asarray(v) for k, v in inputs.items()}
    f32 = np.float32

    def chunks(w, n=P):
        return w.reshape(-1, n, w.shape[1]).transpose(1, 0, 2)

    def rep(v, n=P):
        return np.broadcast_to(v.reshape(1, -1), (n, v.size))

    x_d = i["x"].reshape(T, D)
    ctx = i["ctx_4096"]
    ctx_d = ctx.reshape(B, KC, P, D).transpose(2, 0, 1, 3).reshape(P, B * KC, D)
    tri = lambda n: rep(np.tril(np.ones((n, n), f32), -1))
    cst_d = np.concatenate([
        np.eye(P, dtype=f32), np.kron(np.eye(HPC, dtype=f32), np.ones((DK, 1), f32)), tri(16), tri(4),
        i["L1_xattn_q_norm_w"].reshape(P, 1), i["L1_xattn_k_norm_w"].reshape(P, 1),
        rep(i["L0_ffn_router_b"]), rep(i["L0_ffn_router_bias"]), rep(i["L1_ffn_gate_b"]),
        rep(i["L0_xattn_x1_scale"]), rep(i["L0_xattn_x1_zp"]), rep(i["L0_xattn_x2_scale"]), rep(i["L0_xattn_x2_zp"]),
    ], axis=1)
    wkT, wvT = i["L1_xattn_Wk"].T, i["L1_xattn_Wv"].T
    tiles = [chunks(c.T).reshape(P, KC, 4, P).transpose(0, 2, 1, 3).reshape(P, SLOT) for c in ctx]
    parts = (wkT[:, :512], wkT[:, 512:], wvT[:, :512], wvT[:, 512:])
    kv_d = np.stack(tiles + [chunks(w).reshape(P, SLOT) for w in parts])

    items = [chunks(i[f"L0_attn_w_{n}"].T).reshape(P, SLOT) for n in "kqv"]
    wo = i["L0_attn_w_o"].T.reshape(KC, 2, 4, DK, D).transpose(1, 0, 3, 2, 4)
    items.append(wo.reshape(P, SLOT))
    ein = [i[f"L0_ffn_ew{n}"].reshape(2, 2, 4, 2, 2, P, INTER).transpose(0, 3, 5, 4, 1, 2, 6).reshape(2, 2, P, SLOT)
           for n in (1, 2)]
    shared = np.stack([i[f"L0_ffn_sw{n}"].reshape(KC, P, 2, INTER) for n in (1, 2)])
    items += [*ein[0][0], *ein[1][0], shared.transpose(2, 1, 0, 3, 4).reshape(P, SLOT), *ein[0][1], *ein[1][1]]
    e3 = i["L0_ffn_ew3"].reshape(2, 2, 2, 2, INTER, D)
    items += list(e3.transpose(0, 2, 4, 3, 1, 5).reshape(4, P, SLOT))
    sw3 = np.zeros((P, SLOT), f32)
    sw3[:, 0:1024] = chunks(i["L0_ffn_sw3"]).reshape(P, 1024)
    sw3[0:E, 1024:1536] = i["L0_ffn_eb3"]
    items.append(sw3)
    wq = i["L1_xattn_Wq"].T.reshape(2, 2, P, 2, 4, 512)
    items += list(wq.transpose(4, 0, 2, 1, 3, 5).reshape(8, P, SLOT))
    items += list(i["L1_xattn_Wo"].T.reshape(KVH, GH, HD, D).transpose(0, 2, 1, 3).reshape(KVH, P, SLOT))
    items_d = np.stack(items)

    eb = np.stack([i[f"L0_ffn_eb{n}"].reshape(2, 2, 512) for n in (1, 2)])
    sbs = np.stack([i[f"L0_ffn_sb{n}"].reshape(2, INTER) for n in (1, 2)])
    fb_d = np.concatenate([
        np.repeat(eb.transpose(2, 1, 0, 3).reshape(2, 2048), T, axis=0),
        np.repeat(sbs.transpose(1, 0, 2).reshape(2, 256), T, axis=0), rep(i["L0_ffn_sb3"])], axis=1)
    rw_d = chunks(i["L0_ffn_router_w"]).reshape(P, 64)
    mask_d = i["mask_1x1xSxS2_ff0"].reshape(S, CTX)

    by_d = lambda w: w.reshape(2, 16, DK, -1).transpose(2, 1, 0, 3).reshape(D, -1)
    lwo = i["L1_attn_Wo"].T.reshape(2, 16, 4, 4, D).transpose(3, 1, 0, 2, 4).reshape(P, SLOT)
    l1w_d = np.stack([chunks(i["L1_attn_Wq"].T).reshape(P, SLOT), chunks(i["L1_attn_Wk"].T).reshape(P, SLOT),
                      chunks(by_d(i["L1_attn_Wv"]).T).reshape(P, SLOT), lwo, chunks(i["L1_ffn_W"].T).reshape(P, SLOT)])
    ag = chunks(np.concatenate([i["L1_ffn_A"].T, i["L1_ffn_gate_w"].T], axis=1)).reshape(P, 272)
    bt = np.concatenate([i["L1_ffn_B"].T, np.zeros((P - 64, D), f32)])
    qkb = np.concatenate([np.repeat(i[f"L1_attn_b{n}"].reshape(2, 256), T, axis=0) for n in "qk"], axis=1)
    late_d = np.concatenate([ag, bt, rep(by_d(i["L1_attn_bv"])), rep(i["L1_attn_bo"]), rep(i["L1_ffn_b"]), qkb], axis=1)

    nc = _bacc.Bacc("TRN2", target_bir_lowering=False, num_devices=1)
    arrays, args = {}, []
    for name, a in (("x", x_d), ("cst", cst_d), ("fb", fb_d), ("rw", rw_d), ("ctx", ctx_d), ("kv", kv_d),
                    ("items", items_d), ("mask", mask_d), ("late", late_d), ("l1w", l1w_d)):
        a = np.ascontiguousarray(a)
        arrays[f"in_{name}"] = a
        args.append(nc.dram_tensor(f"in_{name}", a.shape, mybir.dt.from_np(a.dtype), kind="ExternalInput").ap())
    out = nc.dram_tensor("out_latents", (T, D), F32, kind="ExternalOutput").ap()
    build(nc, *args, out)
    r = _run(nc, [arrays], core_ids=[0])
    return r.results[0]["out_latents"].reshape(B, S, D)
```
